# Optimizing a Trainium2 kernel written in Bass

```python
import numpy as np
import jax
import jax.numpy as jnp

def _softmax(x, axis=-1):
    return jax.nn.softmax(x, axis=axis)

def _gelu(x):
    return jax.nn.gelu(x, approximate=True)

def _silu(x):
    return jax.nn.silu(x)

def _sigmoid(x):
    return jax.nn.sigmoid(x)

def _layernorm(x, axis=-1, eps=1e-05):
    m = jnp.mean(x, axis=axis, keepdims=True)
    v = jnp.var(x, axis=axis, keepdims=True)
    return (x - m) / jnp.sqrt(v + eps)

def _scatter_add(tgt, idx, src, axis=0):
    return tgt.at[idx].add(src)

def _segment_sum(src, seg, n):
    return jax.ops.segment_sum(src, seg, n)
kernel_name = 'mk_flamingo_gated_d1_seqx_r2_c1051b'

def setup_inputs(seed: int=0):
    np.random.seed(seed)
    _w = jnp.asarray

    def _rec_inputs():
        import jax
        import jax.numpy as jnp
        _rk = jax.random.key(seed)
        x = -0.0003929 + 0.9999 * jax.random.normal(jax.random.fold_in(_rk, 1), (2, 2048, 512), jnp.float32)
        _lenS = 2048 - jax.random.randint(jax.random.fold_in(_rk, 7), (2,), 0, max(1, 2048 // 4) + 1, jnp.int32)
        _lenS2 = 77 - jax.random.randint(jax.random.fold_in(_rk, 8), (2,), 0, max(1, 77 // 4) + 1, jnp.int32)
        _ctx_1024P = jax.random.normal(jax.random.fold_in(_rk, 11), (2, 16, 512), jnp.float32)
        _ctx_1024c = jax.random.dirichlet(jax.random.fold_in(_rk, 511), 0.3 * jnp.ones((16,), jnp.float32), (2, 77))
        _ctx_1024t = jnp.einsum('bsk,bkd->bsd', _ctx_1024c, _ctx_1024P)
        _ctx_1024t = _ctx_1024t * jax.lax.rsqrt(jnp.mean(jnp.square(_ctx_1024t)) + 1e-12) * 0.953939
        ctx_1024 = 2.81802e-05 + 1.00001 * (_ctx_1024t + 0.3 * jax.random.normal(jax.random.fold_in(_rk, 611), (2, 77, 512), jnp.float32))
        _g = jax.random.normal(jax.random.fold_in(_rk, 9001), (2, 1), jnp.float32)
        _g = jnp.sign(_g) * jnp.maximum(jnp.abs(_g), 1.0) + (_g == 0) * 1.0
        g_xattn = _g[0]
        g_ffn = _g[1]
        return (x, ctx_1024, g_xattn, g_ffn)
    x, ctx_1024, g_xattn, g_ffn = _rec_inputs()

    def _L0_xattn_setup():
        import jax, jax.numpy as jnp
        import numpy as np
        E = 512
        NUM_HEADS = 16
        DK = E // NUM_HEADS
        EPS = 1e-05
        NEG_INF = -jnp.inf

        def layer_norm(x, g, b):
            mu = jnp.mean(x, axis=-1, keepdims=True)
            var = jnp.var(x, axis=-1, keepdims=True)
            return (x - mu) * jax.lax.rsqrt(var + EPS) * g + b

        def self_attn(x, Wq, Wk, Wv):
            Q, K, V = (x @ Wq, x @ Wk, x @ Wv)
            energy = jnp.einsum('bqd,bkd->bqk', Q, K)
            S = energy.shape[-1]
            lengths = jnp.sum(energy[:, 0] != 0, axis=-1)
            kidx = jnp.arange(S)
            pad = kidx[None, None, :] >= lengths[:, None, None]
            causal = kidx[None, :] < kidx[:, None]
            causal = (kidx[None, :] > kidx[:, None])[None]
            energy = jnp.where(pad | causal, NEG_INF, energy)
            score = jax.nn.softmax(energy / np.sqrt(DK), axis=-1)
            return jnp.einsum('bqk,bkd->bqd', score, V)

        def cross_attn(x, context, Wq, Wk, Wv):
            Q = x @ Wq
            K, V = (context @ Wk, context @ Wv)
            energy = jnp.einsum('bqd,bkd->bqk', Q, K)
            Sk = energy.shape[-1]
            lengths = jnp.sum(energy[:, 0] != 0, axis=-1)
            kidx = jnp.arange(Sk)
            pad = kidx[None, None, :] >= lengths[:, None, None]
            energy = jnp.where(pad, NEG_INF, energy)
            score = jax.nn.softmax(energy / np.sqrt(DK), axis=-1)
            return jnp.einsum('bqk,bkd->bqd', score, V)
        key = jax.random.key(seed)
        ks = jax.random.split(key, 12)
        B, S = (8, 1024)
        s = 1.0 / np.sqrt(E)
        inp = {'x': jax.random.normal(ks[0], (B, S, E), jnp.float32), 'context': jax.random.normal(ks[1], (B, S, E), jnp.float32), 'Wq1': jax.random.normal(ks[2], (E, E), jnp.float32) * s, 'Wk1': jax.random.normal(ks[3], (E, E), jnp.float32) * s, 'Wv1': jax.random.normal(ks[4], (E, E), jnp.float32) * s, 'Wq2': jax.random.normal(ks[5], (E, E), jnp.float32) * s, 'Wk2': jax.random.normal(ks[6], (E, E), jnp.float32) * s, 'Wv2': jax.random.normal(ks[7], (E, E), jnp.float32) * s, 'fc1_w': jax.random.normal(ks[8], (E, E), jnp.float32) * s, 'fc1_b': jnp.zeros((E,), jnp.float32), 'fc2_w': jax.random.normal(ks[9], (E, E), jnp.float32) * s, 'fc2_b': jnp.zeros((E,), jnp.float32), 'ln1_g': jnp.ones((E,), jnp.float32), 'ln1_b': jnp.zeros((E,), jnp.float32), 'ln2_g': jnp.ones((E,), jnp.float32), 'ln2_b': jnp.zeros((E,), jnp.float32), 'ln3_g': jnp.ones((E,), jnp.float32), 'ln3_b': jnp.zeros((E,), jnp.float32)}
        return inp
    _L0_xattn_all = _L0_xattn_setup()
    _L0_xattn_in = {k: v for k, v in _L0_xattn_all.items() if k in ('Wq1', 'Wk1', 'Wv1', 'Wq2', 'Wk2', 'Wv2', 'fc1_w', 'fc1_b', 'fc2_w', 'fc2_b', 'ln1_g', 'ln1_b', 'ln2_g', 'ln2_b', 'ln3_g', 'ln3_b')}
    del _L0_xattn_all

    def _L0_ffn_setup():
        import jax, jax.numpy as jnp
        import numpy as np
        B, S, H, F, G = (8, 1024, 512, 2048, 128)
        EPS = 1e-05

        def _dequant(q, scales, g):
            K, N = q.shape
            w = (q.astype(jnp.float32) - 128.0).reshape(K // g, g, N) * scales[:, None, :]
            return w.reshape(K, N)
        key = jax.random.key(seed)
        ks = jax.random.split(key, 8)
        x = jax.random.normal(ks[0], (B, S, H), dtype=jnp.float32)
        ln_gamma = jnp.ones((H,), jnp.float32)
        ln_beta = jnp.zeros((H,), jnp.float32)
        fc1_q = jax.random.randint(ks[1], (H, F), 0, 128, dtype=jnp.int32)
        fc2_q = jax.random.randint(ks[2], (F, H), 0, 128, dtype=jnp.int32)
        fc1_scales = jax.random.uniform(ks[3], (H // G, F), jnp.float32) * 0.02 + 0.001
        fc2_scales = jax.random.uniform(ks[4], (F // G, H), jnp.float32) * 0.02 + 0.001
        fc1_bias = jax.random.normal(ks[5], (F,), jnp.float32) * 0.02
        fc2_bias = jax.random.normal(ks[6], (H,), jnp.float32) * 0.02
        return {'x': x, 'ln_gamma': ln_gamma, 'ln_beta': ln_beta, 'fc1_q': fc1_q, 'fc1_scales': fc1_scales, 'fc1_bias': fc1_bias, 'fc2_q': fc2_q, 'fc2_scales': fc2_scales, 'fc2_bias': fc2_bias}
    _L0_ffn_all = _L0_ffn_setup()
    _L0_ffn_in = {k: v for k, v in _L0_ffn_all.items() if k in ('ln_gamma', 'ln_beta', 'fc1_q', 'fc1_scales', 'fc1_bias', 'fc2_q', 'fc2_scales', 'fc2_bias')}
    del _L0_ffn_all
    return {'x': x, 'ctx_1024': ctx_1024, 'g_xattn': g_xattn, 'g_ffn': g_ffn, 'L0_xattn_Wq1': _L0_xattn_in['Wq1'], 'L0_xattn_Wk1': _L0_xattn_in['Wk1'], 'L0_xattn_Wv1': _L0_xattn_in['Wv1'], 'L0_xattn_Wq2': _L0_xattn_in['Wq2'], 'L0_xattn_Wk2': _L0_xattn_in['Wk2'], 'L0_xattn_Wv2': _L0_xattn_in['Wv2'], 'L0_xattn_fc1_w': _L0_xattn_in['fc1_w'], 'L0_xattn_fc1_b': _L0_xattn_in['fc1_b'], 'L0_xattn_fc2_w': _L0_xattn_in['fc2_w'], 'L0_xattn_fc2_b': _L0_xattn_in['fc2_b'], 'L0_xattn_ln1_g': _L0_xattn_in['ln1_g'], 'L0_xattn_ln1_b': _L0_xattn_in['ln1_b'], 'L0_xattn_ln2_g': _L0_xattn_in['ln2_g'], 'L0_xattn_ln2_b': _L0_xattn_in['ln2_b'], 'L0_xattn_ln3_g': _L0_xattn_in['ln3_g'], 'L0_xattn_ln3_b': _L0_xattn_in['ln3_b'], 'L0_ffn_ln_gamma': _L0_ffn_in['ln_gamma'], 'L0_ffn_ln_beta': _L0_ffn_in['ln_beta'], 'L0_ffn_fc1_q': _L0_ffn_in['fc1_q'], 'L0_ffn_fc1_scales': _L0_ffn_in['fc1_scales'], 'L0_ffn_fc1_bias': _L0_ffn_in['fc1_bias'], 'L0_ffn_fc2_q': _L0_ffn_in['fc2_q'], 'L0_ffn_fc2_scales': _L0_ffn_in['fc2_scales'], 'L0_ffn_fc2_bias': _L0_ffn_in['fc2_bias']}

def reference(x, ctx_1024, g_xattn, g_ffn, L0_xattn_Wq1, L0_xattn_Wk1, L0_xattn_Wv1, L0_xattn_Wq2, L0_xattn_Wk2, L0_xattn_Wv2, L0_xattn_fc1_w, L0_xattn_fc1_b, L0_xattn_fc2_w, L0_xattn_fc2_b, L0_xattn_ln1_g, L0_xattn_ln1_b, L0_xattn_ln2_g, L0_xattn_ln2_b, L0_xattn_ln3_g, L0_xattn_ln3_b, L0_ffn_ln_gamma, L0_ffn_ln_beta, L0_ffn_fc1_q, L0_ffn_fc1_scales, L0_ffn_fc1_bias, L0_ffn_fc2_q, L0_ffn_fc2_scales, L0_ffn_fc2_bias):
    import jax
    import jax.numpy as jnp

    def _L0_xattn_ref(x, context, Wq1, Wk1, Wv1, Wq2, Wk2, Wv2, fc1_w, fc1_b, fc2_w, fc2_b, ln1_g, ln1_b, ln2_g, ln2_b, ln3_g, ln3_b):
        import jax, jax.numpy as jnp
        import numpy as np
        E = 512
        NUM_HEADS = 16
        DK = E // NUM_HEADS
        EPS = 1e-05
        NEG_INF = -jnp.inf

        def layer_norm(x, g, b):
            mu = jnp.mean(x, axis=-1, keepdims=True)
            var = jnp.var(x, axis=-1, keepdims=True)
            return (x - mu) * jax.lax.rsqrt(var + EPS) * g + b

        def self_attn(x, Wq, Wk, Wv):
            Q, K, V = (x @ Wq, x @ Wk, x @ Wv)
            energy = jnp.einsum('bqd,bkd->bqk', Q, K)
            S = energy.shape[-1]
            lengths = jnp.sum(energy[:, 0] != 0, axis=-1)
            kidx = jnp.arange(S)
            pad = kidx[None, None, :] >= lengths[:, None, None]
            causal = kidx[None, :] < kidx[:, None]
            causal = (kidx[None, :] > kidx[:, None])[None]
            energy = jnp.where(pad | causal, NEG_INF, energy)
            score = jax.nn.softmax(energy / np.sqrt(DK), axis=-1)
            return jnp.einsum('bqk,bkd->bqd', score, V)

        def cross_attn(x, context, Wq, Wk, Wv):
            Q = x @ Wq
            K, V = (context @ Wk, context @ Wv)
            energy = jnp.einsum('bqd,bkd->bqk', Q, K)
            Sk = energy.shape[-1]
            lengths = jnp.sum(energy[:, 0] != 0, axis=-1)
            kidx = jnp.arange(Sk)
            pad = kidx[None, None, :] >= lengths[:, None, None]
            energy = jnp.where(pad, NEG_INF, energy)
            score = jax.nn.softmax(energy / np.sqrt(DK), axis=-1)
            return jnp.einsum('bqk,bkd->bqd', score, V)
        z = self_attn(x, Wq1, Wk1, Wv1)
        x = layer_norm(x + z, ln1_g, ln1_b)
        z = cross_attn(x, context, Wq2, Wk2, Wv2)
        x = layer_norm(x + z, ln2_g, ln2_b)
        z = jax.nn.relu(x @ fc1_w + fc1_b)
        z = z @ fc2_w + fc2_b
        return layer_norm(x + z, ln3_g, ln3_b)

    def _L0_ffn_ref(x, ln_gamma, ln_beta, fc1_q, fc1_scales, fc1_bias, fc2_q, fc2_scales, fc2_bias):
        import jax, jax.numpy as jnp
        import numpy as np
        B, S, H, F, G = (8, 1024, 512, 2048, 128)
        EPS = 1e-05

        def _dequant(q, scales, g):
            K, N = q.shape
            w = (q.astype(jnp.float32) - 128.0).reshape(K // g, g, N) * scales[:, None, :]
            return w.reshape(K, N)
        residual = x
        mu = jnp.mean(x, axis=-1, keepdims=True)
        var = jnp.mean(jnp.square(x - mu), axis=-1, keepdims=True)
        h = (x - mu) * jax.lax.rsqrt(var + EPS) * ln_gamma + ln_beta
        hf = h.reshape(-1, H)
        w1 = _dequant(fc1_q, fc1_scales, G)
        y = hf @ w1 + fc1_bias
        y = jax.nn.silu(y)
        w2 = _dequant(fc2_q, fc2_scales, G)
        z = y @ w2 + fc2_bias
        return residual + 0.5 * z.reshape(residual.shape)
    x = x + jnp.tanh(g_xattn[0]) * _L0_xattn_ref(_layernorm(x, axis=-1), ctx_1024, L0_xattn_Wq1, L0_xattn_Wk1, L0_xattn_Wv1, L0_xattn_Wq2, L0_xattn_Wk2, L0_xattn_Wv2, L0_xattn_fc1_w, L0_xattn_fc1_b, L0_xattn_fc2_w, L0_xattn_fc2_b, L0_xattn_ln1_g, L0_xattn_ln1_b, L0_xattn_ln2_g, L0_xattn_ln2_b, L0_xattn_ln3_g, L0_xattn_ln3_b)
    x = x + jnp.tanh(g_ffn[0]) * _L0_ffn_ref(_layernorm(x, axis=-1), L0_ffn_ln_gamma, L0_ffn_ln_beta, L0_ffn_fc1_q, L0_ffn_fc1_scales, L0_ffn_fc1_bias, L0_ffn_fc2_q, L0_ffn_fc2_scales, L0_ffn_fc2_bias)
    return x

_drawn_inputs = setup_inputs


def setup_inputs(seed=0):
    import zlib

    import numpy as np

    out = dict(_drawn_inputs(seed))
    spreads = {'L0_xattn_fc1_b': (0.0, 0.8),
     'L0_xattn_fc2_b': (0.0, 0.625),
     'L0_xattn_ln1_g': (1.0, 0.2),
     'L0_xattn_ln1_b': (0.0, 0.586),
     'L0_xattn_ln2_g': (1.0, 0.534),
     'L0_xattn_ln2_b': (0.0, 0.427),
     'L0_xattn_ln3_g': (1.0, 0.549),
     'L0_xattn_ln3_b': (0.0, 0.459),
     'L0_ffn_ln_gamma': (1.0, 0.2),
     'L0_ffn_ln_beta': (0.0, 0.1)}
    factors = {'L0_ffn_fc1_bias': 8.0, 'L0_ffn_fc2_bias': 8.0}
    for name, (base, spread) in spreads.items():
        noise = np.random.default_rng([zlib.crc32(name.encode()), seed]).standard_normal(out[name].shape)
        drawn = base * np.exp(spread * noise) if base else spread * noise
        out[name] = jnp.asarray(drawn.astype(out[name].dtype))
    for name, factor in factors.items():
        out[name] = (out[name] * factor).astype(out[name].dtype)
    return out
```

```python
from contextlib import ExitStack

import concourse.bass as bass
from concourse import mybir

F32 = mybir.dt.float32
F32R = mybir.dt.float32r
BF16 = mybir.dt.bfloat16
I16 = mybir.dt.int16
I32 = mybir.dt.int32
ALU = mybir.AluOpType
ACT = mybir.ActivationFunctionType
AX = mybir.AxisListType

P = 128
B, S, E = 2, 2048, 512
C = E // P
NB = S // P
SC = 77
SCP = 80
TILE = 512
BT = TILE // P
NT = B * S // TILE
TPB = S // TILE
FF = 2048
NF = FF // P
EPS = 1e-5
SCALE = float(1.0 / (E // 16) ** 0.5)
BIG = 1e38
PASSES = ((0, 0), (0, 1), (1, 0))

KB = 256


class Steps:

    def __init__(self, eng, sem, per=0, turn=0):
        self.eng, self.sem, self.per, self.turn, self.n = eng, sem, per, turn, 0

    def done(self, ins):
        ins.then_inc(self.sem, 1)
        self.n += 1
        return self.n

    def wait(self, n=None):
        self.eng.wait_ge(self.sem, self.turn * self.per + (self.n if n is None else n))

    def link(self, ins):
        self.done(ins)
        self.wait()


def chunks_of(i):
    return i // 4 + 1


def width_of(i, c):
    return 512 if c < i // 4 else (i % 4 + 1) * P


T_BEFORE = [sum(chunks_of(j) for j in range(i)) for i in range(NB + 1)]


def attention_order():
    order = [("S", 0, 0)]
    for i in range(NB):
        n0 = chunks_of(i)
        n1 = chunks_of(i + 1) if i + 1 < NB else 0
        new_group = i % 4 == 3 and i + 1 < NB
        order.append(("T", i, 0))
        if i:
            order.append(("A", i - 1, 0))
        if new_group:
            order += [("Q", i // 4 + 1, m) for m in range(C)]
        if n1 and not new_group:
            order.append(("S", i + 1, 0))
        if i:
            order.append(("B", i - 1, 0))
        s = 0 if new_group else 1
        for c in range(1, n0):
            order.append(("T", i, c))
            if new_group:
                order.append(("V", i, c - 1))
            if s < n1:
                order.append(("S", i + 1, s))
                s += 1
            if not new_group:
                order.append(("V", i, c - 1))
        order.append(("V", i, n0 - 1))
        while s < n1:
            order.append(("S", i + 1, s))
            s += 1
    order += [("A", NB - 1, 0), ("B", NB - 1, 0)]
    return order


ORDER = attention_order()
TURN_AT = (7, 9, 11, 13)

TP0, MM0 = 16, 14
TP1 = NB + T_BEFORE[NB]
MM1 = 2 * NB
SS1 = 4 + 2 + T_BEFORE[NB]
TP2 = TP0 + B * TP1
TPL = 2
TPT = 2 * BT + 2
TP3 = TP2 + TPL + NT * TPT
MM2 = MM0 + B * MM1

DVE1, DVE2, DVE3 = 134, 27, 27
PTK = T_BEFORE[NB]


def build(nc, a, out):
    ctx = ExitStack()
    with ctx:
        def sb(name, shape, dt=F32):
            return ctx.enter_context(nc.sbuf_tensor(name, shape, dt))

        def sem(name):
            return ctx.enter_context(nc.semaphore(name))

        x1_dram = nc.dram_tensor("x1_scratch", (B * S, E), F32, kind="Internal").ap()
        xg_dram = nc.dram_tensor("xg_scratch", (B * S, E), F32, kind="Internal").ap()
        g_dram = nc.dram_tensor("g_scratch", (P, C * 2 * 2 * SCP), F32, kind="Internal").ap()
        v_dram = nc.dram_tensor("v_scratch", (SC, B * 2 * E), F32, kind="Internal").ap()
        x_dram = a["x"].rearrange("b s e -> (b s) e")
        out_dram = out.rearrange("b s e -> (b s) e")

        R = sb("split", [P, 168 * KB], F32R)
        F = sb("plain", [P, 37 * KB], F32)

        def pair(at, chunks, width):
            return R[:, at * KB:at * KB + chunks * 2 * width].rearrange(
                "p (c h n) -> p c h n", c=chunks, h=2)

        def plain(at, *dims):
            n = 1
            for d in dims:
                n *= d
            v = F[:, at:at + n]
            if len(dims) == 2:
                v = v.rearrange("p (a b) -> p a b", a=dims[0])
            if len(dims) == 3:
                v = v.rearrange("p (a b c) -> p a b c", a=dims[0], b=dims[1])
            return v

        wq1T, wk1T, wq2T = pair(0, C, E), pair(16, C, E), pair(32, C, E)
        wk2, wv2 = pair(48, C, E), pair(64, C, E)
        ctxT, kT2 = pair(80, C, 2 * SCP), pair(85, C, 2 * SCP)
        g_0, v_0 = pair(90, C, 2 * SCP), pair(95, B, E)
        stage = plain(0, 2, C, E)
        ctx_in = plain(6144, B, E)
        xT, V = pair(0, C, S), pair(64, NB, E)
        A, QT, PT = pair(128, C, E), pair(144, C, E), pair(160, 2, E)
        wv = pair(144, C, E)
        Srow = plain(0, 2, S)
        xin, xn, U = plain(4096, 2, E), plain(5120, 2, E), plain(6144, 2, E)
        ln1 = plain(7168, 2, E)
        pad = plain(8192, S // 2).bitcast(BF16)
        x1T, x2T, hid2 = pair(0, C, E), pair(16, C, E), pair(32, C, E)
        G, V2 = pair(48, C, 2 * SCP), pair(53, B, E)
        PT2 = pair(160, 1, E)
        fc1, fc2 = pair(128, C, E), pair(144, C, E)
        N = plain(0, 2, BT, E)
        vec2 = plain(4096, 5, E)
        xo = plain(6656, 1, E)
        HF2 = plain(7168, 2, E)
        S2 = plain(8192, 2, BT * SCP)
        q1, sc1 = plain(8832, 256), plain(9088, 256)
        W2, W1 = pair(0, NF, E), pair(64, C, FF)
        hT = pair(128, 2 * C, TILE)
        hid3 = pair(160, 2, E)
        base = plain(0, 2, BT, E)
        H0 = plain(4096, 2, E)
        HF3 = plain(5120, 2, E)
        vec3 = plain(6144, 3, E)
        q2, sc2 = plain(7680, 2, E), plain(8704, E)

        ident = sb("ident", [P, P])
        tri = sb("tri", [P, P], BF16)
        keys = sb("keys", [P, 512], I16)
        small = sb("small", [P, 148])

        def col(at, n=1):
            return small[:, at:at + n]

        st = small[:, 0:12].rearrange("p (a b) -> p a b", a=2)
        mv1 = small[:, 12:44].rearrange("p (a b) -> p a b", a=NB)
        rs1 = col(44, NB)
        mvE = small[:, 60:68].rearrange("p (a b) -> p a b", a=4)
        rsE = col(68, 4)
        mx = small[:, 72:82].rearrange("p (a b) -> p a b", a=2)
        nmx, nb = col(82, 2), col(84, 2)
        rowsum, rcp = col(86, 4), col(90, 4)
        half, cnt, ln, lnc = col(94), col(95, 4), col(99), col(100, 4)
        gate_x, gate_f, gf_half = col(104), col(105), col(106)
        b1x, b1f = col(107, C), col(111, NF)
        mx2, sum2, rc2 = col(127, 4), col(131, 4), col(135, 4)
        len2 = col(139, 2)
        eps_col = col(141)
        keys_seen, keys_seen2 = col(142), col(143, 2)
        mvX, rs_x = small[:, 72:80].rearrange("p (a b) -> p a b", a=BT), col(127, BT)
        mask2 = sb("mask2", [P, 2, SC], BF16)
        ones = plain(9344, P)[0:1]

        PS = ctx.enter_context(nc.psum_tensor("banks", [P, 8, 512], F32))

        stage_in = [sem("stage_in_0"), sem("stage_in_1")]
        ctx_loaded, const_in, parked, consts = sem("ctx_loaded"), sem("const_in"), sem("parked"), sem("consts")
        tp_full, tp_hi, tp_free = sem("tp_full"), sem("tp_hi"), sem("tp_free")
        mm_full, mm_hi, mm_free = sem("mm_full"), sem("mm_hi"), sem("mm_free")
        split_hi, split_lo = sem("split_hi"), sem("split_lo")
        dve_p0, dve_p1, dve_p2, dve_p3 = sem("dve_p0"), sem("dve_p1"), sem("dve_p2"), sem("dve_p3")
        x_in = [sem("x_in_0"), sem("x_in_1")]
        x_normed, var_ready, rstd_ready, eps_added = (
            sem("x_normed"), sem("var_ready"), sem("rstd_ready"), sem("eps_added"))
        wv_in, wv_hi, wv_lo = sem("wv_in"), sem("wv_hi"), sem("wv_lo")
        s_full, s_free, counted = sem("s_full"), sem("s_free"), sem("counted")
        waited = sem("waited")
        mx_ready, p_ready, pt_free, z_free = sem("mx_ready"), sem("p_ready"), sem("pt_free"), sem("z_free")
        x1_ready = sem("x1_ready")
        x1_out = [sem("x1_out_0"), sem("x1_out_1")]
        vec2_in, cross_in, fcw_in = sem("vec2_in"), sem("cross_in"), sem("fcw_in")
        fcw_hi, fcw_lo = sem("fcw_hi"), sem("fcw_lo")
        len_in, len_seen = sem("len_in"), sem("len_seen")
        n_in = [sem("n_in_0"), sem("n_in_1")]
        c_full, c_free, sm_ready, e_ready = sem("c_full"), sem("c_free"), sem("sm_ready"), sem("e_ready")
        z2_full, x2_ready = sem("z2_full"), sem("x2_ready")
        h_full, hf_ready, h_hi, h_lo = sem("h_full"), sem("hf_ready"), sem("h_hi"), sem("h_lo")
        y_full, y_free = sem("y_full"), sem("y_free")
        xo_in, xg_ready = sem("xo_in"), sem("xg_ready")
        xg_out = [sem("xg_out_0"), sem("xg_out_1")]
        codes_seen = sem("codes_seen")
        q1_in, w1_ready, dequant = sem("q1_in"), sem("w1_ready"), sem("dequant")
        p2_end, vec3_in = sem("p2_end"), sem("vec3_in")
        q2_in = [sem("q2_in_0"), sem("q2_in_1")]
        w2_ready = sem("w2_ready")
        b_in = [sem("b_in_0"), sem("b_in_1")]
        hn_ready = sem("hn_ready")
        f_full, hf3_ready, f_hi, f_lo, hid_free = (
            sem("f_full"), sem("hf3_ready"), sem("f_hi"), sem("f_lo"), sem("hid_free"))
        o_full, o_free, sc2_in = sem("o_full"), sem("o_free"), sem("sc2_in")
        o_out = [sem("o_out_0"), sem("o_out_1")]

        block = ctx.enter_context(nc.Block())

        def bcast(v):
            return v.rearrange("(a e) -> a e", a=1).to_broadcast([P, v.shape[0]])

        def blocks(dram, t):
            return dram[bass.ds(t * TILE, TILE), :].rearrange("(k p) e -> p k e", p=P)

        def tiles(eng, body):
            with eng.Fori(0, NT // 2 - 1) as u:
                for slot in range(2):
                    body(u * 2 + slot, slot, False)
            body(NT - 2, 0, False)
            body(NT - 1, 1, True)

        @block.sync
        def _(sp):
            sp.sem_inc(x1_out[0], 16)
            sp.sem_inc(x1_out[1], 16)

            def weight(name, slot, done):
                sp.dma_start(stage[:, slot], a[name].rearrange("(c p) n -> p c n", p=P)).then_inc(done, 16)

            weight("L0_xattn_Wq1", 0, stage_in[0])
            weight("L0_xattn_Wk1", 1, stage_in[1])
            sp.dma_start(ctx_in[0:SC], a["ctx_1024"].rearrange("b s e -> s b e")).then_inc(ctx_loaded, 16)
            sp.dma_start(ln1[:, 0], bcast(a["L0_xattn_ln1_g"])).then_inc(const_in, 16)
            sp.dma_start(ln1[:, 1], bcast(a["L0_xattn_ln1_b"])).then_inc(const_in, 16)
            sp.dma_start(gate_x, bcast(a["g_xattn"])).then_inc(const_in, 16)
            sp.dma_start(gate_f, bcast(a["g_ffn"])).then_inc(const_in, 16)
            sp.dma_start(b1x, a["L0_xattn_fc1_b"].rearrange("(c p) -> p c", p=P),
                         allow_slow_non_contiguous=True).then_inc(const_in, 16)
            sp.dma_start(b1f, a["L0_ffn_fc1_bias"].rearrange("(c p) -> p c", p=P),
                         allow_slow_non_contiguous=True).then_inc(const_in, 16)
            sp.wait_ge(tp_full, C)
            weight("L0_xattn_Wq2", 0, stage_in[0])
            sp.wait_ge(tp_full, 2 * C)
            weight("L0_xattn_Wk2", 1, stage_in[1])
            sp.wait_ge(tp_full, 3 * C)
            weight("L0_xattn_Wv2", 0, stage_in[0])
            sp.wait_ge(mm_free, 2 + MM0)
            sp.dma_start(g_dram, g_0.rearrange("p c h n -> p (c h n)").bitcast(F32)).then_inc(parked, 16)
            sp.dma_start(v_dram, v_0[0:SC].rearrange("p c h n -> p (c h n)").bitcast(F32)).then_inc(parked, 16)
            sp.wait_ge(parked, 32)

            with sp.Fori(0, B) as b:
                sp.wait_ge(pt_free, 2 + b * PTK)
                weight("L0_xattn_Wv1", 0, wv_in)

                def load_x(k, blk):
                    if k < 2:
                        sp.wait_ge(z_free, b * NB + k + 1)
                    elif k < NB + 2:
                        sp.wait_ge(x_normed, b * NB + k - 1)
                    else:
                        sp.wait_ge(z_free, b * NB + k - NB + 1)
                    sp.dma_start(xin[:, k % 2], x_dram[bass.ds(b * S + blk * P, P), :]).then_inc(
                        x_in[k % 2], 16)

                for t in range(NB):
                    load_x(t, t)
                load_x(NB, 0)
                load_x(NB + 1, 1)
                for i in range(NB):
                    sp.wait_ge(x1_ready, b * NB + i + 1)
                    sp.dma_start(x1_dram[bass.ds(b * S + i * P, P), :], U[:, i % 2]).then_inc(
                        x1_out[i % 2], 16)
                    if i + 2 < NB:
                        load_x(NB + i + 2, i + 2)

            for p in range(2):
                sp.wait_ge(x1_out[p], 16 + 16 * B * NB // 2)
            sp.dma_start(G.rearrange("p c h n -> p (c h n)").bitcast(F32), g_dram).then_inc(cross_in, 16)
            sp.dma_start(V2[0:SC].rearrange("p c h n -> p (c h n)").bitcast(F32), v_dram).then_inc(
                cross_in, 16)
            sp.dma_start(xin[:, 0], x1_dram[0:P, :]).then_inc(len_in, 16)
            sp.dma_start(xin[:, 1], x1_dram[S:S + P, :]).then_inc(len_in, 16)
            weight("L0_xattn_fc1_w", 0, fcw_in)
            weight("L0_xattn_fc2_w", 1, fcw_in)
            sp.wait_ge(len_seen, 1)
            for n, v in enumerate(("ln2_g", "ln2_b", "ln3_g", "ln3_b", "fc2_b")):
                sp.dma_start(vec2[:, n], bcast(a[f"L0_xattn_{v}"])).then_inc(vec2_in, 16)
            sp.wait_ge(fcw_lo, 2 * C)

            for slot in range(2):
                sp.dma_start(N[:, slot], blocks(x1_dram, slot)).then_inc(n_in[slot], 16)

            def tile2(t, slot, last):
                for k in range(BT):
                    sp.wait_ge(xg_ready, t * BT + k + 1)
                    sp.dma_start(xo[:, 0], x_dram[bass.ds(t * TILE + k * P, P), :]).then_inc(xo_in, 16)
                sp.wait_ge(xg_ready, t * BT + BT + 1)
                sp.dma_start(blocks(xg_dram, t), N[:, slot]).then_inc(xg_out[slot], 16)

            with sp.Fori(0, NT // 2 - 1) as u:
                for slot in range(2):
                    tile2(u * 2 + slot, slot, False)
                    sp.wait_ge(xg_out[slot], u * 16 + 16)
                    sp.dma_start(N[:, slot], blocks(x1_dram, u * 2 + slot + 2)).then_inc(n_in[slot], 16)
            for slot in range(2):
                tile2(NT - 2 + slot, slot, True)

            for slot in range(2):
                sp.wait_ge(xg_out[slot], NT // 2 * 16)
            sp.wait_ge(p2_end, 1)
            for n, v in enumerate(("ln_gamma", "ln_beta", "fc2_bias")):
                sp.dma_start(vec3[:, n], bcast(a[f"L0_ffn_{v}"])).then_inc(vec3_in, 16)
            for slot in range(2):
                sp.dma_start(base[:, slot], blocks(xg_dram, slot)).then_inc(b_in[slot], 16)
            with sp.Fori(0, NT // 2 - 1) as u:
                for slot in range(2):
                    sp.wait_ge(o_free, (u * 2 + slot) * BT + 2 * BT)
                    sp.dma_start(blocks(out_dram, u * 2 + slot), base[:, slot]).then_inc(o_out[slot], 16)
                    sp.wait_ge(o_out[slot], u * 16 + 16)
                    sp.dma_start(base[:, slot], blocks(xg_dram, u * 2 + slot + 2)).then_inc(b_in[slot], 16)
            for slot in range(2):
                sp.wait_ge(o_free, (NT - 2 + slot) * BT + 2 * BT)
                sp.dma_start(blocks(out_dram, NT - 2 + slot), base[:, slot]).then_inc(o_out[slot], 16)
            for slot in range(2):
                sp.wait_ge(o_out[slot], NT // 2 * 16)

        @block.tensor
        def _(pe):
            pe.sem_inc(pt_free, 2)
            pe.sem_inc(hid_free, 2)
            pe.wait_ge(consts, 3)

            def product(out, left, right, chunks, done=None, start=True, stop=True):
                for c in range(chunks):
                    for l, r in PASSES:
                        mm = nc.tensor.matmul(out, left(c, l), right(c, r),
                                              start=start and c == 0 and (l, r) == PASSES[0],
                                              stop=stop and c == chunks - 1 and (l, r) == PASSES[-1])
                if done is not None:
                    mm.then_inc(done, 1)
                return mm

            def turn(bank, block_of, inc=1):
                for c in range(C):
                    mm = nc.tensor.transpose(bank[:, c * P:(c + 1) * P], block_of(c), ident[:])
                mm.then_inc(tp_full, inc)

            def turn_weight(k0, slot):
                for j in range(C):
                    pe.wait_ge(tp_free, k0 + j + 1)
                    turn(PS[:, 2 + j % 2], lambda e: stage[:, slot, e, j * P:(j + 1) * P])

            pe.wait_ge(stage_in[0], 16)
            turn_weight(0, 0)
            pe.wait_ge(stage_in[1], 16)
            turn_weight(C, 1)
            pe.wait_ge(stage_in[0], 32)
            turn_weight(2 * C, 0)
            pe.wait_ge(ctx_loaded, 16)
            for c in range(C):
                pe.wait_ge(tp_free, 3 * C + c + 1)
                for b in range(B):
                    mm = nc.tensor.transpose(PS[:, 2 + c % 2, b * SCP:b * SCP + SC],
                                             ctx_in[0:SC, b, c * P:(c + 1) * P], ident[0:SC, 0:SC])
                mm.then_inc(tp_full, 1)

            k = 0
            for m in range(C):
                pe.wait_ge(tp_free, 2 + 2 * C)
                pe.wait_ge(mm_free, k + 1)
                product(PS[:, 4 + k % 2], lambda j, h: wq1T[:, j, h, m * P:(m + 1) * P],
                        lambda j, h: wk1T[:, j, h, :], C, mm_full)
                k += 1
            pe.wait_ge(tp_free, 2 + TP0)
            for m in range(C):
                pe.wait_ge(split_lo, C)
                pe.wait_ge(mm_free, k + 1)
                product(PS[:, 4 + k % 2, 0:2 * SCP], lambda c, h: wk2[:, c, h, m * P:(m + 1) * P],
                        lambda c, h: ctxT[:, c, h, :], C, mm_full)
                k += 1
            for b in range(B):
                pe.wait_ge(split_lo, 2 * C)
                pe.wait_ge(mm_free, k + 1)
                product(PS[0:SC, 4 + k % 2], lambda c, h: ctxT[:, c, h, b * SCP:b * SCP + SC],
                        lambda c, h: wv2[:, c, h, :], C, mm_full)
                k += 1
            for m in range(C):
                pe.wait_ge(mm_free, max(2 + 2 * C, k + 1))
                product(PS[:, 4 + k % 2, 0:2 * SCP], lambda j, h: wq2T[:, j, h, m * P:(m + 1) * P],
                        lambda j, h: kT2[:, j, h, :], C, mm_full)
                k += 1

            with pe.Fori(0, B) as b:
                def turn_x(t):
                    pe.wait_ge(x_normed, b * NB + t + 1)
                    pe.wait_ge(tp_free, b * TP1 + TP0 + t + 1)
                    turn(PS[:, 2 + t % 2], lambda c: xn[:, t % 2, c * P:(c + 1) * P])

                def values(t):
                    if t == 0:
                        pe.wait_ge(wv_lo, b * C + C)
                    pe.wait_ge(tp_free, b * TP1 + 2 + TP0 + t + 1)
                    pe.wait_ge(mm_free, b * MM1 + MM0 + t + 1)
                    product(PS[:, 4 + t % 2], lambda c, h: xT[:, c, h, t * P:(t + 1) * P],
                            lambda c, h: wv[:, c, h, :], C, mm_full)

                def queries(g, m):
                    pe.wait_ge(mm_free, b * MM1 + MM0 + NB + g * C + m + 1)
                    product(PS[:, 4 + m % 2], lambda c, h: A[:, c, h, m * P:(m + 1) * P],
                            lambda c, h: xT[:, c, h, g * 512:(g + 1) * 512], C, mm_full)

                def score(k, q, lo, w):
                    pe.wait_ge(s_free, b * SS1 + k + 1)
                    product(PS[:, k % 2, 0:w], lambda m, h: QT[:, m, h, q * P:(q + 1) * P],
                            lambda m, h: xT[:, m, h, lo:lo + w], C, s_full)

                turn_x(0)
                for t in range(1, NB):
                    turn_x(t)
                    values(t - 1)
                values(NB - 1)
                for m in range(C):
                    queries(0, m)
                pe.wait_ge(mm_free, b * MM1 + 2 + MM0 + NB + C)
                for c in range(4):
                    score(c, 0, c * 512, 512)
                pe.wait_ge(s_free, b * SS1 + 5)
                pe.wait_ge(counted, b + 1)
                nc.tensor.matmul(PS[:, 0, 0:1], ones, keys_seen[0:1], start=True, stop=True).then_inc(
                    s_full, 2)

                for kind, i, c in ORDER:
                    if kind == "S":
                        if i % 4 == 0 and c == 0 and i:
                            pe.wait_ge(mm_free, b * MM1 + 2 + MM0 + NB + C * (i // 4 + 1))
                        score(6 + T_BEFORE[i] + c, i % 4, c * 512, width_of(i, c))
                    elif kind == "Q":
                        queries(i, c)
                    elif kind == "T":
                        k = NB + T_BEFORE[i] + c
                        if c == 0:
                            pe.wait_ge(p_ready, b * NB + i + 1)
                        pe.wait_ge(tp_free, b * TP1 + TP0 + k + 1)
                        for j in range(width_of(i, c) // P):
                            lo = c * 512 + j * P
                            mm = nc.tensor.transpose(PS[:, 2 + k % 2, j * P:(j + 1) * P],
                                                     Srow[:, i % 2, lo:lo + P], ident[:])
                        mm.then_inc(tp_full, 1)
                    elif kind == "V":
                        k = T_BEFORE[i] + c
                        if c == 0:
                            pe.wait_ge(z_free, b * NB + i + 1)
                        pe.wait_ge(tp_free, b * TP1 + 2 + TP0 + NB + k + 1)
                        n = width_of(i, c) // P
                        product(PS[:, 6 + i % 2], lambda j, h: PT[:, k % 2, h, j * P:(j + 1) * P],
                                lambda j, h: V[:, c * 4 + j, h, :], n, pt_free,
                                start=c == 0, stop=c == i // 4)

            pe.wait_ge(s_free, 2 + B * SS1)
            pe.wait_ge(mm_free, 2 + MM2)
            pe.wait_ge(z_free, 2 + B * NB)
            pe.wait_ge(cross_in, 32)
            pe.wait_ge(len_in, 32)
            for b in range(B):
                pe.wait_ge(tp_free, TP2 + b + 1)
                turn(PS[:, 2 + b % 2], lambda c: xin[:, b, c * P:(c + 1) * P])
            pe.wait_ge(tp_free, 2 + TP2 + B)
            for b in range(B):
                mm = product(PS[:, 0, b * SCP:(b + 1) * SCP], lambda c, h: x1T[:, c, h, b * P:(b + 1) * P],
                             lambda c, h: G[:, c, h, b * SCP:(b + 1) * SCP], C)
            mm.then_inc(c_full, 1)
            pe.wait_ge(counted, B + 1)
            nc.tensor.matmul(PS[:, 1, 0:B], ones, keys_seen2[0:1], start=True, stop=True).then_inc(c_full, 1)

            def cross_scores(t, slot, first=False):
                if first:
                    pe.wait_ge(n_in[slot], 16)
                else:
                    pe.wait_ge(n_in[slot], (t // 2) * 16 + 16)
                for k in range(BT):
                    pe.wait_ge(tp_free, t * TPT + TP2 + TPL + k + 1)
                    turn(PS[:, 2 + k % 2], lambda c: N[:, slot, k, c * P:(c + 1) * P])
                pe.wait_ge(c_free, t + 1)
                for k in range(BT):
                    pe.wait_ge(tp_free, t * TPT + 2 + TP2 + TPL + k + 1)
                    mm = product(PS[:, 0, k * SCP:(k + 1) * SCP],
                                 lambda c, h: x1T[:, c, h, k * P:(k + 1) * P],
                                 lambda c, h: G[:, c, h, bass.ds((t // TPB) * SCP, SCP)], C)
                mm.then_inc(c_full, 1)

            def cross_values(t, slot):
                pe.wait_ge(e_ready, t + 1)
                pe.wait_ge(tp_free, t * TPT + TP2 + TPL + BT + 1)
                for k in range(BT):
                    mm = nc.tensor.transpose(PS[0:SC, 2, k * P:(k + 1) * P],
                                             S2[:, slot, k * SCP:k * SCP + SC], ident[:])
                mm.then_inc(tp_full, 2)
                pe.wait_ge(tp_free, t * TPT + 2 + TP2 + TPL + BT + 2)
                for k in range(BT):
                    pe.wait_ge(z_free, t * BT + B * NB + k + 1)
                    product(PS[:, 6 + k % 2], lambda _, h: PT2[0:SC, 0, h, k * P:(k + 1) * P],
                            lambda _, h: V2[0:SC, bass.ds(t // TPB, 1), h, :].rearrange("p a n -> p (a n)"),
                            1, z2_full)

            def turn_x2(t, slot):
                for k in range(BT):
                    pe.wait_ge(x2_ready, t * BT + k + 1)
                    pe.wait_ge(tp_free, t * TPT + TP2 + TPL + BT + 2 + k + 1)
                    turn(PS[:, 2 + k % 2], lambda c: N[:, slot, k, c * P:(c + 1) * P])

            def mlp_in(t):
                pe.wait_ge(tp_free, t * TPT + 2 + TP2 + TPL + TPT)
                for f in range(C):
                    if f < 2:
                        pe.wait_ge(y_free, t * BT + f + 3)
                    else:
                        pe.wait_ge(hf_ready, t * C + f - 1)
                    product(PS[:, 4 + f % 2], lambda c, h: fc1[:, c, h, f * P:(f + 1) * P],
                            lambda c, h: x2T[:, c, h, :], C, h_full)

            def mlp_out(t):
                pe.wait_ge(h_lo, t * C + 2 + C)
                for k in range(BT):
                    if k > 1:
                        pe.wait_ge(y_free, t * BT + 4 + k - 1)
                    product(PS[:, 4 + k % 2], lambda f, h: hid2[:, f, h, k * P:(k + 1) * P],
                            lambda f, h: fc2[:, f, h, :], C, y_full)

            cross_scores(0, 0, True)
            cross_values(0, 0)
            turn_x2(0, 0)
            pe.wait_ge(fcw_lo, 2 * C)

            def tile2(t, slot, last):
                mlp_in(t)
                if not last:
                    cross_scores(t + 1, 1 - slot)
                mlp_out(t)
                if not last:
                    cross_values(t + 1, 1 - slot)
                    turn_x2(t + 1, 1 - slot)

            tiles(pe, tile2)

            pe.wait_ge(p2_end, 1)

            def turn_h(t, slot, k):
                pe.wait_ge(hn_ready, t * BT + k + 1)
                pe.wait_ge(tp_free, t * BT + TP3 + k + 1)
                turn(PS[:, 2 + k % 2], lambda c: H0[:, k % 2, c * P:(c + 1) * P])

            def ffn_in(t, slot, f):
                if f == 0:
                    pe.wait_ge(tp_free, t * BT + 2 + TP3 + BT)
                pe.wait_ge(hf3_ready, t * NF + f + 1)
                product(PS[:, f % 2], lambda c, h: W1[:, c, h, f * P:(f + 1) * P],
                        lambda c, h: hT[:, slot * C + c, h, :], C, f_full)

            def ffn_out(t, f):
                pe.wait_ge(f_lo, t * NF + 2 + f + 1)
                pe.wait_ge(w2_ready, f + 1)
                for k in range(BT):
                    if f == 0:
                        pe.wait_ge(o_free, t * BT + k + 1)
                    mm = product(PS[:, 4 + k], lambda _, h: hid3[:, f % 2, h, k * P:(k + 1) * P],
                                 lambda _, h: W2[:, f, h, :], 1,
                                 o_full if f == NF - 1 and k < BT - 1 else None,
                                 start=f == 0, stop=f == NF - 1)
                mm.then_inc(hid_free, 1)

            for k in range(BT):
                turn_h(0, 0, k)
            pe.wait_ge(w1_ready, 8 * C)
            ffn_in(0, 0, 0)

            def tile3(t, slot, last):
                for f in range(NF):
                    if f + 1 < NF:
                        ffn_in(t, slot, f + 1)
                    elif not last:
                        ffn_in(t + 1, 1 - slot, 0)
                    ffn_out(t, f)
                    if f in TURN_AT and not last:
                        turn_h(t + 1, 1 - slot, TURN_AT.index(f))

            tiles(pe, tile3)

        @block.scalar
        def _(act):
            nc.scalar.preload_act_table(ACT.Exp)
            copy = ACT.Copy

            def hi(k, dst, src, turn=0, per=0, sems=(tp_full, tp_hi), inc=1):
                act.wait_ge(sems[0], turn * per + k + 1)
                nc.scalar.activation(dst, src, copy).then_inc(sems[1], inc)

            def thirds(bank):
                return bank.rearrange("p (c n) -> p c n", c=C)

            for k in range(3 * C):
                w = (wq1T, wk1T, wq2T)[k // C]
                hi(k, w[:, k % C, 0, :], PS[:, 2 + k % 2])
            for c in range(C):
                hi(3 * C + c, ctxT[:, c, 0, :].rearrange("p (b n) -> p b n", b=B)[:, :, 0:SC],
                   PS[:, 2 + c % 2, 0:2 * SCP].rearrange("p (b n) -> p b n", b=B)[:, :, 0:SC])

            def split_stage(slot, loaded, w, done):
                act.wait_ge(loaded[0], loaded[1])
                for c in range(C):
                    nc.scalar.activation(w[:, c, 0, :], stage[:, slot, c], copy).then_inc(done, 1)

            split_stage(1, (stage_in[1], 32), wk2, split_hi)
            for m in range(C):
                hi(m, A[:, m, 0, :], PS[:, 4 + m % 2], sems=(mm_full, mm_hi))
            split_stage(0, (stage_in[0], 48), wv2, split_hi)
            for m in range(C):
                hi(C + m, kT2[:, m, 0, :], PS[:, 4 + m % 2, 0:2 * SCP], sems=(mm_full, mm_hi))
            for b in range(B):
                hi(2 * C + b, v_0[0:SC, b, 0, :], PS[0:SC, 4 + b % 2], sems=(mm_full, mm_hi))
            for m in range(C):
                hi(2 * C + B + m, g_0[:, m, 0, :], PS[:, 4 + m % 2, 0:2 * SCP], sems=(mm_full, mm_hi))
            act.wait_ge(const_in, 16 * 6)
            nc.scalar.activation(gate_x, gate_x, ACT.Tanh).then_inc(split_hi, 1)
            nc.scalar.activation(gate_f, gate_f, ACT.Tanh).then_inc(split_hi, 1)

            with act.Fori(0, B) as b:
                def hi_x(t):
                    hi(TP0 + t, xT[:, :, 0, t * P:(t + 1) * P], thirds(PS[:, 2 + t % 2]), b, TP1)

                def hi_v(t):
                    hi(MM0 + t, V[:, t, 0, :], PS[:, 4 + t % 2], b, MM1, (mm_full, mm_hi))

                def hi_q(g, m):
                    hi(MM0 + NB + g * C + m, QT[:, m, 0, :], PS[:, 4 + m % 2], b, MM1, (mm_full, mm_hi))

                hi_x(0)
                act.wait_ge(wv_in, b * 16 + 16)
                for c in range(C):
                    nc.scalar.activation(wv[:, c, 0, :], stage[:, 0, c], copy).then_inc(wv_hi, 1)
                for t in range(1, NB):
                    hi_x(t)
                    hi_v(t - 1)
                hi_v(NB - 1)
                for m in range(C):
                    hi_q(0, m)
                for kind, i, c in ORDER:
                    if kind == "S" and c == i // 4:
                        w = i // 4 * 512 + width_of(i, i // 4)
                        act.wait_ge(mx_ready, b * NB + i + 1)
                        nc.scalar.activation(Srow[:, i % 2, 0:w], Srow[:, i % 2, 0:w], ACT.Exp,
                                             bias=nb[:, i % 2:i % 2 + 1], scale=SCALE,
                                             accum_out=rowsum[:, i % 4:i % 4 + 1]).then_inc(p_ready, 1)
                    elif kind == "Q":
                        hi_q(i, c)
                    elif kind == "T":
                        k, w = T_BEFORE[i] + c, width_of(i, c)
                        act.wait_ge(pt_free, b * PTK + k + 1)
                        hi(TP0 + NB + k, PT[:, k % 2, 0, 0:w], PS[:, 2 + k % 2, 0:w], b, TP1)

            for b in range(B):
                hi(TP2 + b, x1T[:, :, 0, b * P:(b + 1) * P], thirds(PS[:, 2 + b % 2]))

            def hi_x1(t):
                for k in range(BT):
                    hi(TP2 + TPL + k, x1T[:, :, 0, k * P:(k + 1) * P], thirds(PS[:, 2 + k % 2]), t, TPT)

            def probs(t, slot):
                act.wait_ge(sm_ready, t + 1)
                s = S2[:, slot, :].rearrange("p (k n) -> p k n", k=BT)[:, :, 0:SC]
                nc.scalar.activation(s, s, ACT.Exp, scale=SCALE).then_inc(e_ready, 1)

            def hi_p(t):
                hi(TP2 + TPL + BT + 1, PT2[0:SC, 0, 0, :], PS[0:SC, 2], t, TPT, inc=2)

            def hi_x2(t):
                for k in range(BT):
                    hi(TP2 + TPL + BT + 2 + k, x2T[:, :, 0, k * P:(k + 1) * P],
                       thirds(PS[:, 2 + k % 2]), t, TPT)

            act.wait_ge(fcw_in, 32)
            for slot, w in ((0, fc1), (1, fc2)):
                for c in range(C):
                    nc.scalar.activation(w[:, c, 0, :], stage[:, slot, c], copy).then_inc(fcw_hi, 1)
            hi_x1(0)
            probs(0, 0)
            hi_p(0)
            hi_x2(0)

            def tile2(t, slot, last):
                for f in range(C):
                    act.wait_ge(h_full, t * C + f + 1)
                    act.wait_ge(h_lo, t * C + f + 1)
                    nc.scalar.activation(HF2[:, f % 2], PS[:, 4 + f % 2], ACT.Relu,
                                         bias=b1x[:, f:f + 1]).then_inc(hf_ready, 1)
                    act.wait_ge(hf_ready, t * C + f + 1)
                    nc.scalar.activation(hid2[:, f, 0, :], HF2[:, f % 2], copy).then_inc(h_hi, 1)
                if not last:
                    hi_x1(t + 1)
                    probs(t + 1, 1 - slot)
                    hi_p(t + 1)
                    hi_x2(t + 1)

            tiles(act, tile2)

            nc.scalar.preload_act_table(ACT.Silu)
            act.sem_inc(hf3_ready, 2)

            def hi_h(t, slot, k):
                hi(TP3 + k, hT[:, slot * C:(slot + 1) * C, 0, k * P:(k + 1) * P],
                   thirds(PS[:, 2 + k % 2]), t, BT)

            for k in range(BT):
                hi_h(0, 0, k)

            def tile3(t, slot, last):
                for f in range(NF):
                    act.wait_ge(f_full, t * NF + f + 1)
                    act.wait_ge(f_lo, t * NF + f + 1)
                    nc.scalar.activation(HF3[:, f % 2], PS[:, f % 2], ACT.Silu,
                                         bias=b1f[:, f:f + 1]).then_inc(hf3_ready, 1)
                    act.wait_ge(hf3_ready, t * NF + 2 + f + 1)
                    act.wait_ge(hid_free, t * NF + f + 1)
                    nc.scalar.activation(hid3[:, f % 2, 0, :], HF3[:, f % 2], copy).then_inc(f_hi, 1)
                    if f in TURN_AT and not last:
                        hi_h(t + 1, 1 - slot, TURN_AT.index(f))

            tiles(act, tile3)

        @block.gpsimd
        def _(pool):
            nc.gpsimd.memset(ident[:], 0.0).then_inc(dequant, 1)
            nc.gpsimd.memset(tri[:], 0.0).then_inc(dequant, 1)
            nc.gpsimd.memset(half, -0.5)
            nc.gpsimd.memset(eps_col, EPS).then_inc(dequant, 1)
            pool.wait_ge(dequant, 3)
            nc.gpsimd.affine_select(out=ident[:], in_=ident[:], compare_op=ALU.not_equal, fill=1.0, base=0,
                                    pattern=[[-1, P]], channel_multiplier=1).then_inc(consts, 1)
            nc.gpsimd.affine_select(out=tri[:], in_=tri[:], compare_op=ALU.is_ge, fill=-BIG, base=0,
                                    pattern=[[-1, P]], channel_multiplier=1).then_inc(consts, 1)
            nc.gpsimd.iota(keys[:], [[1, 512]], base=0, channel_multiplier=0).then_inc(consts, 1)

            def rstd(n, var, out, turn=0, per=0):
                pool.wait_ge(var_ready, turn * per + n + 1)
                nc.gpsimd.tensor_tensor(out, var, eps_col.to_broadcast(list(out.shape)), ALU.add).then_inc(eps_added, 1)
                pool.wait_ge(eps_added, turn * per + n + 1)
                nc.gpsimd.tensor_tensor(out, out, half.to_broadcast(list(out.shape)), ALU.pow).then_inc(
                    rstd_ready, 1)

            with pool.Fori(0, B) as b:
                for t in range(NB):
                    rstd(t, mv1[:, t, 1:2], rs1[:, t:t + 1], b, 2 * NB)
                for i in range(NB):
                    rstd(NB + i, mvE[:, i % 2, 1:2], rsE[:, i % 2:i % 2 + 1], b, 2 * NB)

            R2 = 2 * NB * B

            def norm2(n):
                for k in range(BT):
                    rstd(R2 + n + k, mvE[:, k, 1:2], rsE[:, k:k + 1])

            def norms2(t, first):
                for k in range(BT):
                    rstd(R2 + BT + first + k, mvE[:, k, 1:2], rsE[:, k:k + 1], t, 2 * BT)

            def dequant_w1(u, j):
                cols = slice(j * 256, (j + 1) * 256)
                nc.gpsimd.dma_start(q1.bitcast(I32), a["L0_ffn_fc1_q"][bass.ds(u * P, P), cols]).then_inc(
                    q1_in, 16)
                nc.gpsimd.dma_start(sc1, a["L0_ffn_fc1_scales"][bass.ds(u, 1), cols].to_broadcast(
                    [P, 256])).then_inc(q1_in, 16)
                pool.wait_ge(q1_in, u * 8 * 32 + j * 32 + 32)
                n = 3 + j * 3
                pool.sem_inc(codes_seen, 1)
                nc.gpsimd.tensor_scalar(q1, q1.bitcast(I32), -128.0, None, ALU.add).then_inc(dequant, 1)
                pool.wait_ge(dequant, u * 24 + n + 1)
                nc.gpsimd.tensor_tensor(q1, q1, sc1, ALU.mult).then_inc(dequant, 1)
                pool.wait_ge(dequant, u * 24 + n + 2)
                w = [W1[:, bass.ds(u, 1), h, cols].rearrange("p a n -> p (a n)") for h in range(2)]
                nc.gpsimd.tensor_copy(w[0], q1).then_inc(dequant, 1)
                pool.wait_ge(dequant, u * 24 + n + 3)
                nc.gpsimd.tensor_tensor(w[1], q1, w[0].bitcast(F32), ALU.subtract).then_inc(w1_ready, 1)
                pool.wait_ge(w1_ready, u * 8 + j + 1)

            norm2(0)
            pool.wait_ge(len_seen, 1)

            def tile2(t, u, slot, last):
                norms2(t, 0)
                for j in range(4):
                    dequant_w1(u, slot * 4 + j)
                if not last:
                    norms2(t, BT)

            with pool.Fori(0, NT // 2 - 1) as u:
                for slot in range(2):
                    tile2(u * 2 + slot, u, slot, False)
            tile2(NT - 2, NT // 2 - 1, 0, False)
            tile2(NT - 1, NT // 2 - 1, 1, True)

            R3 = R2 + NT * 2 * BT
            D3 = 3 + 24 * (NT // 2)

            def rstd_of_x(t):
                rstd(R3, mvX[:, :, 1], rs_x, t, 1 + BT)

            def rstd_of_h0(t, k):
                rstd(R3 + 1 + k, mvE[:, k, 1:2], rsE[:, k:k + 1], t, 1 + BT)

            def load_w2(f):
                nc.gpsimd.dma_start(q2[:, f % 2].bitcast(I32), a["L0_ffn_fc2_q"][f * P:(f + 1) * P, :]).then_inc(
                    q2_in[f % 2], 16)

            def dequant_w2(f):
                if f + 1 < NF:
                    load_w2(f + 1)
                nc.gpsimd.dma_start(sc2, a["L0_ffn_fc2_scales"][f:f + 1, :].to_broadcast([P, E])).then_inc(
                    sc2_in, 16)
                pool.wait_ge(q2_in[f % 2], 16 * (f // 2 + 1))
                pool.wait_ge(sc2_in, 16 * (f + 1))
                q, n = q2[:, f % 2], D3 + f * 3
                nc.gpsimd.tensor_scalar(q, q.bitcast(I32), -128.0, None, ALU.add).then_inc(dequant, 1)
                pool.wait_ge(dequant, n + 1)
                nc.gpsimd.tensor_tensor(q, q, sc2, ALU.mult).then_inc(dequant, 1)
                pool.wait_ge(dequant, n + 2)
                nc.gpsimd.tensor_copy(W2[:, f, 0, :], q).then_inc(dequant, 1)
                pool.wait_ge(dequant, n + 3)
                nc.gpsimd.tensor_tensor(W2[:, f, 1, :], q, W2[:, f, 0, :].bitcast(F32), ALU.subtract).then_inc(
                    w2_ready, 1)
                pool.wait_ge(w2_ready, f + 1)

            pool.wait_ge(p2_end, 1)
            load_w2(0)
            rstd_of_x(0)
            for k in range(BT):
                rstd_of_h0(0, k)
            for f in range(NF):
                dequant_w2(f)
                if f == 5:
                    rstd_of_x(1)
                if f in (6, 8, 10, 12):
                    rstd_of_h0(1, (f - 6) // 2)
            with pool.Fori(2, NT) as t:
                rstd_of_x(t)
                for k in range(BT):
                    rstd_of_h0(t, k)

        @block.vector
        def _(dve):
            for s, n in ((tp_free, 2), (mm_free, 2), (s_free, 2), (z_free, 2), (y_free, 4), (h_lo, 2),
                         (f_lo, 2), (o_free, 4), (xg_ready, 1)):
                dve.sem_inc(s, n)

            def lo(k, dst, src, hi_part, turn=0, per=0, sems=(tp_hi, tp_free), inc=1):
                dve.wait_ge(sems[0], turn * per + k + 1)
                nc.vector.tensor_tensor(dst, src, hi_part.bitcast(F32), ALU.subtract).then_inc(sems[1], inc)

            def thirds(bank):
                return bank.rearrange("p (c n) -> p c n", c=C)

            def apart():
                dve.sem_inc(waited, 1)

            p0 = Steps(dve, dve_p0)
            for at in (SC, SCP + SC):
                p0.done(nc.vector.memset(ctxT[:, :, :, at:at + SCP - SC].bitcast(F32), 0.0))
            p0.done(nc.vector.memset(ones, 1.0))
            dve.wait_ge(consts, 3)

            for k in range(3 * C):
                w = (wq1T, wk1T, wq2T)[k // C]
                lo(k, w[:, k % C, 1, :], PS[:, 2 + k % 2], w[:, k % C, 0, :])
            for c in range(C):
                half_of = [ctxT[:, c, h, :].rearrange("p (b n) -> p b n", b=B)[:, :, 0:SC] for h in range(2)]
                lo(3 * C + c, half_of[1],
                   PS[:, 2 + c % 2, 0:2 * SCP].rearrange("p (b n) -> p b n", b=B)[:, :, 0:SC], half_of[0])

            def split_stage(slot, w, his, n0, done):
                for c in range(C):
                    dve.wait_ge(his, n0 + c + 1)
                    nc.vector.tensor_tensor(w[:, c, 1, :], stage[:, slot, c], w[:, c, 0, :].bitcast(F32),
                                            ALU.subtract).then_inc(done, 1)

            mm = (mm_hi, mm_free)
            split_stage(1, wk2, split_hi, 0, split_lo)
            for m in range(C):
                lo(m, A[:, m, 1, :], PS[:, 4 + m % 2], A[:, m, 0, :], sems=mm)
            split_stage(0, wv2, split_hi, C, split_lo)
            for m in range(C):
                lo(C + m, kT2[:, m, 1, :], PS[:, 4 + m % 2, 0:2 * SCP], kT2[:, m, 0, :], sems=mm)
            for b in range(B):
                lo(2 * C + b, v_0[0:SC, b, 1, :], PS[0:SC, 4 + b % 2], v_0[0:SC, b, 0, :], sems=mm)
            for m in range(C):
                lo(2 * C + B + m, g_0[:, m, 1, :], PS[:, 4 + m % 2, 0:2 * SCP], g_0[:, m, 0, :], sems=mm)
            dve.wait_ge(split_hi, 2 * C + 2)
            p0.link(nc.vector.tensor_scalar(gf_half, gate_f, 0.5, None, ALU.mult))

            def statistics(steps, x, mv, k):
                steps.link(nc.vector.bn_stats(st[:, k % 2], x))
                apart()
                nc.vector.bn_aggr(mv, st[:, k % 2]).then_inc(var_ready, 1)

            def scale_shift(steps, x, mean, rs, g, b, done):
                steps.link(nc.vector.scalar_tensor_tensor(out=x, in0=x, scalar=mean, in1=g,
                                                          op0=ALU.subtract, op1=ALU.mult))
                nc.vector.scalar_tensor_tensor(out=x, in0=x, scalar=rs, in1=b,
                                               op0=ALU.mult, op1=ALU.add).then_inc(done, 1)

            with dve.Fori(0, B) as b:
                p1 = Steps(dve, dve_p1, DVE1, b)

                def stats_x(t):
                    dve.wait_ge(x_in[t % 2], b * NB * 16 + (t // 2 + 1) * 16)
                    statistics(p1, xin[:, t % 2], mv1[:, t], t)

                def norm_x(t):
                    dve.wait_ge(rstd_ready, b * 2 * NB + t + 1)
                    dve.wait_ge(tp_full, b * TP1 + TP0 + max(t - 1, 0))
                    nc.vector.tensor_scalar(xn[:, t % 2], xin[:, t % 2], mv1[:, t, 0:1], rs1[:, t:t + 1],
                                            ALU.subtract, ALU.mult).then_inc(x_normed, 1)

                def lo_x(t):
                    half_of = [xT[:, :, h, t * P:(t + 1) * P] for h in range(2)]
                    lo(TP0 + t, half_of[1], thirds(PS[:, 2 + t % 2]), half_of[0], b, TP1)

                def lo_v(t):
                    lo(MM0 + t, V[:, t, 1, :], PS[:, 4 + t % 2], V[:, t, 0, :], b, MM1, mm)

                def lo_q(g, m):
                    lo(MM0 + NB + g * C + m, QT[:, m, 1, :], PS[:, 4 + m % 2], QT[:, m, 0, :], b, MM1, mm)

                stats_x(0)
                for t in range(NB + 2):
                    if t + 1 < NB:
                        stats_x(t + 1)
                    if t < NB:
                        norm_x(t)
                    if 1 <= t <= NB:
                        lo_x(t - 1)
                    if t == 1:
                        for c in range(C):
                            dve.wait_ge(wv_hi, b * C + c + 1)
                            nc.vector.tensor_tensor(wv[:, c, 1, :], stage[:, 0, c],
                                                    wv[:, c, 0, :].bitcast(F32),
                                                    ALU.subtract).then_inc(wv_lo, 1)
                    if t >= 2:
                        lo_v(t - 2)
                for m in range(C):
                    lo_q(0, m)
                for c in range(4):
                    dve.wait_ge(s_full, b * SS1 + c + 1)
                    if c > 1:
                        dve.wait_ge(s_free, b * SS1 + 2 + c - 1)
                    nc.vector.tensor_scalar(xn[0:1, c % 2], PS[0:1, c % 2], 0.0, None, ALU.not_equal, ALU.add,
                                            accum_out=cnt[0:1, c:c + 1]).then_inc(s_free, 1)
                dve.wait_ge(s_free, b * SS1 + 2 + 4)
                nc.vector.tensor_reduce(keys_seen[0:1], cnt[0:1], AX.X, ALU.add).then_inc(counted, 1)
                dve.wait_ge(s_full, b * SS1 + 6)
                for c in range(4):
                    ins = nc.vector.tensor_scalar(lnc[:, c:c + 1], PS[:, 0, 0:1], -512.0 * c, None, ALU.add)
                    if c < 3:
                        p1.done(ins)
                ins.then_inc(s_free, 2)
                dve.wait_ge(s_free, b * SS1 + 2 + 6)
                for c in range(4):
                    last = p1.done(nc.vector.tensor_scalar(pad[:, c * 512:(c + 1) * 512], keys[:],
                                                           lnc[:, c:c + 1], -BIG, ALU.is_ge, ALU.mult))
                p1.wait(last)
                p1.link(nc.vector.reciprocal(ln, lnc[:, 0:1]))
                p1.link(nc.vector.tensor_scalar(ln, ln, 0.0, None, ALU.mult))
                p1.link(nc.vector.tensor_scalar(pad, pad, ln, None, ALU.add))

                def scores(i, c):
                    k, w, at = 6 + T_BEFORE[i] + c, width_of(i, c), c * 512
                    bank, row = PS[:, k % 2], Srow[:, i % 2]
                    dve.wait_ge(s_full, b * SS1 + k + 1)
                    if c == 0:
                        dve.wait_ge(tp_full, b * TP1 + TP0 + (NB + T_BEFORE[i - 1] if i > 1 else 0))

                    def masked_max(lo_, n, src, m):
                        apart()
                        return nc.vector.tensor_tensor_reduce(
                            out=row[:, at + lo_:at + lo_ + n], in0=src, in1=pad[:, at + lo_:at + lo_ + n],
                            scale=1.0, scalar=-3.4e38, op0=ALU.add, op1=ALU.max, accum_out=mx[:, i % 2, m:m + 1])

                    if c < i // 4:
                        masked_max(0, w, bank[:, 0:w], c).then_inc(s_free, 1)
                        return
                    d = w - P
                    if d:
                        p1.done(masked_max(0, d, bank[:, 0:d], c))
                    nc.vector.tensor_tensor(row[:, at + d:at + w], bank[:, d:w], tri[:], ALU.add).then_inc(
                        s_free, 1)
                    dve.wait_ge(s_free, b * SS1 + 2 + k + 1)
                    n = c + (2 if d else 1)
                    p1.link(masked_max(d, P, row[:, at + d:at + w], n - 1))
                    p1.link(nc.vector.tensor_reduce(nmx[:, 0:1], mx[:, i % 2, 0:n], AX.X, ALU.max))
                    nc.vector.tensor_scalar(nb[:, i % 2:i % 2 + 1], nmx[:, 0:1], -SCALE, None,
                                            ALU.mult).then_inc(mx_ready, 1)

                def end_a(i):
                    dve.wait_ge(x_in[i % 2], b * NB * 16 + (NB // 2 + i // 2 + 1) * 16)
                    p1.done(nc.vector.tensor_scalar(xin[:, i % 2], xin[:, i % 2], mv1[:, i, 0:1],
                                                    rs1[:, i:i + 1], ALU.subtract, ALU.mult))
                    p1.link(nc.vector.reciprocal(rcp[:, i % 2:i % 2 + 1], rowsum[:, i % 4:i % 4 + 1]))
                    dve.wait_ge(x1_out[i % 2], b * NB * 8 + (i // 2 + 1) * 16)
                    dve.wait_ge(pt_free, b * PTK + 2 + T_BEFORE[i + 1])
                    nc.vector.scalar_tensor_tensor(out=U[:, i % 2], in0=PS[:, 6 + i % 2],
                                                   scalar=rcp[:, i % 2:i % 2 + 1], in1=xin[:, i % 2],
                                                   op0=ALU.mult, op1=ALU.add).then_inc(z_free, 1)
                    dve.wait_ge(z_free, b * NB + 2 + i + 1)
                    statistics(p1, U[:, i % 2], mvE[:, i % 2], i)

                def end_b(i):
                    dve.wait_ge(rstd_ready, b * 2 * NB + NB + i + 1)
                    scale_shift(p1, U[:, i % 2], mvE[:, i % 2, 0:1], rsE[:, i % 2:i % 2 + 1],
                                ln1[:, 0], ln1[:, 1], x1_ready)

                for kind, i, c in ORDER:
                    if kind == "S":
                        scores(i, c)
                    elif kind == "Q":
                        lo_q(i, c)
                    elif kind == "T":
                        k, w = T_BEFORE[i] + c, width_of(i, c)
                        lo(TP0 + NB + k, PT[:, k % 2, 1, 0:w], PS[:, 2 + k % 2, 0:w],
                           PT[:, k % 2, 0, 0:w], b, TP1)
                    elif kind == "A":
                        end_a(i)
                    elif kind == "B":
                        end_b(i)
            assert p1.n == DVE1

            R2 = 2 * NB * B
            def lo_t(k, dst, k_bank, turn=0, per=0):
                lo(k, dst[1], thirds(PS[:, 2 + k_bank % 2]), dst[0], turn, per)

            for b in range(B):
                lo_t(TP2 + b, [x1T[:, :, h, b * P:(b + 1) * P] for h in range(2)], b)
            dve.wait_ge(c_full, 1)
            for b in range(B):
                ins = nc.vector.tensor_scalar(xn[0:1, b, 0:SC], PS[0:1, 0, b * SCP:b * SCP + SC], 0.0, None,
                                              ALU.not_equal, ALU.add, accum_out=keys_seen2[0:1, b:b + 1])
                if b == 0:
                    p0.done(ins)
            ins.then_inc(c_free, 1)
            dve.wait_ge(c_free, 1)
            p0.wait()
            nc.vector.tensor_copy(sum2[0:1, 0:1], keys_seen2[0:1, 0:1]).then_inc(counted, 1)
            dve.wait_ge(c_full, 2)
            p0.link(nc.vector.tensor_copy(len2, PS[:, 1, 0:B]))
            for b in range(B):
                p0.done(nc.vector.tensor_scalar(mask2[:, b], keys[:, 0:SC], len2[:, b:b + 1], -BIG,
                                                ALU.is_ge, ALU.mult))
            p0.wait()
            p0.link(nc.vector.reciprocal(rc2[:, 0:B], len2))
            p0.link(nc.vector.tensor_scalar(rc2[:, 0:B], rc2[:, 0:B], 0.0, None, ALU.mult))
            p0.link(nc.vector.tensor_tensor(mask2[:], mask2[:],
                                            rc2[:, 0:B].unsqueeze(2).to_broadcast([P, B, SC]), ALU.add))
            nc.vector.tensor_copy(sum2[:, 0:1], len2[:, 0:1]).then_inc(len_seen, 1)
            dve.wait_ge(vec2_in, 16 * 5)

            def rows(slot):
                return S2[:, slot, :].rearrange("p (k n) -> p k n", k=BT)[:, :, 0:SC]

            def softmax(steps, t, slot):
                for k in range(BT):
                    lo_t(TP2 + TPL + k, [x1T[:, :, h, k * P:(k + 1) * P] for h in range(2)], k, t, TPT)
                s = rows(slot)
                dve.wait_ge(c_full, t + 3)
                bank = PS[:, 0, 0:BT * SCP].rearrange("p (k n) -> p k n", k=BT)[:, :, 0:SC]
                m = mask2[:, bass.ds(t // TPB, 1), :].to_broadcast([P, BT, SC])
                nc.vector.tensor_tensor(s, bank, m, ALU.add).then_inc(c_free, 1)
                dve.wait_ge(c_free, t + 2)
                steps.link(nc.vector.tensor_reduce(mx2, s, AX.X, ALU.max))
                nc.vector.tensor_tensor(s, s, mx2.unsqueeze(2).to_broadcast([P, BT, SC]),
                                        ALU.subtract).then_inc(sm_ready, 1)

            def cross_end(steps, t, slot):
                dve.wait_ge(e_ready, t + 1)
                steps.link(nc.vector.tensor_reduce(sum2, rows(slot), AX.X, ALU.add))
                steps.link(nc.vector.reciprocal(rc2, sum2))
                lo(TP2 + TPL + BT + 1, PT2[0:SC, 0, 1, :], PS[0:SC, 2], PT2[0:SC, 0, 0, :], t, TPT, inc=2)

                def norm(k):
                    dve.wait_ge(rstd_ready, t * 2 * BT + R2 + k + 1)
                    scale_shift(steps, N[:, slot, k], mvE[:, k, 0:1], rsE[:, k:k + 1],
                                vec2[:, 0], vec2[:, 1], x2_ready)

                for k in range(BT):
                    x = N[:, slot, k]
                    dve.wait_ge(z2_full, t * BT + k + 1)
                    nc.vector.scalar_tensor_tensor(out=x, in0=PS[:, 6 + k % 2], scalar=rc2[:, k:k + 1], in1=x,
                                                   op0=ALU.mult, op1=ALU.add).then_inc(z_free, 1)
                    dve.wait_ge(z_free, t * BT + 2 + B * NB + k + 1)
                    statistics(steps, x, mvE[:, k], k)
                    if k:
                        norm(k - 1)
                norm(BT - 1)
                for k in range(BT):
                    lo_t(TP2 + TPL + BT + 2 + k, [x2T[:, :, h, k * P:(k + 1) * P] for h in range(2)], k, t, TPT)

            for n, w in enumerate((fc1, fc2)):
                for c in range(C):
                    dve.wait_ge(fcw_hi, n * C + c + 1)
                    nc.vector.tensor_tensor(w[:, c, 1, :], stage[:, n, c], w[:, c, 0, :].bitcast(F32),
                                            ALU.subtract).then_inc(fcw_lo, 1)
            softmax(p0, 0, 0)
            cross_end(p0, 0, 0)

            def tile2(t, slot, last):
                p2 = Steps(dve, dve_p2, DVE2, t)
                for f in range(C):
                    dve.wait_ge(h_hi, t * C + f + 1)
                    nc.vector.tensor_tensor(hid2[:, f, 1, :], HF2[:, f % 2], hid2[:, f, 0, :].bitcast(F32),
                                            ALU.subtract).then_inc(h_lo, 1)
                if not last:
                    softmax(p2, t + 1, 1 - slot)

                def norm(k):
                    x = N[:, slot, k]
                    dve.wait_ge(rstd_ready, t * 2 * BT + R2 + BT + k + 1)
                    p2.link(nc.vector.scalar_tensor_tensor(out=x, in0=x, scalar=mvE[:, k, 0:1], in1=vec2[:, 2],
                                                           op0=ALU.subtract, op1=ALU.mult))
                    p2.link(nc.vector.scalar_tensor_tensor(out=x, in0=x, scalar=rsE[:, k:k + 1],
                                                           in1=vec2[:, 3], op0=ALU.mult, op1=ALU.add))
                    dve.wait_ge(xo_in, t * BT * 16 + (k + 1) * 16)
                    nc.vector.scalar_tensor_tensor(out=x, in0=x, scalar=gate_x, in1=xo[:, 0],
                                                   op0=ALU.mult, op1=ALU.add).then_inc(xg_ready, 1)

                for k in range(BT):
                    x = N[:, slot, k]
                    dve.wait_ge(y_full, t * BT + k + 1)
                    nc.vector.tensor_tensor(x, PS[:, 4 + k % 2], x, ALU.add).then_inc(y_free, 1)
                    dve.wait_ge(y_free, t * BT + 4 + k + 1)
                    p2.link(nc.vector.tensor_tensor(x, x, vec2[:, 4], ALU.add))
                    statistics(p2, x, mvE[:, k], k)
                    if k:
                        norm(k - 1)
                norm(BT - 1)
                if not last:
                    cross_end(p2, t + 1, 1 - slot)
                    assert p2.n == DVE2

            tiles(dve, tile2)
            nc.vector.tensor_copy(sum2[:, 0:1], len2[:, 0:1]).then_inc(p2_end, 1)

            R3 = R2 + NT * 2 * BT
            dve.wait_ge(vec3_in, 16 * 3)
            p0.link(nc.vector.tensor_scalar(vec3[:, 2], vec3[:, 2], gf_half, None, ALU.mult))

            def stats_x3(steps, t, slot):
                dve.wait_ge(b_in[slot], (t // 2) * 16 + 16)
                for k in range(BT):
                    steps.link(nc.vector.bn_stats(st[:, k % 2], base[:, slot, k]))
                    apart()
                    ins = nc.vector.bn_aggr(mvX[:, k], st[:, k % 2])
                    if k < BT - 1:
                        steps.done(ins)
                ins.then_inc(var_ready, 1)

            def make_h0(steps, t, slot, k):
                if k == 0:
                    dve.wait_ge(rstd_ready, t * (1 + BT) + R3 + 1)
                dve.wait_ge(tp_full, t * BT + TP3 + max(k - 1, 0))
                steps.link(nc.vector.tensor_scalar(H0[:, k % 2], base[:, slot, k], mvX[:, k, 0:1],
                                                   rs_x[:, k:k + 1], ALU.subtract, ALU.mult))
                statistics(steps, H0[:, k % 2], mvE[:, k], k)

            def norm_h(steps, t, slot, k):
                x = base[:, slot, k]
                steps.link(nc.vector.scalar_tensor_tensor(out=x, in0=H0[:, k % 2], scalar=gate_f, in1=x,
                                                          op0=ALU.mult, op1=ALU.add))
                steps.done(nc.vector.tensor_tensor(x, x, vec3[:, 2], ALU.add))
                dve.wait_ge(rstd_ready, t * (1 + BT) + R3 + 1 + k + 1)
                scale_shift(steps, H0[:, k % 2], mvE[:, k, 0:1], rsE[:, k:k + 1], vec3[:, 0], vec3[:, 1],
                            hn_ready)

            def lo_h(t, slot, k):
                lo_t(TP3 + k, [hT[:, slot * C:(slot + 1) * C, h, k * P:(k + 1) * P] for h in range(2)],
                     k, t, BT)

            stats_x3(p0, 0, 0)
            for k in range(BT):
                make_h0(p0, 0, 0, k)
                norm_h(p0, 0, 0, k)
                lo_h(0, 0, k)

            def tile3(t, slot, last):
                p3 = Steps(dve, dve_p3, DVE3, t)
                for f in range(NF):
                    dve.wait_ge(f_hi, t * NF + f + 1)
                    nc.vector.tensor_tensor(hid3[:, f % 2, 1, :], HF3[:, f % 2],
                                            hid3[:, f % 2, 0, :].bitcast(F32), ALU.subtract).then_inc(f_lo, 1)
                    if not last:
                        if f in TURN_AT:
                            lo_h(t + 1, 1 - slot, TURN_AT.index(f))
                        if f == TURN_AT[0] - 3:
                            stats_x3(p3, t + 1, 1 - slot)
                        if f + 2 in TURN_AT:
                            make_h0(p3, t + 1, 1 - slot, TURN_AT.index(f + 2))
                        if f + 1 in TURN_AT:
                            norm_h(p3, t + 1, 1 - slot, TURN_AT.index(f + 1))
                for k in range(BT):
                    x = base[:, slot, k]
                    if k < BT - 1:
                        dve.wait_ge(o_full, t * (BT - 1) + k + 1)
                    else:
                        dve.wait_ge(hid_free, t * NF + 2 + NF)
                    nc.vector.scalar_tensor_tensor(out=x, in0=PS[:, 4 + k], scalar=gf_half, in1=x,
                                                   op0=ALU.mult, op1=ALU.add).then_inc(o_free, 1)
                if not last:
                    assert p3.n == DVE3

            tiles(dve, tile3)


_INS = ["x", "ctx_1024", "g_xattn", "g_ffn", "L0_xattn_Wq1", "L0_xattn_Wk1", "L0_xattn_Wv1", "L0_xattn_Wq2",
        "L0_xattn_Wk2", "L0_xattn_Wv2", "L0_xattn_fc1_w", "L0_xattn_fc1_b", "L0_xattn_fc2_w", "L0_xattn_fc2_b",
        "L0_xattn_ln1_g", "L0_xattn_ln1_b", "L0_xattn_ln2_g", "L0_xattn_ln2_b", "L0_xattn_ln3_g",
        "L0_xattn_ln3_b", "L0_ffn_ln_gamma", "L0_ffn_ln_beta", "L0_ffn_fc1_q", "L0_ffn_fc1_scales",
        "L0_ffn_fc1_bias", "L0_ffn_fc2_q", "L0_ffn_fc2_scales", "L0_ffn_fc2_bias"]


def kernel(**inputs):
    import numpy as _np
    import concourse.bacc as _bacc
    from concourse import mybir as _mybir
    from concourse.bass_utils import run_bass_kernel_spmd as _run

    nc = _bacc.Bacc("TRN2", target_bir_lowering=False, num_devices=1)
    arrays, aps = {}, {}
    for name in _INS:
        v = _np.ascontiguousarray(inputs[name])
        arrays[f"in_{name}"] = v
        aps[name] = nc.dram_tensor(f"in_{name}", v.shape, _mybir.dt.from_np(v.dtype), kind="ExternalInput").ap()
    out = nc.dram_tensor("out_0", (B, S, E), F32, kind="ExternalOutput").ap()
    build(nc, aps, out)
    r = _run(nc, [arrays], core_ids=[0])
    return r.results[0]["out_0"]
```

```python
from contextlib import ExitStack

import concourse.bass as bass
from concourse import mybir

F32 = mybir.dt.float32
F32R = mybir.dt.float32r
BF16 = mybir.dt.bfloat16
I16 = mybir.dt.int16
I32 = mybir.dt.int32
ALU = mybir.AluOpType
ACT = mybir.ActivationFunctionType
AX = mybir.AxisListType

P = 128
B, S, E = 2, 2048, 512
C = E // P
NB = S // P
SC = 77
SCP = 80
TILE = 512
BT = TILE // P
NT = B * S // TILE
TPB = S // TILE
FF = 2048
NF = FF // P
EPS = 1e-5
SCALE = float(1.0 / (E // 16) ** 0.5)
BIG = 1e38
PASSES = ((0, 0), (0, 1), (1, 0))

KB = 256


class Steps:

    def __init__(self, eng, sem, per=0, turn=0):
        self.eng, self.sem, self.per, self.turn, self.n = eng, sem, per, turn, 0

    def done(self, ins):
        ins.then_inc(self.sem, 1)
        self.n += 1
        return self.n

    def wait(self, n=None):
        self.eng.wait_ge(self.sem, self.turn * self.per + (self.n if n is None else n))

    def link(self, ins):
        self.done(ins)
        self.wait()


def chunks_of(i):
    return i // 4 + 1


def width_of(i, c):
    return 512 if c < i // 4 else (i % 4 + 1) * P


T_BEFORE = [sum(chunks_of(j) for j in range(i)) for i in range(NB + 1)]


def attention_order():
    order = [("S", 0, 0)]
    for i in range(NB):
        n0 = chunks_of(i)
        n1 = chunks_of(i + 1) if i + 1 < NB else 0
        new_group = i % 4 == 3 and i + 1 < NB
        order.append(("T", i, 0))
        if i:
            order.append(("A", i - 1, 0))
        if new_group:
            order += [("Q", i // 4 + 1, m) for m in range(C)]
        if n1 and not new_group:
            order.append(("S", i + 1, 0))
        if i:
            order.append(("B", i - 1, 0))
        s = 0 if new_group else 1
        for c in range(1, n0):
            order.append(("T", i, c))
            if new_group:
                order.append(("V", i, c - 1))
            if s < n1:
                order.append(("S", i + 1, s))
                s += 1
            if not new_group:
                order.append(("V", i, c - 1))
        order.append(("V", i, n0 - 1))
        while s < n1:
            order.append(("S", i + 1, s))
            s += 1
    order += [("A", NB - 1, 0), ("B", NB - 1, 0)]
    return order


ORDER = attention_order()
TURN_AT = (7, 9, 11, 13)

TP0, MM0 = 16, 14
TP1 = NB + T_BEFORE[NB]
MM1 = 2 * NB
SS1 = 4 + 2 + T_BEFORE[NB]
TP2 = TP0 + B * TP1
TPL = 2
TPT = 2 * BT + 2
TP3 = TP2 + TPL + NT * TPT
MM2 = MM0 + B * MM1

DVE1, DVE2, DVE3 = 134, 19, 27
PTK = T_BEFORE[NB]


def build(nc, a, out):
    ctx = ExitStack()
    with ctx:
        def sb(name, shape, dt=F32):
            return ctx.enter_context(nc.sbuf_tensor(name, shape, dt))

        def sem(name):
            return ctx.enter_context(nc.semaphore(name))

        x1_dram = nc.dram_tensor("x1_scratch", (B * S, E), F32, kind="Internal").ap()
        xg_dram = nc.dram_tensor("xg_scratch", (B * S, E), F32, kind="Internal").ap()
        g_dram = nc.dram_tensor("g_scratch", (P, C * 2 * 2 * SCP), F32, kind="Internal").ap()
        v_dram = nc.dram_tensor("v_scratch", (SC, B * 2 * E), F32, kind="Internal").ap()
        x_dram = a["x"].rearrange("b s e -> (b s) e")
        out_dram = out.rearrange("b s e -> (b s) e")

        R = sb("split", [P, 160 * KB], F32R)
        F = sb("plain", [P, 37 * KB], F32)
        T0 = sb("split_0", [P, 4 * KB], F32R)
        with nc.sbuf_tensor("split_1", [P, 4 * KB], F32R) as T1:
            pass
        codes1 = sb("codes", [P, 2, E], F32)
        T = [t[:].rearrange("p (h n) -> p h n", h=2) for t in (T0, T1)]

        def pair(at, chunks, width):
            return R[:, at * KB:at * KB + chunks * 2 * width].rearrange(
                "p (c h n) -> p c h n", c=chunks, h=2)

        def plain(at, *dims):
            n = 1
            for d in dims:
                n *= d
            v = F[:, at:at + n]
            if len(dims) == 2:
                v = v.rearrange("p (a b) -> p a b", a=dims[0])
            if len(dims) == 3:
                v = v.rearrange("p (a b c) -> p a b c", a=dims[0], b=dims[1])
            return v

        wq1T, wk1T, wq2T = pair(0, C, E), pair(16, C, E), pair(32, C, E)
        wk2, wv2 = pair(48, C, E), pair(64, C, E)
        ctxT, kT2 = pair(80, C, 2 * SCP), pair(85, C, 2 * SCP)
        g_0, v_0 = pair(90, C, 2 * SCP), pair(95, B, E)
        stage = plain(0, 2, C, E)
        ctx_in = plain(6144, B, E)
        xT, V = pair(0, C, S), pair(64, NB, E)
        A, QT, PT = pair(128, C, E), pair(144, C, E), T
        wv = pair(144, C, E)
        Srow = plain(0, 2, S)
        xin, xn, U = plain(4096, 2, E), plain(5120, 2, E), plain(6144, 2, E)
        ln1 = plain(7168, 2, E)
        pad = plain(8192, S // 2).bitcast(BF16)
        x1T, x2T, hid2 = pair(0, C, E), pair(16, C, E), pair(32, C, E)
        G, V2 = pair(48, C, 2 * SCP), pair(53, B, E)
        PT2 = T[0]
        fc1, fc2 = pair(128, C, E), pair(144, C, E)
        N = plain(0, 2, BT, E)
        vec2 = plain(4096, 5, E)
        xo = [plain(6656, E), plain(8832, E)]
        HF2 = plain(7168, 2, E)
        S2 = plain(8192, 2, BT * SCP)
        xo_last = [xo[0], HF2[:, 1]]
        q1, sc1 = codes1[:, 0], codes1[:, 1]
        W2, W1 = pair(0, NF, E), pair(64, C, FF)
        hT = pair(128, 2 * C, TILE)
        hid3 = T
        base = plain(0, 2, BT, E)
        H0 = plain(4096, 2, E)
        q2, sc2 = plain(5120, 2, E), plain(6144, E)
        bias3 = plain(6656, E)
        HF3 = plain(7168, 2, E)
        vec3 = plain(8192, 2, E)

        ident = sb("ident", [P, P])
        tri = sb("tri", [P, P], BF16)
        keys = sb("keys", [P, 512], I16)
        small = sb("small", [P, 148])

        def col(at, n=1):
            return small[:, at:at + n]

        st = small[:, 0:12].rearrange("p (a b) -> p a b", a=2)
        mv1 = small[:, 12:44].rearrange("p (a b) -> p a b", a=NB)
        rs1 = col(44, NB)
        mvE = small[:, 60:68].rearrange("p (a b) -> p a b", a=4)
        rsE = col(68, 4)
        mx = small[:, 72:82].rearrange("p (a b) -> p a b", a=2)
        nmx, nb = col(82, 2), col(84, 2)
        rowsum, rcp = col(86, 4), col(90, 4)
        half, cnt, ln, lnc = col(94), col(95, 4), col(99), col(100, 4)
        gate_x, gate_f, gf_half = col(104), col(105), col(106)
        b1x, b1f = col(107, C), col(111, NF)
        mx2, sum2, rc2 = col(127, 4), col(131, 4), col(135, 4)
        len2 = col(139, 2)
        eps_col = col(141)
        keys_seen, keys_seen2 = col(142), col(143, 2)
        mvX, rs_x = small[:, 12:20].rearrange("p (a b) -> p a b", a=BT), col(44, BT)
        mvH, rsH = small[:, 20:28].rearrange("p (a b) -> p a b", a=BT), col(48, BT)
        mask2 = sb("mask2", [P, 2, SC], BF16)
        ones = plain(9344, P)[0:1]

        PS = ctx.enter_context(nc.psum_tensor("banks", [P, 8, 512], F32))

        stage_in = [sem("stage_in_0"), sem("stage_in_1")]
        ctx_loaded, const_in, parked, consts = sem("ctx_loaded"), sem("const_in"), sem("parked"), sem("consts")
        tp_full, tp_hi, tp_free = sem("tp_full"), sem("tp_hi"), sem("tp_free")
        mm_full, mm_hi, mm_free = sem("mm_full"), sem("mm_hi"), sem("mm_free")
        split_hi, split_lo = sem("split_hi"), sem("split_lo")
        dve_p0, dve_p1, dve_p2, dve_p3 = sem("dve_p0"), sem("dve_p1"), sem("dve_p2"), sem("dve_p3")
        x_in = [sem("x_in_0"), sem("x_in_1")]
        x_normed, var_ready, rstd_ready, eps_added = (
            sem("x_normed"), sem("var_ready"), sem("rstd_ready"), sem("eps_added"))
        wv_in, wv_hi, wv_lo = sem("wv_in"), sem("wv_hi"), sem("wv_lo")
        s_full, s_free, counted = sem("s_full"), sem("s_free"), sem("counted")
        waited = sem("waited")
        mx_ready, p_ready, pt_free, z_free = sem("mx_ready"), sem("p_ready"), sem("pt_free"), sem("z_free")
        x1_ready = sem("x1_ready")
        x1_out = [sem("x1_out_0"), sem("x1_out_1")]
        vec2_ready = sem("vec2_ready")
        vec2_in, cross_in, fcw_in = sem("vec2_in"), sem("cross_in"), sem("fcw_in")
        fcw_hi, fcw_lo = sem("fcw_hi"), sem("fcw_lo")
        len_in, len_seen = sem("len_in"), sem("len_seen")
        n_in = [sem("n_in_0"), sem("n_in_1")]
        c_full, c_free, sm_ready, e_ready = sem("c_full"), sem("c_free"), sem("sm_ready"), sem("e_ready")
        z2_full, x2_ready = sem("z2_full"), sem("x2_ready")
        h_full, hf_ready, h_hi, h_lo = sem("h_full"), sem("hf_ready"), sem("h_hi"), sem("h_lo")
        y_full, y_free = sem("y_full"), sem("y_free")
        x2_biased, xo_ready, xg_ready = sem("x2_biased"), sem("xo_ready"), sem("xg_ready")
        xo_in = [sem("xo_in_0"), sem("xo_in_1")]
        xg_out = [sem("xg_out_0"), sem("xg_out_1")]
        q1_in, sc2_in = sem("q1_in"), sem("sc2_in")
        q2_in = [sem("q2_in_0"), sem("q2_in_1")]
        codes_scaled, w_hi, w_ready = sem("codes_scaled"), sem("w_hi"), sem("w_ready")
        made = sem("made")
        p2_end, vec3_in, bias3_in, bias3_ready = sem("p2_end"), sem("vec3_in"), sem("bias3_in"), sem("bias3_ready")
        b_in = [sem("b_in_0"), sem("b_in_1")]
        hn_ready = sem("hn_ready")
        f_full, hf3_ready, f_hi, f_lo, hid_free = (
            sem("f_full"), sem("hf3_ready"), sem("f_hi"), sem("f_lo"), sem("hid_free"))
        o_full, o_free, base_biased = sem("o_full"), sem("o_free"), sem("base_biased")
        o_out = [sem("o_out_0"), sem("o_out_1")]

        block = ctx.enter_context(nc.Block())

        def bcast(v):
            return v.rearrange("(a e) -> a e", a=1).to_broadcast([P, v.shape[0]])

        def blocks(dram, t):
            return dram[bass.ds(t * TILE, TILE), :].rearrange("(k p) e -> p k e", p=P)

        def tiles(eng, body):
            with eng.Fori(0, NT // 2 - 1) as u:
                for slot in range(2):
                    body(u * 2 + slot, slot, False)
            body(NT - 2, 0, False)
            body(NT - 1, 1, True)

        def tiles3(eng, body):
            body(0, 0, True, False)
            with eng.Fori(0, NT // 2 - 1) as u:
                body(u * 2 + 1, 1, False, False)
                body(u * 2 + 2, 0, False, False)
            body(NT - 1, 1, False, True)

        def w1_unit(u, n):
            return [W1[:, n, h, bass.ds(u * E, E)] for h in range(2)]

        def w2_unit(f):
            return [W2[:, f, h, :] for h in range(2)]

        @block.sync
        def _(sp):
            sp.sem_inc(x1_out[0], 16)
            sp.sem_inc(x1_out[1], 16)

            def weight(name, slot, done):
                sp.dma_start(stage[:, slot], a[name].rearrange("(c p) n -> p c n", p=P)).then_inc(done, 16)

            weight("L0_xattn_Wq1", 0, stage_in[0])
            weight("L0_xattn_Wk1", 1, stage_in[1])
            sp.dma_start(ctx_in[0:SC], a["ctx_1024"].rearrange("b s e -> s b e")).then_inc(ctx_loaded, 16)
            sp.dma_start(ln1[:, 0], bcast(a["L0_xattn_ln1_g"])).then_inc(const_in, 16)
            sp.dma_start(ln1[:, 1], bcast(a["L0_xattn_ln1_b"])).then_inc(const_in, 16)
            sp.dma_start(gate_x, bcast(a["g_xattn"])).then_inc(const_in, 16)
            sp.dma_start(gate_f, bcast(a["g_ffn"])).then_inc(const_in, 16)
            sp.dma_start(b1x, a["L0_xattn_fc1_b"].rearrange("(c p) -> p c", p=P),
                         allow_slow_non_contiguous=True).then_inc(const_in, 16)
            sp.dma_start(b1f, a["L0_ffn_fc1_bias"].rearrange("(c p) -> p c", p=P),
                         allow_slow_non_contiguous=True).then_inc(const_in, 16)
            sp.wait_ge(tp_full, C)
            weight("L0_xattn_Wq2", 0, stage_in[0])
            sp.wait_ge(tp_full, 2 * C)
            weight("L0_xattn_Wk2", 1, stage_in[1])
            sp.wait_ge(tp_full, 3 * C)
            weight("L0_xattn_Wv2", 0, stage_in[0])
            sp.wait_ge(mm_free, 2 + MM0)
            sp.dma_start(g_dram, g_0.rearrange("p c h n -> p (c h n)").bitcast(F32)).then_inc(parked, 16)
            sp.dma_start(v_dram, v_0[0:SC].rearrange("p c h n -> p (c h n)").bitcast(F32)).then_inc(parked, 16)
            sp.wait_ge(parked, 32)

            with sp.Fori(0, B) as b:
                sp.wait_ge(pt_free, 2 + b * PTK)
                weight("L0_xattn_Wv1", 0, wv_in)

                def load_x(k, blk):
                    if k < 2:
                        sp.wait_ge(z_free, b * NB + k + 1)
                    elif k < NB + 2:
                        sp.wait_ge(x_normed, b * NB + k - 1)
                    else:
                        sp.wait_ge(z_free, b * NB + k - NB + 1)
                    sp.dma_start(xin[:, k % 2], x_dram[bass.ds(b * S + blk * P, P), :]).then_inc(
                        x_in[k % 2], 16)

                for t in range(NB):
                    load_x(t, t)
                load_x(NB, 0)
                load_x(NB + 1, 1)
                for i in range(NB):
                    sp.wait_ge(x1_ready, b * NB + i + 1)
                    sp.dma_start(x1_dram[bass.ds(b * S + i * P, P), :], U[:, i % 2]).then_inc(
                        x1_out[i % 2], 16)
                    if i + 2 < NB:
                        load_x(NB + i + 2, i + 2)

            for p in range(2):
                sp.wait_ge(x1_out[p], 16 + 16 * B * NB // 2)
            sp.dma_start(G.rearrange("p c h n -> p (c h n)").bitcast(F32), g_dram).then_inc(cross_in, 16)
            sp.dma_start(V2[0:SC].rearrange("p c h n -> p (c h n)").bitcast(F32), v_dram).then_inc(
                cross_in, 16)
            sp.dma_start(xin[:, 0], x1_dram[0:P, :]).then_inc(len_in, 16)
            sp.dma_start(xin[:, 1], x1_dram[S:S + P, :]).then_inc(len_in, 16)
            weight("L0_xattn_fc1_w", 0, fcw_in)
            weight("L0_xattn_fc2_w", 1, fcw_in)
            sp.wait_ge(len_seen, 1)
            for n, v in enumerate(("ln2_g", "ln2_b", "ln3_g", "ln3_b", "fc2_b")):
                sp.dma_start(vec2[:, n], bcast(a[f"L0_xattn_{v}"])).then_inc(vec2_in, 16)
            sp.wait_ge(fcw_lo, 2 * C)

            for slot in range(2):
                sp.dma_start(N[:, slot], blocks(x1_dram, slot)).then_inc(n_in[slot], 16)

            def load_w1(u, n):
                cols = bass.ds(u * E, E)
                sp.dma_start(q1.bitcast(I32), a["L0_ffn_fc1_q"][n * P:(n + 1) * P, cols]).then_inc(q1_in, 16)
                sp.dma_start(sc1, a["L0_ffn_fc1_scales"][n:n + 1, cols].to_broadcast([P, E])).then_inc(q1_in, 16)

            def load_w2(f):
                q, sc, q_in, sc_in = (q1, sc1, q1_in, q1_in) if f < 2 else (q2[:, f % 2], sc2, q2_in[f % 2], sc2_in)
                sp.dma_start(q.bitcast(I32), a["L0_ffn_fc2_q"][f * P:(f + 1) * P, :]).then_inc(q_in, 16)
                sp.dma_start(sc, a["L0_ffn_fc2_scales"][f:f + 1, :].to_broadcast([P, E])).then_inc(sc_in, 16)

            def load_xo(t, k, last):
                if k < 2:
                    sp.wait_ge(xg_ready, t * BT + k + 1)
                else:
                    sp.wait_ge(xg_ready, t * BT + 2 + k - 1)
                if last and k == 1:
                    sp.wait_ge(h_lo, NT * C + 2)
                sp.dma_start((xo_last if last else xo)[k % 2], x_dram[bass.ds(t * TILE + k * P, P), :]).then_inc(
                    xo_in[k % 2], 16)

            def store_xg(t, slot, k):
                sp.wait_ge(xg_ready, t * BT + 2 + k + 1)
                sp.dma_start(xg_dram[bass.ds(t * TILE + k * P, P), :], N[:, slot, k]).then_inc(xg_out[slot], 16)

            def tile2(t, u, slot, last):
                sp.wait_ge(w_ready, t * 2 + 1)
                load_w1(u, slot * 2 + 1)
                load_xo(t, 0, last)
                load_xo(t, 1, last)
                sp.wait_ge(w_ready, t * 2 + 2)
                if last:
                    load_w2(0)
                elif slot:
                    load_w1(u + 1, 0)
                else:
                    load_w1(u, 2)
                if last:
                    sp.wait_ge(xg_out[0], NT // 2 * 16 * BT)
                    sp.dma_start(base[:, 0], blocks(xg_dram, 0)).then_inc(b_in[0], 16)
                    sp.wait_ge(x2_ready, NT * BT)
                    for n, v in enumerate(("ln_gamma", "ln_beta")):
                        sp.dma_start(vec3[:, n], bcast(a[f"L0_ffn_{v}"])).then_inc(vec3_in, 16)
                    sp.wait_ge(w_ready, NT * 2 + 1)
                    load_w2(1)
                for k in range(BT):
                    store_xg(t, slot, k)
                    if k + 2 < BT:
                        load_xo(t, k + 2, last)

            load_w1(0, 0)
            with sp.Fori(0, NT // 2 - 1) as u:
                for slot in range(2):
                    tile2(u * 2 + slot, u, slot, False)
                    sp.wait_ge(xg_out[slot], u * 16 * BT + 16 * BT)
                    sp.dma_start(N[:, slot], blocks(x1_dram, u * 2 + slot + 2)).then_inc(n_in[slot], 16)
            for slot in range(2):
                tile2(NT - 2 + slot, NT // 2 - 1, slot, slot == 1)

            sp.wait_ge(p2_end, 1)
            sp.dma_start(bias3, bcast(a["L0_ffn_fc2_bias"])).then_inc(bias3_in, 16)
            load_w2(2)
            sp.wait_ge(xg_out[1], NT // 2 * 16 * BT)
            sp.dma_start(base[:, 1], blocks(xg_dram, 1)).then_inc(b_in[1], 16)
            for f in range(3, NF):
                sp.wait_ge(codes_scaled, NT * 2 + f)
                if f > 3:
                    sp.wait_ge(w_ready, NT * 2 + f - 1)
                load_w2(f)

            def store_out(t, slot):
                for k in range(BT):
                    sp.wait_ge(o_free, t * BT + BT + k + 1)
                    sp.dma_start(out_dram[bass.ds(t * TILE + k * P, P), :], base[:, slot, k]).then_inc(
                        o_out[slot], 16)

            with sp.Fori(0, NT // 2 - 1) as u:
                for slot in range(2):
                    store_out(u * 2 + slot, slot)
                    sp.wait_ge(o_out[slot], u * 16 * BT + 16 * BT)
                    sp.dma_start(base[:, slot], blocks(xg_dram, u * 2 + slot + 2)).then_inc(b_in[slot], 16)
            for slot in range(2):
                store_out(NT - 2 + slot, slot)
            for slot in range(2):
                sp.wait_ge(o_out[slot], NT // 2 * 16 * BT)

        @block.tensor
        def _(pe):
            pe.sem_inc(pt_free, 2)
            pe.sem_inc(hid_free, 2)
            pe.wait_ge(consts, 3)

            def product(out, left, right, chunks, done=None, start=True, stop=True):
                for c in range(chunks):
                    for l, r in PASSES:
                        mm = nc.tensor.matmul(out, left(c, l), right(c, r),
                                              start=start and c == 0 and (l, r) == PASSES[0],
                                              stop=stop and c == chunks - 1 and (l, r) == PASSES[-1])
                if done is not None:
                    mm.then_inc(done, 1)
                return mm

            def turn(bank, block_of, inc=1):
                for c in range(C):
                    mm = nc.tensor.transpose(bank[:, c * P:(c + 1) * P], block_of(c), ident[:])
                mm.then_inc(tp_full, inc)

            def turn_weight(k0, slot):
                for j in range(C):
                    pe.wait_ge(tp_free, k0 + j + 1)
                    turn(PS[:, 2 + j % 2], lambda e: stage[:, slot, e, j * P:(j + 1) * P])

            pe.wait_ge(stage_in[0], 16)
            turn_weight(0, 0)
            pe.wait_ge(stage_in[1], 16)
            turn_weight(C, 1)
            pe.wait_ge(stage_in[0], 32)
            turn_weight(2 * C, 0)
            pe.wait_ge(ctx_loaded, 16)
            for c in range(C):
                pe.wait_ge(tp_free, 3 * C + c + 1)
                for b in range(B):
                    mm = nc.tensor.transpose(PS[:, 2 + c % 2, b * SCP:b * SCP + SC],
                                             ctx_in[0:SC, b, c * P:(c + 1) * P], ident[0:SC, 0:SC])
                mm.then_inc(tp_full, 1)

            k = 0
            for m in range(C):
                pe.wait_ge(tp_free, 2 + 2 * C)
                pe.wait_ge(mm_free, k + 1)
                product(PS[:, 4 + k % 2], lambda j, h: wq1T[:, j, h, m * P:(m + 1) * P],
                        lambda j, h: wk1T[:, j, h, :], C, mm_full)
                k += 1
            pe.wait_ge(tp_free, 2 + TP0)
            for m in range(C):
                pe.wait_ge(split_lo, C)
                pe.wait_ge(mm_free, k + 1)
                product(PS[:, 4 + k % 2, 0:2 * SCP], lambda c, h: wk2[:, c, h, m * P:(m + 1) * P],
                        lambda c, h: ctxT[:, c, h, :], C, mm_full)
                k += 1
            for b in range(B):
                pe.wait_ge(split_lo, 2 * C)
                pe.wait_ge(mm_free, k + 1)
                product(PS[0:SC, 4 + k % 2], lambda c, h: ctxT[:, c, h, b * SCP:b * SCP + SC],
                        lambda c, h: wv2[:, c, h, :], C, mm_full)
                k += 1
            for m in range(C):
                pe.wait_ge(mm_free, max(2 + 2 * C, k + 1))
                product(PS[:, 4 + k % 2, 0:2 * SCP], lambda j, h: wq2T[:, j, h, m * P:(m + 1) * P],
                        lambda j, h: kT2[:, j, h, :], C, mm_full)
                k += 1

            with pe.Fori(0, B) as b:
                def turn_x(t):
                    pe.wait_ge(x_normed, b * NB + t + 1)
                    pe.wait_ge(tp_free, b * TP1 + TP0 + t + 1)
                    turn(PS[:, 2 + t % 2], lambda c: xn[:, t % 2, c * P:(c + 1) * P])

                def values(t):
                    if t == 0:
                        pe.wait_ge(wv_lo, b * C + C)
                    pe.wait_ge(tp_free, b * TP1 + 2 + TP0 + t + 1)
                    pe.wait_ge(mm_free, b * MM1 + MM0 + t + 1)
                    product(PS[:, 4 + t % 2], lambda c, h: xT[:, c, h, t * P:(t + 1) * P],
                            lambda c, h: wv[:, c, h, :], C, mm_full)

                def queries(g, m):
                    pe.wait_ge(mm_free, b * MM1 + MM0 + NB + g * C + m + 1)
                    product(PS[:, 4 + m % 2], lambda c, h: A[:, c, h, m * P:(m + 1) * P],
                            lambda c, h: xT[:, c, h, g * 512:(g + 1) * 512], C, mm_full)

                def score(k, q, lo, w):
                    pe.wait_ge(s_free, b * SS1 + k + 1)
                    product(PS[:, k % 2, 0:w], lambda m, h: QT[:, m, h, q * P:(q + 1) * P],
                            lambda m, h: xT[:, m, h, lo:lo + w], C, s_full)

                turn_x(0)
                for t in range(1, NB):
                    turn_x(t)
                    values(t - 1)
                values(NB - 1)
                for m in range(C):
                    queries(0, m)
                pe.wait_ge(mm_free, b * MM1 + 2 + MM0 + NB + C)
                for c in range(4):
                    score(c, 0, c * 512, 512)
                pe.wait_ge(s_free, b * SS1 + 5)
                pe.wait_ge(counted, b + 1)
                nc.tensor.matmul(PS[:, 0, 0:1], ones, keys_seen[0:1], start=True, stop=True).then_inc(
                    s_full, 2)

                for kind, i, c in ORDER:
                    if kind == "S":
                        if i % 4 == 0 and c == 0 and i:
                            pe.wait_ge(mm_free, b * MM1 + 2 + MM0 + NB + C * (i // 4 + 1))
                        score(6 + T_BEFORE[i] + c, i % 4, c * 512, width_of(i, c))
                    elif kind == "Q":
                        queries(i, c)
                    elif kind == "T":
                        k = NB + T_BEFORE[i] + c
                        if c == 0:
                            pe.wait_ge(p_ready, b * NB + i + 1)
                        pe.wait_ge(tp_free, b * TP1 + TP0 + k + 1)
                        for j in range(width_of(i, c) // P):
                            lo = c * 512 + j * P
                            mm = nc.tensor.transpose(PS[:, 2 + k % 2, j * P:(j + 1) * P],
                                                     Srow[:, i % 2, lo:lo + P], ident[:])
                        mm.then_inc(tp_full, 1)
                    elif kind == "V":
                        k = T_BEFORE[i] + c
                        if c == 0:
                            pe.wait_ge(z_free, b * NB + i + 1)
                        pe.wait_ge(tp_free, b * TP1 + 2 + TP0 + NB + k + 1)
                        n = width_of(i, c) // P
                        product(PS[:, 6 + i % 2], lambda j, h: PT[k % 2][:, h, j * P:(j + 1) * P],
                                lambda j, h: V[:, c * 4 + j, h, :], n, pt_free,
                                start=c == 0, stop=c == i // 4)

            pe.wait_ge(s_free, 2 + B * SS1)
            pe.wait_ge(mm_free, 2 + MM2)
            pe.wait_ge(z_free, 2 + B * NB)
            pe.wait_ge(cross_in, 32)
            pe.wait_ge(len_in, 32)
            for b in range(B):
                pe.wait_ge(tp_free, TP2 + b + 1)
                turn(PS[:, 2 + b % 2], lambda c: xin[:, b, c * P:(c + 1) * P])
            pe.wait_ge(tp_free, 2 + TP2 + B)
            for b in range(B):
                mm = product(PS[:, 0, b * SCP:(b + 1) * SCP], lambda c, h: x1T[:, c, h, b * P:(b + 1) * P],
                             lambda c, h: G[:, c, h, b * SCP:(b + 1) * SCP], C)
            mm.then_inc(c_full, 1)
            pe.wait_ge(counted, B + 1)
            nc.tensor.matmul(PS[:, 1, 0:B], ones, keys_seen2[0:1], start=True, stop=True).then_inc(c_full, 1)

            def cross_scores(t, slot, first=False):
                if first:
                    pe.wait_ge(n_in[slot], 16)
                else:
                    pe.wait_ge(n_in[slot], (t // 2) * 16 + 16)
                for k in range(BT):
                    pe.wait_ge(tp_free, t * TPT + TP2 + TPL + k + 1)
                    turn(PS[:, 2 + k % 2], lambda c: N[:, slot, k, c * P:(c + 1) * P])
                pe.wait_ge(c_free, t + 1)
                for k in range(BT):
                    pe.wait_ge(tp_free, t * TPT + 2 + TP2 + TPL + k + 1)
                    mm = product(PS[:, 0, k * SCP:(k + 1) * SCP],
                                 lambda c, h: x1T[:, c, h, k * P:(k + 1) * P],
                                 lambda c, h: G[:, c, h, bass.ds((t // TPB) * SCP, SCP)], C)
                mm.then_inc(c_full, 1)

            def cross_values(t, slot):
                pe.wait_ge(e_ready, t + 1)
                pe.wait_ge(tp_free, t * TPT + TP2 + TPL + BT + 1)
                for k in range(BT):
                    mm = nc.tensor.transpose(PS[0:SC, 2, k * P:(k + 1) * P],
                                             S2[:, slot, k * SCP:k * SCP + SC], ident[:])
                mm.then_inc(tp_full, 2)
                pe.wait_ge(tp_free, t * TPT + 2 + TP2 + TPL + BT + 2)
                for k in range(BT):
                    pe.wait_ge(z_free, t * BT + B * NB + k + 1)
                    product(PS[:, 6 + k % 2], lambda _, h: PT2[0:SC, h, k * P:(k + 1) * P],
                            lambda _, h: V2[0:SC, bass.ds(t // TPB, 1), h, :].rearrange("p a n -> p (a n)"),
                            1, z2_full)

            def turn_x2(t, slot):
                for k in range(BT):
                    pe.wait_ge(x2_ready, t * BT + k + 1)
                    pe.wait_ge(tp_free, t * TPT + TP2 + TPL + BT + 2 + k + 1)
                    turn(PS[:, 2 + k % 2], lambda c: N[:, slot, k, c * P:(c + 1) * P])

            def mlp_in(t):
                pe.wait_ge(tp_free, t * TPT + 2 + TP2 + TPL + TPT)
                for f in range(C):
                    if f < 2:
                        pe.wait_ge(y_free, t * BT + f + 3)
                    else:
                        pe.wait_ge(hf_ready, t * C + f - 1)
                    product(PS[:, 4 + f % 2], lambda c, h: fc1[:, c, h, f * P:(f + 1) * P],
                            lambda c, h: x2T[:, c, h, :], C, h_full)

            def mlp_out(t, k):
                if k == 0:
                    pe.wait_ge(h_lo, t * C + 2 + C)
                if k > 1:
                    pe.wait_ge(y_free, t * BT + 4 + k - 1)
                product(PS[:, 4 + k % 2], lambda f, h: hid2[:, f, h, k * P:(k + 1) * P],
                        lambda f, h: fc2[:, f, h, :], C, y_full)

            def turn_h(t, slot, k):
                pe.wait_ge(hn_ready, t * BT + k + 1)
                pe.wait_ge(tp_free, t * BT + TP3 + k + 1)
                turn(PS[:, 2 + k % 2], lambda c: H0[:, k % 2, c * P:(c + 1) * P])

            cross_scores(0, 0, True)
            cross_values(0, 0)
            turn_x2(0, 0)
            pe.wait_ge(fcw_lo, 2 * C)

            def tile2(t, slot, last):
                mlp_in(t)
                if not last:
                    cross_scores(t + 1, 1 - slot)
                for k in range(BT):
                    mlp_out(t, k)
                    if last and k:
                        turn_h(0, 0, k - 1)
                if not last:
                    cross_values(t + 1, 1 - slot)
                    turn_x2(t + 1, 1 - slot)

            tiles(pe, tile2)

            def ffn_in(t, slot, f):
                if f == 0:
                    pe.wait_ge(tp_free, t * BT + 2 + TP3 + BT)
                pe.wait_ge(hf3_ready, t * NF + f + 1)
                product(PS[:, f % 2], lambda c, h: W1[:, c, h, f * P:(f + 1) * P],
                        lambda c, h: hT[:, slot * C + c, h, :], C, f_full)

            def ffn_out(t, f):
                pe.wait_ge(f_lo, t * NF + 2 + f + 1)
                pe.wait_ge(w_ready, NT * 2 + f + 1)
                for k in range(BT):
                    if f == 0:
                        pe.wait_ge(o_free, t * BT + k + 1)
                    mm = product(PS[:, 4 + k], lambda _, h: hid3[f % 2][:, h, k * P:(k + 1) * P],
                                 lambda _, h: W2[:, f, h, :], 1,
                                 o_full if f == NF - 1 and k < BT - 1 else None,
                                 start=f == 0, stop=f == NF - 1)
                mm.then_inc(hid_free, 1)

            turn_h(0, 0, BT - 1)
            pe.wait_ge(w_ready, NT * 2)
            ffn_in(0, 0, 0)

            def tile3(t, slot, first, last):
                for f in range(NF):
                    if f + 1 < NF:
                        ffn_in(t, slot, f + 1)
                    elif not last:
                        ffn_in(t + 1, 1 - slot, 0)
                    if first and f == 0:
                        pe.wait_ge(y_free, NT * BT + 4)
                    ffn_out(t, f)
                    if f in TURN_AT and not last:
                        turn_h(t + 1, 1 - slot, TURN_AT.index(f))

            tiles3(pe, tile3)

        @block.scalar
        def _(act):
            nc.scalar.preload_act_table(ACT.Exp)
            copy = ACT.Copy

            def hi(k, dst, src, turn=0, per=0, sems=(tp_full, tp_hi), inc=1):
                act.wait_ge(sems[0], turn * per + k + 1)
                nc.scalar.activation(dst, src, copy).then_inc(sems[1], inc)

            def thirds(bank):
                return bank.rearrange("p (c n) -> p c n", c=C)

            for k in range(3 * C):
                w = (wq1T, wk1T, wq2T)[k // C]
                hi(k, w[:, k % C, 0, :], PS[:, 2 + k % 2])
            for c in range(C):
                hi(3 * C + c, ctxT[:, c, 0, :].rearrange("p (b n) -> p b n", b=B)[:, :, 0:SC],
                   PS[:, 2 + c % 2, 0:2 * SCP].rearrange("p (b n) -> p b n", b=B)[:, :, 0:SC])

            def split_stage(slot, loaded, w, done):
                act.wait_ge(loaded[0], loaded[1])
                for c in range(C):
                    nc.scalar.activation(w[:, c, 0, :], stage[:, slot, c], copy).then_inc(done, 1)

            split_stage(1, (stage_in[1], 32), wk2, split_hi)
            for m in range(C):
                hi(m, A[:, m, 0, :], PS[:, 4 + m % 2], sems=(mm_full, mm_hi))
            split_stage(0, (stage_in[0], 48), wv2, split_hi)
            for m in range(C):
                hi(C + m, kT2[:, m, 0, :], PS[:, 4 + m % 2, 0:2 * SCP], sems=(mm_full, mm_hi))
            for b in range(B):
                hi(2 * C + b, v_0[0:SC, b, 0, :], PS[0:SC, 4 + b % 2], sems=(mm_full, mm_hi))
            for m in range(C):
                hi(2 * C + B + m, g_0[:, m, 0, :], PS[:, 4 + m % 2, 0:2 * SCP], sems=(mm_full, mm_hi))
            act.wait_ge(const_in, 16 * 6)
            nc.scalar.activation(gate_x, gate_x, ACT.Tanh).then_inc(split_hi, 1)
            nc.scalar.activation(gate_f, gate_f, ACT.Tanh).then_inc(split_hi, 1)

            with act.Fori(0, B) as b:
                def hi_x(t):
                    hi(TP0 + t, xT[:, :, 0, t * P:(t + 1) * P], thirds(PS[:, 2 + t % 2]), b, TP1)

                def hi_v(t):
                    hi(MM0 + t, V[:, t, 0, :], PS[:, 4 + t % 2], b, MM1, (mm_full, mm_hi))

                def hi_q(g, m):
                    hi(MM0 + NB + g * C + m, QT[:, m, 0, :], PS[:, 4 + m % 2], b, MM1, (mm_full, mm_hi))

                hi_x(0)
                act.wait_ge(wv_in, b * 16 + 16)
                for c in range(C):
                    nc.scalar.activation(wv[:, c, 0, :], stage[:, 0, c], copy).then_inc(wv_hi, 1)
                for t in range(1, NB):
                    hi_x(t)
                    hi_v(t - 1)
                hi_v(NB - 1)
                for m in range(C):
                    hi_q(0, m)
                for kind, i, c in ORDER:
                    if kind == "S" and c == i // 4:
                        w = i // 4 * 512 + width_of(i, i // 4)
                        act.wait_ge(mx_ready, b * NB + i + 1)
                        nc.scalar.activation(Srow[:, i % 2, 0:w], Srow[:, i % 2, 0:w], ACT.Exp,
                                             bias=nb[:, i % 2:i % 2 + 1], scale=SCALE,
                                             accum_out=rowsum[:, i % 4:i % 4 + 1]).then_inc(p_ready, 1)
                    elif kind == "Q":
                        hi_q(i, c)
                    elif kind == "T":
                        k, w = T_BEFORE[i] + c, width_of(i, c)
                        act.wait_ge(pt_free, b * PTK + k + 1)
                        hi(TP0 + NB + k, PT[k % 2][:, 0, 0:w], PS[:, 2 + k % 2, 0:w], b, TP1)

            for b in range(B):
                hi(TP2 + b, x1T[:, :, 0, b * P:(b + 1) * P], thirds(PS[:, 2 + b % 2]))

            def hi_x1(t):
                for k in range(BT):
                    hi(TP2 + TPL + k, x1T[:, :, 0, k * P:(k + 1) * P], thirds(PS[:, 2 + k % 2]), t, TPT)

            def probs(t, slot):
                act.wait_ge(sm_ready, t + 1)
                s = S2[:, slot, :].rearrange("p (k n) -> p k n", k=BT)[:, :, 0:SC]
                nc.scalar.activation(s, s, ACT.Exp, scale=SCALE).then_inc(e_ready, 1)

            def hi_p(t):
                hi(TP2 + TPL + BT + 1, PT2[0:SC, 0, :], PS[0:SC, 2], t, TPT, inc=2)

            def hi_x2(t):
                for k in range(BT):
                    hi(TP2 + TPL + BT + 2 + k, x2T[:, :, 0, k * P:(k + 1) * P],
                       thirds(PS[:, 2 + k % 2]), t, TPT)

            act.wait_ge(fcw_in, 32)
            for slot, w in ((0, fc1), (1, fc2)):
                for c in range(C):
                    nc.scalar.activation(w[:, c, 0, :], stage[:, slot, c], copy).then_inc(fcw_hi, 1)
            hi_x1(0)
            probs(0, 0)
            hi_p(0)
            hi_x2(0)

            def hi_w(n, src, dst):
                act.wait_ge(codes_scaled, n + 1)
                nc.scalar.activation(dst[0], src, copy).then_inc(w_hi, 1)

            def hi_h(t, slot, k):
                hi(TP3 + k, hT[:, slot * C:(slot + 1) * C, 0, k * P:(k + 1) * P],
                   thirds(PS[:, 2 + k % 2]), t, BT)

            def tile2(t, u, slot, last):
                for f in range(C):
                    act.wait_ge(h_full, t * C + f + 1)
                    act.wait_ge(h_lo, t * C + f + 1)
                    nc.scalar.activation(HF2[:, f % 2], PS[:, 4 + f % 2], ACT.Relu,
                                         bias=b1x[:, f:f + 1]).then_inc(hf_ready, 1)
                    act.wait_ge(hf_ready, t * C + f + 1)
                    nc.scalar.activation(hid2[:, f, 0, :], HF2[:, f % 2], copy).then_inc(h_hi, 1)
                    if f == 0:
                        hi_w(t * 2, q1, w1_unit(u, slot * 2))
                if not last:
                    hi_x1(t + 1)
                    probs(t + 1, 1 - slot)
                    hi_w(t * 2 + 1, q1, w1_unit(u, slot * 2 + 1))
                    hi_p(t + 1)
                    hi_x2(t + 1)
                else:
                    hi_w(t * 2 + 1, q1, w1_unit(u, slot * 2 + 1))
                    nc.scalar.preload_act_table(ACT.Silu)
                    act.sem_inc(hf3_ready, 2)
                    hi_w(NT * 2, q1, w2_unit(0))
                    for k in range(BT):
                        hi_h(0, 0, k)
                        if k == 0:
                            hi_w(NT * 2 + 1, q1, w2_unit(1))

            with act.Fori(0, NT // 2 - 1) as u:
                for slot in range(2):
                    tile2(u * 2 + slot, u, slot, False)
            for slot in range(2):
                tile2(NT - 2 + slot, NT // 2 - 1, slot, slot == 1)


            def tile3(t, slot, first, last):
                for f in range(NF):
                    act.wait_ge(f_full, t * NF + f + 1)
                    act.wait_ge(f_lo, t * NF + f + 1)
                    if first and f == 1:
                        act.wait_ge(xg_ready, NT * BT + 2)
                    nc.scalar.activation(HF3[:, f % 2], PS[:, f % 2], ACT.Silu,
                                         bias=b1f[:, f:f + 1]).then_inc(hf3_ready, 1)
                    act.wait_ge(hf3_ready, t * NF + 2 + f + 1)
                    act.wait_ge(hid_free, t * NF + f + 1)
                    nc.scalar.activation(hid3[f % 2][:, 0, :], HF3[:, f % 2], copy).then_inc(f_hi, 1)
                    if first and f + 2 < NF:
                        hi_w(NT * 2 + f + 2, q2[:, f % 2], w2_unit(f + 2))
                    if f in TURN_AT and not last:
                        hi_h(t + 1, 1 - slot, TURN_AT.index(f))

            tiles3(act, tile3)

        @block.gpsimd
        def _(pool):
            nc.gpsimd.memset(ident[:], 0.0).then_inc(made, 1)
            nc.gpsimd.memset(tri[:], 0.0).then_inc(made, 1)
            nc.gpsimd.memset(half, -0.5)
            nc.gpsimd.memset(eps_col, EPS).then_inc(made, 1)
            pool.wait_ge(made, 3)
            nc.gpsimd.affine_select(out=ident[:], in_=ident[:], compare_op=ALU.not_equal, fill=1.0, base=0,
                                    pattern=[[-1, P]], channel_multiplier=1).then_inc(consts, 1)
            nc.gpsimd.affine_select(out=tri[:], in_=tri[:], compare_op=ALU.is_ge, fill=-BIG, base=0,
                                    pattern=[[-1, P]], channel_multiplier=1).then_inc(consts, 1)
            nc.gpsimd.iota(keys[:], [[1, 512]], base=0, channel_multiplier=0).then_inc(consts, 1)

            def rstd(n, var, out, turn=0, per=0):
                pool.wait_ge(var_ready, turn * per + n + 1)
                nc.gpsimd.tensor_tensor(out, var, eps_col.to_broadcast(list(out.shape)), ALU.add).then_inc(eps_added, 1)
                pool.wait_ge(eps_added, turn * per + n + 1)
                nc.gpsimd.tensor_tensor(out, out, half.to_broadcast(list(out.shape)), ALU.pow).then_inc(
                    rstd_ready, 1)

            with pool.Fori(0, B) as b:
                for t in range(NB):
                    rstd(t, mv1[:, t, 1:2], rs1[:, t:t + 1], b, 2 * NB)
                for i in range(NB):
                    rstd(NB + i, mvE[:, i % 2, 1:2], rsE[:, i % 2:i % 2 + 1], b, 2 * NB)

            R2 = 2 * NB * B

            def norm2(k, t, first):
                rstd(R2 + BT + first + k, mvE[:, k, 1:2], rsE[:, k:k + 1], t, 2 * BT)

            def bias_x2(t, slot, k):
                pool.wait_ge(tp_full, t * TPT + TP2 + TPL + BT + 2 + k + 1)
                nc.gpsimd.tensor_tensor(N[:, slot, k], N[:, slot, k], vec2[:, 4], ALU.add).then_inc(x2_biased, 1)

            def bias_xo(t, k, x):
                pool.wait_ge(xo_in[k % 2], t * 32 + k // 2 * 16 + 16)
                nc.gpsimd.tensor_tensor(x, x, vec2[:, 3], ALU.add).then_inc(xo_ready, 1)

            for k in range(BT):
                rstd(R2 + k, mvE[:, k, 1:2], rsE[:, k:k + 1])

            R3 = R2 + NT * 2 * BT

            def rstd_of_x(t):
                rstd(R3, mvX[:, :, 1], rs_x, t, 1 + BT)

            def rstd_of_h0(t, k):
                rstd(R3 + 1 + k, mvH[:, k, 1:2], rsH[:, k:k + 1], t, 1 + BT)

            def tile2(t, slot, last):
                for k in range(BT):
                    bias_x2(t, slot, k)
                x = xo_last if last else xo
                bias_xo(t, 0, x[0])
                bias_xo(t, 1, x[1])
                if last:
                    first = R2 + BT + (NT - 1) * 2 * BT
                    rstd(first, mvX[:, :, 1], rs_x)
                    for k in range(BT):
                        rstd(first + 1 + 2 * k, mvH[:, k, 1:2], rsH[:, k:k + 1])
                        rstd(first + 2 + 2 * k, mvE[:, k, 1:2], rsE[:, k:k + 1])
                else:
                    for k in range(BT):
                        norm2(k, t, 0)
                bias_xo(t, 2, x[0])
                bias_xo(t, 3, x[1])
                if not last:
                    for k in range(BT):
                        norm2(k, t, BT)

            pool.wait_ge(vec2_ready, 2)
            tiles(pool, tile2)

            pool.wait_ge(bias3_ready, 1)
            for k in range(BT):
                pool.wait_ge(hn_ready, k + 1)
                nc.gpsimd.tensor_tensor(base[:, 0, k], base[:, 0, k], bias3, ALU.add).then_inc(base_biased, 1)
            with pool.Fori(1, NT) as t:
                rstd_of_x(t)
                for k in range(BT):
                    rstd_of_h0(t, k)

        @block.vector
        def _(dve):
            for s, n in ((tp_free, 2), (mm_free, 2), (s_free, 2), (z_free, 2), (y_free, 4), (h_lo, 2),
                         (f_lo, 2), (o_free, 4), (xg_ready, 2)):
                dve.sem_inc(s, n)

            def lo(k, dst, src, hi_part, turn=0, per=0, sems=(tp_hi, tp_free), inc=1):
                dve.wait_ge(sems[0], turn * per + k + 1)
                nc.vector.tensor_tensor(dst, src, hi_part.bitcast(F32), ALU.subtract).then_inc(sems[1], inc)

            def thirds(bank):
                return bank.rearrange("p (c n) -> p c n", c=C)

            def apart():
                dve.sem_inc(waited, 1)

            p0 = Steps(dve, dve_p0)
            for at in (SC, SCP + SC):
                p0.done(nc.vector.memset(ctxT[:, :, :, at:at + SCP - SC].bitcast(F32), 0.0))
            p0.done(nc.vector.memset(ones, 1.0))
            dve.wait_ge(consts, 3)

            for k in range(3 * C):
                w = (wq1T, wk1T, wq2T)[k // C]
                lo(k, w[:, k % C, 1, :], PS[:, 2 + k % 2], w[:, k % C, 0, :])
            for c in range(C):
                half_of = [ctxT[:, c, h, :].rearrange("p (b n) -> p b n", b=B)[:, :, 0:SC] for h in range(2)]
                lo(3 * C + c, half_of[1],
                   PS[:, 2 + c % 2, 0:2 * SCP].rearrange("p (b n) -> p b n", b=B)[:, :, 0:SC], half_of[0])

            def split_stage(slot, w, his, n0, done):
                for c in range(C):
                    dve.wait_ge(his, n0 + c + 1)
                    nc.vector.tensor_tensor(w[:, c, 1, :], stage[:, slot, c], w[:, c, 0, :].bitcast(F32),
                                            ALU.subtract).then_inc(done, 1)

            mm = (mm_hi, mm_free)
            split_stage(1, wk2, split_hi, 0, split_lo)
            for m in range(C):
                lo(m, A[:, m, 1, :], PS[:, 4 + m % 2], A[:, m, 0, :], sems=mm)
            split_stage(0, wv2, split_hi, C, split_lo)
            for m in range(C):
                lo(C + m, kT2[:, m, 1, :], PS[:, 4 + m % 2, 0:2 * SCP], kT2[:, m, 0, :], sems=mm)
            for b in range(B):
                lo(2 * C + b, v_0[0:SC, b, 1, :], PS[0:SC, 4 + b % 2], v_0[0:SC, b, 0, :], sems=mm)
            for m in range(C):
                lo(2 * C + B + m, g_0[:, m, 1, :], PS[:, 4 + m % 2, 0:2 * SCP], g_0[:, m, 0, :], sems=mm)
            dve.wait_ge(split_hi, 2 * C + 2)
            p0.link(nc.vector.tensor_scalar(gf_half, gate_f, 0.5, None, ALU.mult))

            def statistics(steps, x, mv, k):
                steps.link(nc.vector.bn_stats(st[:, k % 2], x))
                apart()
                nc.vector.bn_aggr(mv, st[:, k % 2]).then_inc(var_ready, 1)

            def scale_shift(steps, x, mean, rs, g, b, done):
                steps.link(nc.vector.scalar_tensor_tensor(out=x, in0=x, scalar=mean, in1=g,
                                                          op0=ALU.subtract, op1=ALU.mult))
                nc.vector.scalar_tensor_tensor(out=x, in0=x, scalar=rs, in1=b,
                                               op0=ALU.mult, op1=ALU.add).then_inc(done, 1)

            with dve.Fori(0, B) as b:
                p1 = Steps(dve, dve_p1, DVE1, b)

                def stats_x(t):
                    dve.wait_ge(x_in[t % 2], b * NB * 16 + (t // 2 + 1) * 16)
                    statistics(p1, xin[:, t % 2], mv1[:, t], t)

                def norm_x(t):
                    dve.wait_ge(rstd_ready, b * 2 * NB + t + 1)
                    dve.wait_ge(tp_full, b * TP1 + TP0 + max(t - 1, 0))
                    nc.vector.tensor_scalar(xn[:, t % 2], xin[:, t % 2], mv1[:, t, 0:1], rs1[:, t:t + 1],
                                            ALU.subtract, ALU.mult).then_inc(x_normed, 1)

                def lo_x(t):
                    half_of = [xT[:, :, h, t * P:(t + 1) * P] for h in range(2)]
                    lo(TP0 + t, half_of[1], thirds(PS[:, 2 + t % 2]), half_of[0], b, TP1)

                def lo_v(t):
                    lo(MM0 + t, V[:, t, 1, :], PS[:, 4 + t % 2], V[:, t, 0, :], b, MM1, mm)

                def lo_q(g, m):
                    lo(MM0 + NB + g * C + m, QT[:, m, 1, :], PS[:, 4 + m % 2], QT[:, m, 0, :], b, MM1, mm)

                stats_x(0)
                for t in range(NB + 2):
                    if t + 1 < NB:
                        stats_x(t + 1)
                    if t < NB:
                        norm_x(t)
                    if 1 <= t <= NB:
                        lo_x(t - 1)
                    if t == 1:
                        for c in range(C):
                            dve.wait_ge(wv_hi, b * C + c + 1)
                            nc.vector.tensor_tensor(wv[:, c, 1, :], stage[:, 0, c],
                                                    wv[:, c, 0, :].bitcast(F32),
                                                    ALU.subtract).then_inc(wv_lo, 1)
                    if t >= 2:
                        lo_v(t - 2)
                for m in range(C):
                    lo_q(0, m)
                for c in range(4):
                    dve.wait_ge(s_full, b * SS1 + c + 1)
                    if c > 1:
                        dve.wait_ge(s_free, b * SS1 + 2 + c - 1)
                    nc.vector.tensor_scalar(xn[0:1, c % 2], PS[0:1, c % 2], 0.0, None, ALU.not_equal, ALU.add,
                                            accum_out=cnt[0:1, c:c + 1]).then_inc(s_free, 1)
                dve.wait_ge(s_free, b * SS1 + 2 + 4)
                nc.vector.tensor_reduce(keys_seen[0:1], cnt[0:1], AX.X, ALU.add).then_inc(counted, 1)
                dve.wait_ge(s_full, b * SS1 + 6)
                for c in range(4):
                    ins = nc.vector.tensor_scalar(lnc[:, c:c + 1], PS[:, 0, 0:1], -512.0 * c, None, ALU.add)
                    if c < 3:
                        p1.done(ins)
                ins.then_inc(s_free, 2)
                dve.wait_ge(s_free, b * SS1 + 2 + 6)
                for c in range(4):
                    last = p1.done(nc.vector.tensor_scalar(pad[:, c * 512:(c + 1) * 512], keys[:],
                                                           lnc[:, c:c + 1], -BIG, ALU.is_ge, ALU.mult))
                p1.wait(last)
                p1.link(nc.vector.reciprocal(ln, lnc[:, 0:1]))
                p1.link(nc.vector.tensor_scalar(ln, ln, 0.0, None, ALU.mult))
                p1.link(nc.vector.tensor_scalar(pad, pad, ln, None, ALU.add))

                def scores(i, c):
                    k, w, at = 6 + T_BEFORE[i] + c, width_of(i, c), c * 512
                    bank, row = PS[:, k % 2], Srow[:, i % 2]
                    dve.wait_ge(s_full, b * SS1 + k + 1)
                    if c == 0:
                        dve.wait_ge(tp_full, b * TP1 + TP0 + (NB + T_BEFORE[i - 1] if i > 1 else 0))

                    def masked_max(lo_, n, src, m):
                        apart()
                        return nc.vector.tensor_tensor_reduce(
                            out=row[:, at + lo_:at + lo_ + n], in0=src, in1=pad[:, at + lo_:at + lo_ + n],
                            scale=1.0, scalar=-3.4e38, op0=ALU.add, op1=ALU.max, accum_out=mx[:, i % 2, m:m + 1])

                    if c < i // 4:
                        masked_max(0, w, bank[:, 0:w], c).then_inc(s_free, 1)
                        return
                    d = w - P
                    if d:
                        p1.done(masked_max(0, d, bank[:, 0:d], c))
                    nc.vector.tensor_tensor(row[:, at + d:at + w], bank[:, d:w], tri[:], ALU.add).then_inc(
                        s_free, 1)
                    dve.wait_ge(s_free, b * SS1 + 2 + k + 1)
                    n = c + (2 if d else 1)
                    p1.link(masked_max(d, P, row[:, at + d:at + w], n - 1))
                    p1.link(nc.vector.tensor_reduce(nmx[:, 0:1], mx[:, i % 2, 0:n], AX.X, ALU.max))
                    nc.vector.tensor_scalar(nb[:, i % 2:i % 2 + 1], nmx[:, 0:1], -SCALE, None,
                                            ALU.mult).then_inc(mx_ready, 1)

                def end_a(i):
                    dve.wait_ge(x_in[i % 2], b * NB * 16 + (NB // 2 + i // 2 + 1) * 16)
                    p1.done(nc.vector.tensor_scalar(xin[:, i % 2], xin[:, i % 2], mv1[:, i, 0:1],
                                                    rs1[:, i:i + 1], ALU.subtract, ALU.mult))
                    p1.link(nc.vector.reciprocal(rcp[:, i % 2:i % 2 + 1], rowsum[:, i % 4:i % 4 + 1]))
                    dve.wait_ge(x1_out[i % 2], b * NB * 8 + (i // 2 + 1) * 16)
                    dve.wait_ge(pt_free, b * PTK + 2 + T_BEFORE[i + 1])
                    nc.vector.scalar_tensor_tensor(out=U[:, i % 2], in0=PS[:, 6 + i % 2],
                                                   scalar=rcp[:, i % 2:i % 2 + 1], in1=xin[:, i % 2],
                                                   op0=ALU.mult, op1=ALU.add).then_inc(z_free, 1)
                    dve.wait_ge(z_free, b * NB + 2 + i + 1)
                    statistics(p1, U[:, i % 2], mvE[:, i % 2], i)

                def end_b(i):
                    dve.wait_ge(rstd_ready, b * 2 * NB + NB + i + 1)
                    scale_shift(p1, U[:, i % 2], mvE[:, i % 2, 0:1], rsE[:, i % 2:i % 2 + 1],
                                ln1[:, 0], ln1[:, 1], x1_ready)

                for kind, i, c in ORDER:
                    if kind == "S":
                        scores(i, c)
                    elif kind == "Q":
                        lo_q(i, c)
                    elif kind == "T":
                        k, w = T_BEFORE[i] + c, width_of(i, c)
                        lo(TP0 + NB + k, PT[k % 2][:, 1, 0:w], PS[:, 2 + k % 2, 0:w],
                           PT[k % 2][:, 0, 0:w], b, TP1)
                    elif kind == "A":
                        end_a(i)
                    elif kind == "B":
                        end_b(i)
            assert p1.n == DVE1

            R2 = 2 * NB * B
            def lo_t(k, dst, k_bank, turn=0, per=0):
                lo(k, dst[1], thirds(PS[:, 2 + k_bank % 2]), dst[0], turn, per)

            for b in range(B):
                lo_t(TP2 + b, [x1T[:, :, h, b * P:(b + 1) * P] for h in range(2)], b)
            dve.wait_ge(c_full, 1)
            for b in range(B):
                ins = nc.vector.tensor_scalar(xn[0:1, b, 0:SC], PS[0:1, 0, b * SCP:b * SCP + SC], 0.0, None,
                                              ALU.not_equal, ALU.add, accum_out=keys_seen2[0:1, b:b + 1])
                if b == 0:
                    p0.done(ins)
            ins.then_inc(c_free, 1)
            dve.wait_ge(c_free, 1)
            p0.wait()
            nc.vector.tensor_copy(sum2[0:1, 0:1], keys_seen2[0:1, 0:1]).then_inc(counted, 1)
            dve.wait_ge(c_full, 2)
            p0.link(nc.vector.tensor_copy(len2, PS[:, 1, 0:B]))
            for b in range(B):
                p0.done(nc.vector.tensor_scalar(mask2[:, b], keys[:, 0:SC], len2[:, b:b + 1], -BIG,
                                                ALU.is_ge, ALU.mult))
            p0.wait()
            p0.link(nc.vector.reciprocal(rc2[:, 0:B], len2))
            p0.link(nc.vector.tensor_scalar(rc2[:, 0:B], rc2[:, 0:B], 0.0, None, ALU.mult))
            p0.link(nc.vector.tensor_tensor(mask2[:], mask2[:],
                                            rc2[:, 0:B].unsqueeze(2).to_broadcast([P, B, SC]), ALU.add))
            nc.vector.tensor_copy(sum2[:, 0:1], len2[:, 0:1]).then_inc(len_seen, 1)
            dve.wait_ge(vec2_in, 16 * 5)
            for n in (2, 3):
                nc.vector.tensor_scalar(vec2[:, n], vec2[:, n], gate_x, None, ALU.mult).then_inc(vec2_ready, 1)
            dve.wait_ge(vec2_ready, 2)

            def rows(slot):
                return S2[:, slot, :].rearrange("p (k n) -> p k n", k=BT)[:, :, 0:SC]

            def softmax(steps, t, slot):
                for k in range(BT):
                    lo_t(TP2 + TPL + k, [x1T[:, :, h, k * P:(k + 1) * P] for h in range(2)], k, t, TPT)
                s = rows(slot)
                dve.wait_ge(c_full, t + 3)
                bank = PS[:, 0, 0:BT * SCP].rearrange("p (k n) -> p k n", k=BT)[:, :, 0:SC]
                m = mask2[:, bass.ds(t // TPB, 1), :].to_broadcast([P, BT, SC])
                nc.vector.tensor_tensor(s, bank, m, ALU.add).then_inc(c_free, 1)
                dve.wait_ge(c_free, t + 2)
                steps.link(nc.vector.tensor_reduce(mx2, s, AX.X, ALU.max))
                nc.vector.tensor_tensor(s, s, mx2.unsqueeze(2).to_broadcast([P, BT, SC]),
                                        ALU.subtract).then_inc(sm_ready, 1)

            def cross_end(steps, t, slot):
                dve.wait_ge(e_ready, t + 1)
                steps.link(nc.vector.tensor_reduce(sum2, rows(slot), AX.X, ALU.add))
                steps.link(nc.vector.reciprocal(rc2, sum2))
                lo(TP2 + TPL + BT + 1, PT2[0:SC, 1, :], PS[0:SC, 2], PT2[0:SC, 0, :], t, TPT, inc=2)

                def norm(k):
                    dve.wait_ge(rstd_ready, t * 2 * BT + R2 + k + 1)
                    scale_shift(steps, N[:, slot, k], mvE[:, k, 0:1], rsE[:, k:k + 1],
                                vec2[:, 0], vec2[:, 1], x2_ready)

                for k in range(BT):
                    x = N[:, slot, k]
                    dve.wait_ge(z2_full, t * BT + k + 1)
                    nc.vector.scalar_tensor_tensor(out=x, in0=PS[:, 6 + k % 2], scalar=rc2[:, k:k + 1], in1=x,
                                                   op0=ALU.mult, op1=ALU.add).then_inc(z_free, 1)
                    dve.wait_ge(z_free, t * BT + 2 + B * NB + k + 1)
                    statistics(steps, x, mvE[:, k], k)
                    if k:
                        norm(k - 1)
                norm(BT - 1)
                for k in range(BT):
                    lo_t(TP2 + TPL + BT + 2 + k, [x2T[:, :, h, k * P:(k + 1) * P] for h in range(2)], k, t, TPT)

            for n, w in enumerate((fc1, fc2)):
                for c in range(C):
                    dve.wait_ge(fcw_hi, n * C + c + 1)
                    nc.vector.tensor_tensor(w[:, c, 1, :], stage[:, n, c], w[:, c, 0, :].bitcast(F32),
                                            ALU.subtract).then_inc(fcw_lo, 1)
            softmax(p0, 0, 0)
            cross_end(p0, 0, 0)

            def scale_codes(q, sc, *loads):
                for sem_, v in loads:
                    dve.wait_ge(sem_, v)
                nc.vector.scalar_tensor_tensor(out=q, in0=q.bitcast(I32), scalar=-128.0, in1=sc,
                                               op0=ALU.add, op1=ALU.mult).then_inc(codes_scaled, 1)

            def lo_w(n, src, dst):
                dve.wait_ge(w_hi, n + 1)
                nc.vector.tensor_tensor(dst[1], src, dst[0].bitcast(F32), ALU.subtract).then_inc(w_ready, 1)

            def tile2(t, u, slot, last):
                p2 = Steps(dve, dve_p2, DVE2, t)
                scale_codes(q1, sc1, (q1_in, t * 64 + 32))
                for f in range(C):
                    dve.wait_ge(h_hi, t * C + f + 1)
                    nc.vector.tensor_tensor(hid2[:, f, 1, :], HF2[:, f % 2], hid2[:, f, 0, :].bitcast(F32),
                                            ALU.subtract).then_inc(h_lo, 1)
                    if f == 1:
                        lo_w(t * 2, q1, w1_unit(u, slot * 2))
                if not last:
                    softmax(p2, t + 1, 1 - slot)
                scale_codes(q1, sc1, (q1_in, t * 64 + 64))
                lo_w(t * 2 + 1, q1, w1_unit(u, slot * 2 + 1))
                if last:
                    stats_x3(p2, 0, 0)

                def add_y(k):
                    x = N[:, slot, k]
                    dve.wait_ge(y_full, t * BT + k + 1)
                    dve.wait_ge(x2_biased, t * BT + k + 1)
                    nc.vector.tensor_tensor(x, PS[:, 4 + k % 2], x, ALU.add).then_inc(y_free, 1)
                    dve.wait_ge(y_free, t * BT + 4 + k + 1)
                    statistics(p2, x, mvE[:, k], k)

                def norm(k, n):
                    x = N[:, slot, k]
                    dve.wait_ge(rstd_ready, n)
                    p2.link(nc.vector.scalar_tensor_tensor(out=x, in0=x, scalar=mvE[:, k, 0:1], in1=vec2[:, 2],
                                                           op0=ALU.subtract, op1=ALU.mult))
                    dve.wait_ge(xo_ready, t * BT + k + 1)
                    nc.vector.scalar_tensor_tensor(out=x, in0=x, scalar=rsE[:, k:k + 1],
                                                   in1=(xo_last if last else xo)[k % 2],
                                                   op0=ALU.mult, op1=ALU.add).then_inc(xg_ready, 1)

                if not last:
                    for k in range(BT):
                        add_y(k)
                        if k:
                            norm(k - 1, t * 2 * BT + R2 + BT + k)
                    norm(BT - 1, t * 2 * BT + R2 + BT + BT)
                    cross_end(p2, t + 1, 1 - slot)
                    assert p2.n == DVE2, p2.n
                    return
                n0 = R2 + BT + t * 2 * BT
                dve.wait_ge(vec3_in, 32)
                for k in range(BT):
                    make_h0(p2, 0, 0, k, n0 + 1)
                    add_y(k)
                    if k == 0:
                        scale_codes(q1, sc1, (q1_in, NT * 64 + 32))
                    norm_h(p2, 0, 0, k, n0 + 2 + 2 * k, False)
                    if k == 0:
                        lo_w(NT * 2, q1, w2_unit(0))
                    if k == 1:
                        scale_codes(q1, sc1, (q1_in, NT * 64 + 64))
                    if k:
                        lo_h(0, 0, k - 1)
                    if k == 1:
                        lo_w(NT * 2 + 1, q1, w2_unit(1))
                lo_h(0, 0, BT - 1)
                for k in range(BT):
                    norm(k, n0 + 3 + 2 * k)

            R3 = R2 + NT * 2 * BT

            def stats_x3(steps, t, slot):
                dve.wait_ge(b_in[slot], (t // 2) * 16 + 16)
                for k in range(BT):
                    steps.link(nc.vector.bn_stats(st[:, k % 2], base[:, slot, k]))
                    apart()
                    ins = nc.vector.bn_aggr(mvX[:, k], st[:, k % 2])
                    if k < BT - 1:
                        steps.done(ins)
                ins.then_inc(var_ready, 1)

            def make_h0(steps, t, slot, k, n):
                if k == 0:
                    dve.wait_ge(rstd_ready, n)
                dve.wait_ge(tp_full, t * BT + TP3 + max(k - 1, 0))
                steps.link(nc.vector.tensor_scalar(H0[:, k % 2], base[:, slot, k], mvX[:, k, 0:1],
                                                   rs_x[:, k:k + 1], ALU.subtract, ALU.mult))
                statistics(steps, H0[:, k % 2], mvH[:, k], k)

            def norm_h(steps, t, slot, k, n, biased=True):
                x = base[:, slot, k]
                steps.link(nc.vector.scalar_tensor_tensor(out=x, in0=H0[:, k % 2], scalar=gate_f, in1=x,
                                                          op0=ALU.mult, op1=ALU.add))
                if biased:
                    steps.done(nc.vector.tensor_tensor(x, x, bias3, ALU.add))
                dve.wait_ge(rstd_ready, n)
                scale_shift(steps, H0[:, k % 2], mvH[:, k, 0:1], rsH[:, k:k + 1], vec3[:, 0], vec3[:, 1],
                            hn_ready)

            def lo_h(t, slot, k):
                lo_t(TP3 + k, [hT[:, slot * C:(slot + 1) * C, h, k * P:(k + 1) * P] for h in range(2)],
                     k, t, BT)

            with dve.Fori(0, NT // 2 - 1) as u:
                for slot in range(2):
                    tile2(u * 2 + slot, u, slot, False)
            for slot in range(2):
                tile2(NT - 2 + slot, NT // 2 - 1, slot, slot == 1)
            nc.vector.tensor_copy(sum2[:, 0:1], len2[:, 0:1]).then_inc(p2_end, 1)

            dve.wait_ge(bias3_in, 16)
            nc.vector.tensor_scalar(bias3, bias3, gf_half, None, ALU.mult).then_inc(bias3_ready, 1)

            def tile3(t, slot, first, last):
                p3 = Steps(dve, dve_p3, DVE3, t)
                for f in range(NF):
                    dve.wait_ge(f_hi, t * NF + f + 1)
                    nc.vector.tensor_tensor(hid3[f % 2][:, 1, :], HF3[:, f % 2],
                                            hid3[f % 2][:, 0, :].bitcast(F32), ALU.subtract).then_inc(f_lo, 1)
                    if first and 0 < f and f + 1 < NF:
                        lo_w(NT * 2 + f + 1, q2[:, (f + 1) % 2], w2_unit(f + 1))
                    if first and f + 2 < NF:
                        scale_codes(q2[:, f % 2], sc2, (q2_in[f % 2], (f + 2) // 2 * 16), (sc2_in, (f + 1) * 16))
                    if not last:
                        n0 = (t + 1) * (1 + BT) + R3 + 1
                        if f in TURN_AT:
                            lo_h(t + 1, 1 - slot, TURN_AT.index(f))
                        if f == TURN_AT[0] - 3:
                            stats_x3(p3, t + 1, 1 - slot)
                        if f + 2 in TURN_AT:
                            make_h0(p3, t + 1, 1 - slot, TURN_AT.index(f + 2), n0)
                        if f + 1 in TURN_AT:
                            k = TURN_AT.index(f + 1)
                            norm_h(p3, t + 1, 1 - slot, k, n0 + k + 1)
                dve.wait_ge(base_biased, BT)
                for k in range(BT):
                    x = base[:, slot, k]
                    if k < BT - 1:
                        dve.wait_ge(o_full, t * (BT - 1) + k + 1)
                    else:
                        dve.wait_ge(hid_free, t * NF + 2 + NF)
                    nc.vector.scalar_tensor_tensor(out=x, in0=PS[:, 4 + k], scalar=gf_half, in1=x,
                                                   op0=ALU.mult, op1=ALU.add).then_inc(o_free, 1)
                if not last:
                    assert p3.n == DVE3, p3.n

            tiles3(dve, tile3)


_INS = ["x", "ctx_1024", "g_xattn", "g_ffn", "L0_xattn_Wq1", "L0_xattn_Wk1", "L0_xattn_Wv1", "L0_xattn_Wq2",
        "L0_xattn_Wk2", "L0_xattn_Wv2", "L0_xattn_fc1_w", "L0_xattn_fc1_b", "L0_xattn_fc2_w", "L0_xattn_fc2_b",
        "L0_xattn_ln1_g", "L0_xattn_ln1_b", "L0_xattn_ln2_g", "L0_xattn_ln2_b", "L0_xattn_ln3_g",
        "L0_xattn_ln3_b", "L0_ffn_ln_gamma", "L0_ffn_ln_beta", "L0_ffn_fc1_q", "L0_ffn_fc1_scales",
        "L0_ffn_fc1_bias", "L0_ffn_fc2_q", "L0_ffn_fc2_scales", "L0_ffn_fc2_bias"]


def kernel(**inputs):
    import numpy as _np
    import concourse.bacc as _bacc
    from concourse import mybir as _mybir
    from concourse.bass_utils import run_bass_kernel_spmd as _run

    nc = _bacc.Bacc("TRN2", target_bir_lowering=False, num_devices=1)
    arrays, aps = {}, {}
    for name in _INS:
        v = _np.ascontiguousarray(inputs[name])
        arrays[f"in_{name}"] = v
        aps[name] = nc.dram_tensor(f"in_{name}", v.shape, _mybir.dt.from_np(v.dtype), kind="ExternalInput").ap()
    out = nc.dram_tensor("out_0", (B, S, E), F32, kind="ExternalOutput").ap()
    build(nc, aps, out)
    r = _run(nc, [arrays], core_ids=[0])
    return r.results[0]["out_0"]
```

```python
from contextlib import ExitStack

import concourse.bass as bass
from concourse import mybir

F32 = mybir.dt.float32
F32R = mybir.dt.float32r
BF16 = mybir.dt.bfloat16
I16 = mybir.dt.int16
I32 = mybir.dt.int32
ALU = mybir.AluOpType
ACT = mybir.ActivationFunctionType
AX = mybir.AxisListType

P = 128
B, S, E = 2, 2048, 512
C = E // P
NB = S // P
SC = 77
SCP = 80
TILE = 512
BT = TILE // P
NT = B * S // TILE
TPB = S // TILE
FF = 2048
NF = FF // P
EPS = 1e-5
SCALE = float(1.0 / (E // 16) ** 0.5)
BIG = 1e38
PASSES = ((0, 0), (0, 1), (1, 0))

KB = 256


class Steps:

    def __init__(self, eng, sem, per=0, turn=0):
        self.eng, self.sem, self.per, self.turn, self.n = eng, sem, per, turn, 0

    def done(self, ins):
        ins.then_inc(self.sem, 1)
        self.n += 1
        return self.n

    def wait(self, n=None):
        self.eng.wait_ge(self.sem, self.turn * self.per + (self.n if n is None else n))

    def link(self, ins):
        self.done(ins)
        self.wait()


def chunks_of(i):
    return i // 4 + 1


def width_of(i, c):
    return 512 if c < i // 4 else (i % 4 + 1) * P


T_BEFORE = [sum(chunks_of(j) for j in range(i)) for i in range(NB + 1)]


def attention_order():
    order = [("S", 0, 0)]
    for i in range(NB):
        n0 = chunks_of(i)
        n1 = chunks_of(i + 1) if i + 1 < NB else 0
        new_group = i % 4 == 3 and i + 1 < NB
        order.append(("T", i, 0))
        if i:
            order.append(("A", i - 1, 0))
        if new_group:
            order += [("Q", i // 4 + 1, m) for m in range(C)]
        if n1 and not new_group:
            order.append(("S", i + 1, 0))
        if i:
            order.append(("B", i - 1, 0))
        s = 0 if new_group else 1
        for c in range(1, n0):
            order.append(("T", i, c))
            if new_group:
                order.append(("V", i, c - 1))
            if s < n1:
                order.append(("S", i + 1, s))
                s += 1
            if not new_group:
                order.append(("V", i, c - 1))
        order.append(("V", i, n0 - 1))
        while s < n1:
            order.append(("S", i + 1, s))
            s += 1
    order += [("A", NB - 1, 0), ("B", NB - 1, 0)]
    return order


ORDER = attention_order()
HIDDEN = (0, 1, 4, 5)
TURN_AT = (7, 9, 11, 13)

TP0, MM0 = 16, 14
TP1 = NB + T_BEFORE[NB]
MM1 = 2 * NB
SS1 = 4 + 2 + T_BEFORE[NB]
TP2 = TP0 + B * TP1
TPT = 2 * BT + 2
TP3 = TP2 + NT * TPT
MM2 = MM0 + B * MM1

DVE1, DVE2, DVE3 = 134, 19, 27
PTK = T_BEFORE[NB]


def build(nc, a, out):
    ctx = ExitStack()
    with ctx:
        def sb(name, shape, dt=F32):
            return ctx.enter_context(nc.sbuf_tensor(name, shape, dt))

        def sem(name):
            return ctx.enter_context(nc.semaphore(name))

        x1_dram = nc.dram_tensor("x1_scratch", (B * S, E), F32, kind="Internal").ap()
        xg_dram = nc.dram_tensor("xg_scratch", (B * S, E), F32, kind="Internal").ap()
        g_dram = nc.dram_tensor("g_scratch", (B, P, C * 2 * SCP), F32, kind="Internal").ap()
        v_dram = nc.dram_tensor("v_scratch", (SC, B * 2 * E), F32, kind="Internal").ap()
        x_dram = a["x"].rearrange("b s e -> (b s) e")
        out_dram = out.rearrange("b s e -> (b s) e")

        R = sb("split", [P, 112 * KB], F32R)
        with nc.sbuf_tensor("split_x", [P, 16 * KB], F32R) as X:
            pass
        tile_x = sb("tile_x", [P, 2, BT, E])
        Q = sb("split_q", [P, 32 * KB], F32R)
        T0 = sb("split_0", [P, 4 * KB], F32R)
        with nc.sbuf_tensor("split_1", [P, 4 * KB], F32R) as T1:
            pass
        codes1 = sb("codes", [P, 2, E])
        F = sb("plain", [P, 37 * KB])
        T = [t[:].rearrange("p (h n) -> p h n", h=2) for t in (T0, T1)]

        def pair(at, chunks, width, mem=R):
            return mem[:, at * KB:at * KB + chunks * 2 * width].rearrange(
                "p (c h n) -> p c h n", c=chunks, h=2)

        def pairs(*places):
            return [pair(at + 4 * i, 1, E, mem)[:, 0] for mem, at, n in places for i in range(n)]

        def plain(at, *dims):
            n = 1
            for d in dims:
                n *= d
            v = F[:, at:at + n]
            if len(dims) == 2:
                v = v.rearrange("p (a b) -> p a b", a=dims[0])
            if len(dims) == 3:
                v = v.rearrange("p (a b c) -> p a b c", a=dims[0], b=dims[1])
            return v

        wq1T, wk1T, wq2T = pair(0, C, E), pair(16, C, E), pair(32, C, E)
        wk2, wv2 = pair(48, C, E), pair(64, C, E)
        ctxT, kT2 = pair(80, C, 2 * SCP), pair(85, C, 2 * SCP)
        g_0 = R[:, 90 * KB:95 * KB].rearrange("p (b c h n) -> p b c h n", b=B, c=C, h=2)
        v_0 = pair(95, B, E)
        stage = plain(0, 2, C, E)
        ctx_in = plain(6144, B, E)
        xT, V = pair(0, C, S), pairs((R, 64, 12), (X, 0, 4))
        A, QT, PT = pair(0, C, E, Q), pair(16, C, E, Q), T
        wv = QT
        Srow = plain(0, 2, S)
        xa = plain(2048, 4, E)
        xin, xn, U = plain(4096, 2, E), plain(5120, 2, E), plain(6144, 2, E)
        ln1 = plain(7168, 2, E)
        pad = plain(8192, S // 2).bitcast(BF16)
        x1T, x2T, hid2 = pair(16, C, E), pair(16, C, E), pair(32, C, E)
        G = R[:, 48 * KB:53 * KB].rearrange("p (s c h n) -> p s c h n", s=2, c=C, h=2)
        V2 = pair(53, B, E)
        PT2 = T[0]
        fc1, fc2 = pair(0, C, E, Q), pair(16, C, E, Q)
        N = plain(0, 2, BT, E)
        vec2 = plain(4096, 5, E)
        x1b, xo = tile_x[:, 0], tile_x[:, 1]
        fc_stage = [N[:, 0], N[:, 1]]
        rows_1 = T0[:, 0:2 * B * C].rearrange("p (h b c) -> p h b c", h=2, b=B)
        HF2 = plain(7168, 2, E)
        ST = HF2[0:SC, 0]
        S2 = plain(8192, 2, BT * SCP)
        q1, sc1 = codes1[:, 0], codes1[:, 1]
        W2 = pairs((R, 16, 12), (X, 0, 4))
        W1 = [pair(at, 1, FF)[:, 0] for at in (64, 80, 96, 0)]
        hT = pair(0, 2 * C, TILE, Q)
        hid3 = T
        base = plain(0, 2, BT, E)
        H0 = plain(4096, 2, E)
        q2, sc2 = plain(5120, 2, E), plain(6144, E)
        bias3 = plain(6656, E)
        HF3 = plain(7168, 2, E)
        vec3 = plain(8192, 2, E)

        ident = sb("ident", [P, P])
        tri = sb("tri", [P, P], BF16)
        keys = sb("keys", [P, 512], I16)
        small = sb("small", [P, 148])

        def col(at, n=1):
            return small[:, at:at + n]

        st = small[:, 0:12].rearrange("p (a b) -> p a b", a=2)
        mv1 = small[:, 12:44].rearrange("p (a b) -> p a b", a=NB)
        rs1 = col(44, NB)
        mvE = small[:, 60:68].rearrange("p (a b) -> p a b", a=4)
        rsE = col(68, 4)
        mx = small[:, 72:82].rearrange("p (a b) -> p a b", a=2)
        nmx, nb = col(82, 2), col(84, 2)
        rowsum, rcp = col(86, 4), col(90, 4)
        half, cnt, ln, lnc = col(94), col(95, 4), col(99), col(100, 4)
        gate_x, gate_f, gf_half = col(104), col(105), col(106)
        b1x, b1f = col(107, C), col(111, NF)
        mx2, sum2, rc2 = col(127, 4), col(131, 4), col(135, 4)
        len2 = col(139, 2)
        eps_col = col(141)
        keys_seen, keys_seen2 = col(142), col(143, 2)
        mvX, rs_x = small[:, 12:20].rearrange("p (a b) -> p a b", a=BT), col(44, BT)
        mvZ, rsZ = small[:, 28:36].rearrange("p (a b) -> p a b", a=BT), col(52, BT)
        mvH, rsH = small[:, 20:28].rearrange("p (a b) -> p a b", a=BT), col(48, BT)
        rows_in = small[:, 28:36].rearrange("p (b c) -> p b c", b=B)
        mask2 = sb("mask2", [P, 2, SC], BF16)
        ones = plain(9344, P)[0:1]

        PS = ctx.enter_context(nc.psum_tensor("banks", [P, 8, 512], F32))

        stage_in = [sem("stage_in_0"), sem("stage_in_1")]
        wq1_in = [sem(f"wq1_in_{j}") for j in range(C)]
        ctx_loaded, const_in, parked, consts = sem("ctx_loaded"), sem("const_in"), sem("parked"), sem("consts")
        tp_full, tp_hi, tp_free = sem("tp_full"), sem("tp_hi"), sem("tp_free")
        mm_full, mm_hi, mm_free = sem("mm_full"), sem("mm_hi"), sem("mm_free")
        split_hi, split_lo, gates_ready = sem("split_hi"), sem("split_lo"), sem("gates_ready")
        dve_p0, dve_p1, dve_p2, dve_p3 = sem("dve_p0"), sem("dve_p1"), sem("dve_p2"), sem("dve_p3")
        xa_in = [sem(f"xa_in_{k}") for k in range(4)]
        x_in = [sem("x_in_0"), sem("x_in_1")]
        x_normed, var_ready, rstd_ready, eps_added = (
            sem("x_normed"), sem("var_ready"), sem("rstd_ready"), sem("eps_added"))
        wv_in, wv_hi, wv_lo = sem("wv_in"), sem("wv_hi"), sem("wv_lo")
        s_full, s_free, counted = sem("s_full"), sem("s_free"), sem("counted")
        waited = sem("waited")
        mx_ready, p_ready, pt_free, z_free = sem("mx_ready"), sem("p_ready"), sem("pt_free"), sem("z_free")
        x1_ready = sem("x1_ready")
        x1_out = [sem("x1_out_0"), sem("x1_out_1")]
        vec2_ready = sem("vec2_ready")
        vec2_in, cross_in, fcw_in = sem("vec2_in"), sem("cross_in"), [sem("fc1_in"), sem("fc2_in")]
        fcw_hi, fcw_lo = sem("fcw_hi"), sem("fcw_lo")
        len_seen = sem("len_seen")
        n_in = [[sem(f"n_in_{s}_{k}") for k in range(BT)] for s in range(2)]
        g_in = [sem("g_in_0"), sem("g_in_1")]
        st_full, st_copied = sem("st_full"), sem("st_copied")
        c_full, c_free, sm_ready, e_ready = sem("c_full"), sem("c_free"), sem("sm_ready"), sem("e_ready")
        z2_full, x2_ready = sem("z2_full"), sem("x2_ready")
        rows_loaded, rows_hi, rows_lo = sem("rows_loaded"), sem("rows_hi"), sem("rows_lo")
        h_full, hf_ready, h_hi, h_lo = sem("h_full"), sem("hf_ready"), sem("h_hi"), sem("h_lo")
        y_full, y_free = sem("y_full"), sem("y_free")
        x2_biased, xo_ready, xg_ready = sem("x2_biased"), sem("xo_ready"), sem("xg_ready")
        xo_in = [sem(f"xo_in_{k}") for k in range(BT)]
        x1b_in = [sem(f"x1b_in_{k}") for k in range(BT)]
        xg_out = [sem(f"xg_out_{k}") for k in range(BT)]
        q1_in, sc2_in = sem("q1_in"), sem("sc2_in")
        q2_in = [sem("q2_in_0"), sem("q2_in_1")]
        codes_scaled, w_hi, w_ready = sem("codes_scaled"), sem("w_hi"), sem("w_ready")
        made = sem("made")
        p2_end, vec3_in, bias3_in, bias3_ready = sem("p2_end"), sem("vec3_in"), sem("bias3_in"), sem("bias3_ready")
        b_in = [sem("b_in_0"), sem("b_in_1")]
        hn_ready = sem("hn_ready")
        f_full, hf3_ready, f_hi, f_lo, hid_free = (
            sem("f_full"), sem("hf3_ready"), sem("f_hi"), sem("f_lo"), sem("hid_free"))
        o_full, o_free, base_biased = sem("o_full"), sem("o_free"), sem("base_biased")
        o_out = [sem("o_out_0"), sem("o_out_1")]

        block = ctx.enter_context(nc.Block())

        def bcast(v):
            return v.rearrange("(a e) -> a e", a=1).to_broadcast([P, v.shape[0]])

        def blocks(dram, t):
            return dram[bass.ds(t * TILE, TILE), :].rearrange("(k p) e -> p k e", p=P)

        def load_xa(eng, b, t):
            eng.dma_start(xa[:, t % 4], x_dram[bass.ds(b * S + t * P, P), :]).then_inc(xa_in[t % 4], 16)

        def tiles(eng, body):
            body(0, 0, True, False)
            with eng.Fori(0, NT // 2 - 1) as u:
                body(u * 2 + 1, 1, False, False)
                body(u * 2 + 2, 0, False, False)
            body(NT - 1, 1, False, True)

        def w1_unit(u, n):
            return [W1[n][:, h, bass.ds(u * E, E)] for h in range(2)]

        def w2_stage(f):
            return (q1, sc1) if f < 2 else (x1b[:, f - 2], x1b[:, f]) if f < 4 else (q2[:, f % 2], sc2)

        def w2_unit(f):
            return [W2[f][:, h, :] for h in range(2)]

        LAST_UNITS = [w2_unit(0), w2_unit(1), w1_unit(NT // 2 - 1, 2), w1_unit(NT // 2 - 1, 3)]

        @block.sync
        def _(sp):
            sp.sem_inc(x1_out[0], 16)
            sp.sem_inc(x1_out[1], 16)

            def weight(name, slot, done):
                sp.dma_start(stage[:, slot], a[name].rearrange("(c p) n -> p c n", p=P)).then_inc(done, 16)

            for j in range(C):
                cols = slice(j * P, (j + 1) * P)
                sp.dma_start(stage[:, 0, :, cols], a["L0_xattn_Wq1"][:, cols].rearrange("(c p) n -> p c n", p=P)
                             ).then_inc(wq1_in[j], 16)
            weight("L0_xattn_Wk1", 1, stage_in[1])
            sp.dma_start(ctx_in[0:SC], a["ctx_1024"].rearrange("b s e -> s b e")).then_inc(ctx_loaded, 16)
            sp.dma_start(ln1[:, 0], bcast(a["L0_xattn_ln1_g"])).then_inc(const_in, 16)
            sp.dma_start(ln1[:, 1], bcast(a["L0_xattn_ln1_b"])).then_inc(const_in, 16)
            sp.dma_start(gate_x, bcast(a["g_xattn"])).then_inc(const_in, 16)
            sp.dma_start(gate_f, bcast(a["g_ffn"])).then_inc(const_in, 16)
            sp.dma_start(b1x, a["L0_xattn_fc1_b"].rearrange("(c p) -> p c", p=P),
                         allow_slow_non_contiguous=True).then_inc(const_in, 16)
            sp.dma_start(b1f, a["L0_ffn_fc1_bias"].rearrange("(c p) -> p c", p=P),
                         allow_slow_non_contiguous=True).then_inc(const_in, 16)
            sp.wait_ge(tp_full, C)
            weight("L0_xattn_Wq2", 0, stage_in[0])
            sp.wait_ge(tp_full, 2 * C)
            weight("L0_xattn_Wk2", 1, stage_in[1])
            sp.wait_ge(tp_full, 3 * C)
            weight("L0_xattn_Wv2", 0, stage_in[0])
            sp.wait_ge(mm_free, 2 + MM0)
            sp.wait_ge(x_normed, 1)
            sp.dma_start(g_dram.rearrange("b p n -> p b n"),
                         g_0.rearrange("p b c h n -> p b (c h n)").bitcast(F32)).then_inc(parked, 16)
            sp.dma_start(v_dram, v_0[0:SC].rearrange("p c h n -> p (c h n)").bitcast(F32)).then_inc(parked, 16)

            with sp.Fori(0, B) as b:
                def load_x(i):
                    sp.wait_ge(z_free, b * NB + i + 1)
                    sp.dma_start(xin[:, i % 2], x_dram[bass.ds(b * S + i * P, P), :]).then_inc(x_in[i % 2], 16)

                for t in range(4, NB):
                    sp.wait_ge(x_normed, b * NB + t - 3)
                    load_xa(sp, b, t)
                load_x(0)
                load_x(1)
                for i in range(NB):
                    sp.wait_ge(x1_ready, b * NB + i + 1)
                    sp.dma_start(x1_dram[bass.ds(b * S + i * P, P), :], U[:, i % 2]).then_inc(
                        x1_out[i % 2], 16)
                    if i + 2 < NB:
                        load_x(i + 2)

            def load_n(t, slot, k):
                sp.dma_start(N[:, slot, k], x1_dram[bass.ds(t * TILE + k * P, P), :]).then_inc(n_in[slot][k], 16)

            def load_g(slot, b):
                sp.dma_start(G[:, slot:slot + 1].rearrange("p s c h n -> p s (c h n)").bitcast(F32),
                             g_dram[bass.ds(b, 1)].rearrange("b p n -> p b n")).then_inc(g_in[slot], 16)

            def load_x1b(t, k):
                sp.dma_start(x1b[:, k], x1_dram[bass.ds(t * TILE + k * P, P), :]).then_inc(x1b_in[k], 16)

            def load_xo(t, k):
                sp.dma_start(xo[:, k], x_dram[bass.ds(t * TILE + k * P, P), :]).then_inc(xo_in[k], 16)

            sp.wait_ge(fcw_lo, C)
            for p in range(2):
                sp.wait_ge(x1_out[p], 16 + 16 * NB // 2)
            for k in range(BT):
                load_n(0, 0, k)
            for p in range(2):
                sp.wait_ge(x1_out[p], 16 + 16 * B * NB // 2)
            for n, v in enumerate(("ln2_g", "ln2_b", "ln3_g", "ln3_b", "fc2_b")):
                sp.dma_start(vec2[:, n], bcast(a[f"L0_xattn_{v}"])).then_inc(vec2_in, 16)
            sp.wait_ge(c_full, 1)
            load_g(1, 0)
            for k in range(BT):
                sp.wait_ge(tp_full, TP2 + k + 1)
                load_x1b(1, k)
            for k in range(BT):
                load_xo(0, k)
            sp.wait_ge(fcw_lo, 2 * C)
            for k in range(BT):
                load_n(1, 1, k)

            def load_w1(u, n):
                cols = bass.ds(u * E, E)
                sp.dma_start(q1.bitcast(I32), a["L0_ffn_fc1_q"][n * P:(n + 1) * P, cols]).then_inc(q1_in, 16)
                sp.dma_start(sc1, a["L0_ffn_fc1_scales"][n:n + 1, cols].to_broadcast([P, E])).then_inc(q1_in, 16)

            def load_w2(f):
                q, sc = w2_stage(f)
                q_in, sc_in = ((q1_in, q1_in) if f < 2 else (x1b_in[f], x1b_in[f]) if f < 4
                               else (q2_in[f % 2], sc2_in))
                sp.dma_start(q.bitcast(I32), a["L0_ffn_fc2_q"][f * P:(f + 1) * P, :]).then_inc(q_in, 16)
                sp.dma_start(sc, a["L0_ffn_fc2_scales"][f:f + 1, :].to_broadcast([P, E])).then_inc(sc_in, 16)

            def tile2(t, u, slot, final, last):
                if not final:
                    for k in range(BT):
                        sp.wait_ge(tp_full, t * TPT + TPT + TP2 + k + 1)
                        load_x1b(t + 2, k)
                    sp.wait_ge(c_full, t + 3)
                    load_g(slot, (t + 2) // TPB)
                elif not last:
                    sp.wait_ge(tp_full, (NT - 1) * TPT + TP2 + BT)
                    sp.dma_start(x1b, blocks(xg_dram, 0)).then_inc(x1b_in[0], 16)
                sp.wait_ge(w_ready, t * 2 + 1)
                if last:
                    load_w2(1)
                    sp.wait_ge(w_ready, t * 2 + 2)
                    load_w1(u, 2)
                    sp.wait_ge(hn_ready, BT)
                    load_w2(2)
                    load_w2(3)
                    sp.wait_ge(w_ready, t * 2 + 3)
                    load_w1(u, 3)
                else:
                    load_w1(u, slot * 2 + 1)
                if final and not last:
                    sp.wait_ge(x2_ready, NT * BT)
                    for n, v in enumerate(("ln_gamma", "ln_beta")):
                        sp.dma_start(vec3[:, n], bcast(a[f"L0_ffn_{v}"])).then_inc(vec3_in, 16)
                    sp.dma_start(bias3, bcast(a["L0_ffn_fc2_bias"])).then_inc(bias3_in, 16)
                for k in range(BT):
                    sp.wait_ge(xg_ready, t * BT + k + 1)
                    sp.dma_start(xg_dram[bass.ds(t * TILE + k * P, P), :], xo[:, k]).then_inc(xg_out[k], 16)
                    if not final:
                        load_n(t + 2, slot, k)
                if not last:
                    for k in range(BT):
                        sp.wait_ge(xg_out[k], t * 16 + 16)
                        load_xo(t + 1, k)
                        if k == 1:
                            sp.wait_ge(w_ready, t * 2 + 2)
                            if final:
                                load_w2(0)
                            elif slot:
                                load_w1(u + 1, 0)
                            else:
                                load_w1(u, 2)

            load_w1(0, 0)
            with sp.Fori(0, NT // 2 - 1) as u:
                for slot in range(2):
                    tile2(u * 2 + slot, u, slot, False, False)
            for slot in range(2):
                tile2(NT - 2 + slot, NT // 2 - 1, slot, True, slot == 1)

            sp.wait_ge(p2_end, 1)
            for f in range(4, NF):
                if f > 4:
                    sp.wait_ge(codes_scaled, NT * 2 + f)
                if f > 5:
                    sp.wait_ge(w_ready, NT * 2 + f - 1)
                load_w2(f)
                if f == 5:
                    for k in range(BT):
                        sp.wait_ge(xg_out[k], NT * 16)
                    sp.dma_start(base[:, 1], blocks(xg_dram, 1)).then_inc(b_in[1], 16)

            def store_out(t, slot):
                for k in range(BT):
                    sp.wait_ge(o_free, t * BT + BT + k + 1)
                    sp.dma_start(out_dram[bass.ds(t * TILE + k * P, P), :], base[:, slot, k]).then_inc(
                        o_out[slot], 16)

            with sp.Fori(0, NT // 2 - 1) as u:
                for slot in range(2):
                    store_out(u * 2 + slot, slot)
                    sp.wait_ge(o_out[slot], u * 16 * BT + 16 * BT)
                    sp.dma_start(base[:, slot], blocks(xg_dram, u * 2 + slot + 2)).then_inc(b_in[slot], 16)
            for slot in range(2):
                store_out(NT - 2 + slot, slot)
            for slot in range(2):
                sp.wait_ge(o_out[slot], NT // 2 * 16 * BT)

        @block.tensor
        def _(pe):
            pe.sem_inc(pt_free, 2)
            pe.sem_inc(hid_free, 2)
            pe.wait_ge(consts, 3)

            def product(out, left, right, chunks, done=None, start=True, stop=True):
                for c in range(chunks):
                    for l, r in PASSES:
                        mm = nc.tensor.matmul(out, left(c, l), right(c, r),
                                              start=start and c == 0 and (l, r) == PASSES[0],
                                              stop=stop and c == chunks - 1 and (l, r) == PASSES[-1])
                if done is not None:
                    mm.then_inc(done, 1)
                return mm

            def turn(bank, block_of, inc=1):
                for c in range(C):
                    mm = nc.tensor.transpose(bank[:, c * P:(c + 1) * P], block_of(c), ident[:])
                mm.then_inc(tp_full, inc)

            def turn_weight(k0, slot):
                for j in range(C):
                    if k0 == 0:
                        pe.wait_ge(wq1_in[j], 16)
                    pe.wait_ge(tp_free, k0 + j + 1)
                    turn(PS[:, 2 + j % 2], lambda e: stage[:, slot, e, j * P:(j + 1) * P])

            turn_weight(0, 0)
            pe.wait_ge(stage_in[1], 16)
            turn_weight(C, 1)
            pe.wait_ge(stage_in[0], 16)
            turn_weight(2 * C, 0)
            pe.wait_ge(ctx_loaded, 16)
            for c in range(C):
                pe.wait_ge(tp_free, 3 * C + c + 1)
                for b in range(B):
                    mm = nc.tensor.transpose(PS[:, 2 + c % 2, b * SCP:b * SCP + SC],
                                             ctx_in[0:SC, b, c * P:(c + 1) * P], ident[0:SC, 0:SC])
                mm.then_inc(tp_full, 1)

            k = 0
            for m in range(C):
                pe.wait_ge(tp_free, 2 + 2 * C)
                pe.wait_ge(mm_free, k + 1)
                product(PS[:, 4 + k % 2], lambda j, h: wq1T[:, j, h, m * P:(m + 1) * P],
                        lambda j, h: wk1T[:, j, h, :], C, mm_full)
                k += 1
            pe.wait_ge(tp_free, 2 + TP0)
            for m in range(C):
                pe.wait_ge(split_lo, C)
                pe.wait_ge(mm_free, k + 1)
                product(PS[:, 4 + k % 2, 0:2 * SCP], lambda c, h: wk2[:, c, h, m * P:(m + 1) * P],
                        lambda c, h: ctxT[:, c, h, :], C, mm_full)
                k += 1
            for b in range(B):
                pe.wait_ge(split_lo, 2 * C)
                pe.wait_ge(mm_free, k + 1)
                product(PS[0:SC, 4 + k % 2], lambda c, h: ctxT[:, c, h, b * SCP:b * SCP + SC],
                        lambda c, h: wv2[:, c, h, :], C, mm_full)
                k += 1
            for m in range(C):
                pe.wait_ge(mm_free, max(2 + 2 * C, k + 1))
                product(PS[:, 4 + k % 2, 0:2 * SCP], lambda j, h: wq2T[:, j, h, m * P:(m + 1) * P],
                        lambda j, h: kT2[:, j, h, :], C, mm_full)
                k += 1

            with pe.Fori(0, B) as b:
                def turn_x(t):
                    pe.wait_ge(x_normed, b * NB + t + 1)
                    pe.wait_ge(tp_free, b * TP1 + TP0 + t + 1)
                    turn(PS[:, 2 + t % 2], lambda c: xn[:, t % 2, c * P:(c + 1) * P])

                def values(t):
                    if t == 0:
                        pe.wait_ge(wv_lo, b * C + C)
                    pe.wait_ge(tp_free, b * TP1 + 2 + TP0 + t + 1)
                    pe.wait_ge(mm_free, b * MM1 + MM0 + t + 1)
                    product(PS[:, 4 + t % 2], lambda c, h: xT[:, c, h, t * P:(t + 1) * P],
                            lambda c, h: wv[:, c, h, :], C, mm_full)

                def queries(g, m):
                    pe.wait_ge(mm_free, b * MM1 + MM0 + NB + g * C + m + 1)
                    product(PS[:, 4 + m % 2], lambda c, h: A[:, c, h, m * P:(m + 1) * P],
                            lambda c, h: xT[:, c, h, g * 512:(g + 1) * 512], C, mm_full)

                def score(k, q, lo, w):
                    pe.wait_ge(s_free, b * SS1 + k + 1)
                    product(PS[:, k % 2, 0:w], lambda m, h: QT[:, m, h, q * P:(q + 1) * P],
                            lambda m, h: xT[:, m, h, lo:lo + w], C, s_full)

                turn_x(0)
                for t in range(1, NB):
                    turn_x(t)
                    values(t - 1)
                values(NB - 1)
                for m in range(C):
                    queries(0, m)
                pe.wait_ge(mm_free, b * MM1 + 2 + MM0 + NB + C)
                for c in range(4):
                    score(c, 0, c * 512, 512)
                pe.wait_ge(s_free, b * SS1 + 5)
                pe.wait_ge(counted, b + 1)
                nc.tensor.matmul(PS[:, 0, 0:1], ones, keys_seen[0:1], start=True, stop=True).then_inc(
                    s_full, 2)

                for kind, i, c in ORDER:
                    if kind == "S":
                        if i % 4 == 0 and c == 0 and i:
                            pe.wait_ge(mm_free, b * MM1 + 2 + MM0 + NB + C * (i // 4 + 1))
                        score(6 + T_BEFORE[i] + c, i % 4, c * 512, width_of(i, c))
                    elif kind == "Q":
                        queries(i, c)
                    elif kind == "T":
                        k = NB + T_BEFORE[i] + c
                        if c == 0:
                            pe.wait_ge(p_ready, b * NB + i + 1)
                        pe.wait_ge(tp_free, b * TP1 + TP0 + k + 1)
                        for j in range(width_of(i, c) // P):
                            lo = c * 512 + j * P
                            mm = nc.tensor.transpose(PS[:, 2 + k % 2, j * P:(j + 1) * P],
                                                     Srow[:, i % 2, lo:lo + P], ident[:])
                        mm.then_inc(tp_full, 1)
                    elif kind == "V":
                        k = T_BEFORE[i] + c
                        if c == 0:
                            pe.wait_ge(z_free, b * NB + i + 1)
                        pe.wait_ge(tp_free, b * TP1 + 2 + TP0 + NB + k + 1)
                        n = width_of(i, c) // P
                        product(PS[:, 6 + i % 2], lambda j, h: PT[k % 2][:, h, j * P:(j + 1) * P],
                                lambda j, h: V[c * 4 + j][:, h, :], n, pt_free,
                                start=c == 0, stop=c == i // 4)

            pe.wait_ge(s_free, 2 + B * SS1)
            pe.wait_ge(mm_free, 2 + MM2)
            for b in range(B):
                pe.wait_ge(g_in[b], 16)
            pe.wait_ge(rows_lo, 1)
            for b in range(B):
                mm = product(PS[0:1, 0, b * SCP:(b + 1) * SCP], lambda c, h: rows_1[:, h, b, c:c + 1],
                             lambda c, h: G[:, b, c, h, :], C)
            mm.then_inc(c_full, 1)

            def count_lengths():
                pe.wait_ge(counted, B + 1)
                nc.tensor.matmul(PS[:, 1, 0:B], ones, keys_seen2[0:1], start=True, stop=True).then_inc(c_full, 1)

            def turn_x1(t, k):
                pe.wait_ge(x1b_in[k], t * 16 + 16)
                pe.wait_ge(tp_free, t * TPT + TP2 + k + 1)
                turn(PS[:, 2 + k % 2], lambda c: x1b[:, k, c * P:(c + 1) * P])

            def cross_scores(t, slot, half):
                if half == 0:
                    pe.wait_ge(g_in[slot], (t // 2) * 16 + 16 + 16 * slot)
                    pe.wait_ge(hf_ready, t * C + 1)
                pe.wait_ge(tp_free, t * TPT + 2 + TP2 + 2 * half + 2)
                tokens = slice(half * 256, half * 256 + 256)
                product(PS[0:SC, 0, tokens], lambda c, h: G[:, slot, c, h, 0:SC],
                        lambda c, h: x1T[:, c, h, tokens], C, st_full if half else None)

            def turn_scores(t):
                pe.wait_ge(st_copied, t + 1)
                pe.wait_ge(hf_ready, t * C + 2)
                pe.wait_ge(c_free, t + 1)
                for k in range(BT):
                    mm = nc.tensor.transpose(PS[:, 1, k * SCP:k * SCP + SC], ST[:, k * P:(k + 1) * P],
                                             ident[0:SC, 0:SC])
                mm.then_inc(c_full, 1)

            def turn_probs(t, slot):
                pe.wait_ge(e_ready, t + 1)
                pe.wait_ge(tp_free, t * TPT + TP2 + BT + 1)
                for k in range(BT):
                    mm = nc.tensor.transpose(PS[0:SC, 2, k * P:(k + 1) * P],
                                             S2[:, slot, k * SCP:k * SCP + SC], ident[:])
                mm.then_inc(tp_full, 2)

            def cross_values(t, k):
                if k == 0:
                    pe.wait_ge(tp_free, t * TPT + 2 + TP2 + BT + 2)
                pe.wait_ge(z_free, t * BT + B * NB + k + 1)
                product(PS[:, 6 + k % 2], lambda _, h: PT2[0:SC, h, k * P:(k + 1) * P],
                        lambda _, h: V2[0:SC, bass.ds(t // TPB, 1), h, :].rearrange("p a n -> p (a n)"),
                        1, z2_full)

            def turn_x2(t, slot, k):
                pe.wait_ge(x2_ready, t * BT + k + 1)
                pe.wait_ge(tp_free, t * TPT + TP2 + BT + 2 + k + 1)
                turn(PS[:, 2 + k % 2], lambda c: N[:, slot, k, c * P:(c + 1) * P])

            def mlp_in(t, half, f):
                if f == 0:
                    pe.wait_ge(tp_free, t * TPT + 2 + TP2 + BT + 2 + 2 * half + 2)
                if half == 0 and f > 1:
                    pe.wait_ge(y_free, t * BT + f + 1)
                tokens = slice(half * 256, half * 256 + 256)
                product(PS[:, HIDDEN[f], tokens], lambda c, h: fc1[:, c, h, f * P:(f + 1) * P],
                        lambda c, h: x2T[:, c, h, tokens], C, h_full if half else None)

            def mlp_out(t, k):
                if k == 0:
                    pe.wait_ge(h_lo, t * C + 2 + C)
                if k > 1:
                    pe.wait_ge(y_free, t * BT + 4 + k - 1)
                product(PS[:, 4 + k % 2], lambda f, h: hid2[:, f, h, k * P:(k + 1) * P],
                        lambda f, h: fc2[:, f, h, :], C, y_full)

            def turn_h(t, k):
                pe.wait_ge(hn_ready, t * BT + k + 1)
                pe.wait_ge(tp_free, t * BT + TP3 + k + 1)
                turn(PS[:, 2 + k % 2], lambda c: H0[:, k % 2, c * P:(c + 1) * P])

            def hidden(t, slot, turn_next=True):
                for f in range(C):
                    mlp_in(t, 0, f)
                    if f in (1, 2):
                        turn_x2(t, slot, f + 1)
                for f in range(C):
                    mlp_in(t, 1, f)
                    if turn_next and f < 2:
                        turn_x1(t + 1, f)
                if turn_next:
                    turn_x1(t + 1, 2)
                    turn_x1(t + 1, 3)
                    cross_scores(t + 1, 1 - slot, 0)
                    cross_scores(t + 1, 1 - slot, 1)

            turn_x1(0, 0)
            turn_x1(0, 1)
            count_lengths()
            turn_x1(0, 2)
            turn_x1(0, 3)
            pe.wait_ge(c_free, 1)
            cross_scores(0, 0, 0)
            cross_scores(0, 0, 1)
            pe.wait_ge(len_seen, 1)
            pe.wait_ge(cross_in, 16)
            turn_scores(0)
            turn_probs(0, 0)
            for k in range(BT):
                cross_values(0, k)
                if k > 1:
                    turn_x2(0, 0, k - 2)
            pe.wait_ge(fcw_lo, C)
            hidden(0, 0)
            pe.wait_ge(fcw_lo, 2 * C)

            def tile2(t, slot, final, last):
                if last:
                    for k in range(BT - 1):
                        mlp_out(t, k)
                    turn_h(0, 0)
                    turn_h(0, 1)
                    mlp_out(t, BT - 1)
                    turn_h(0, 2)
                    turn_h(0, 3)
                    return
                turn_scores(t + 1)
                mlp_out(t, 0)
                turn_probs(t + 1, 1 - slot)
                mlp_out(t, 1)
                cross_values(t + 1, 0)
                cross_values(t + 1, 1)
                mlp_out(t, 2)
                cross_values(t + 1, 2)
                turn_x2(t + 1, 1 - slot, 0)
                cross_values(t + 1, 3)
                turn_x2(t + 1, 1 - slot, 1)
                mlp_out(t, 3)
                hidden(t + 1, 1 - slot, not final)

            with pe.Fori(0, NT // 2 - 1) as u:
                for slot in range(2):
                    tile2(u * 2 + slot, slot, False, False)
            for slot in range(2):
                tile2(NT - 2 + slot, slot, True, slot == 1)

            def ffn_in(t, slot, f):
                if f == 0:
                    pe.wait_ge(tp_free, t * BT + 2 + TP3 + BT)
                pe.wait_ge(hf3_ready, t * NF + f + 1)
                product(PS[:, f % 2], lambda c, h: W1[c][:, h, f * P:(f + 1) * P],
                        lambda c, h: hT[:, slot * C + c, h, :], C, f_full)

            def ffn_out(t, f):
                pe.wait_ge(f_lo, t * NF + 2 + f + 1)
                pe.wait_ge(w_ready, NT * 2 + f + 1 - (2 if f < 2 else 0))
                for k in range(BT):
                    if f == 0:
                        pe.wait_ge(o_free, t * BT + k + 1)
                    mm = product(PS[:, 4 + k], lambda _, h: hid3[f % 2][:, h, k * P:(k + 1) * P],
                                 lambda _, h: W2[f][:, h, :], 1,
                                 o_full if f == NF - 1 and k < BT - 1 else None,
                                 start=f == 0, stop=f == NF - 1)
                mm.then_inc(hid_free, 1)

            pe.wait_ge(w_ready, NT * 2 - 2)
            ffn_in(0, 0, 0)

            def tile3(t, slot, first, last):
                for f in range(NF):
                    if f + 1 < NF:
                        ffn_in(t, slot, f + 1)
                    elif not last:
                        ffn_in(t + 1, 1 - slot, 0)
                    if first and f == 0:
                        pe.wait_ge(y_free, NT * BT + 4)
                    ffn_out(t, f)
                    if f in TURN_AT and not last:
                        turn_h(t + 1, TURN_AT.index(f))

            tiles(pe, tile3)

        @block.scalar
        def _(act):
            copy = ACT.Copy

            def hi(k, dst, src, turn=0, per=0, sems=(tp_full, tp_hi), inc=1):
                act.wait_ge(sems[0], turn * per + k + 1)
                nc.scalar.activation(dst, src, copy).then_inc(sems[1], inc)

            def quarters(bank):
                return bank.rearrange("p (c n) -> p c n", c=C)

            for k in range(3 * C):
                w = (wq1T, wk1T, wq2T)[k // C]
                hi(k, w[:, k % C, 0, :], PS[:, 2 + k % 2])
            for c in range(C):
                hi(3 * C + c, ctxT[:, c, 0, :].rearrange("p (b n) -> p b n", b=B)[:, :, 0:SC],
                   PS[:, 2 + c % 2, 0:2 * SCP].rearrange("p (b n) -> p b n", b=B)[:, :, 0:SC])

            def split_stage(slot, loaded, w, done):
                act.wait_ge(loaded[0], loaded[1])
                for c in range(C):
                    nc.scalar.activation(w[:, c, 0, :], stage[:, slot, c], copy).then_inc(done, 1)

            act.wait_ge(const_in, 16 * 6)
            nc.scalar.activation(gate_x, gate_x, ACT.Tanh).then_inc(gates_ready, 1)
            nc.scalar.activation(gate_f, gate_f, ACT.Tanh).then_inc(gates_ready, 1)
            nc.scalar.preload_act_table(ACT.Exp)
            split_stage(1, (stage_in[1], 32), wk2, split_hi)
            for m in range(C):
                hi(m, A[:, m, 0, :], PS[:, 4 + m % 2], sems=(mm_full, mm_hi))
            split_stage(0, (stage_in[0], 32), wv2, split_hi)
            for m in range(C):
                hi(C + m, kT2[:, m, 0, :], PS[:, 4 + m % 2, 0:2 * SCP], sems=(mm_full, mm_hi))
            for b in range(B):
                hi(2 * C + b, v_0[0:SC, b, 0, :], PS[0:SC, 4 + b % 2], sems=(mm_full, mm_hi))
            for m in range(C):
                hi(2 * C + B + m, g_0[:, :, m, 0, :], PS[:, 4 + m % 2, 0:2 * SCP].rearrange(
                    "p (b n) -> p b n", b=B), sems=(mm_full, mm_hi))

            with act.Fori(0, B) as b:
                def hi_x(t):
                    hi(TP0 + t, xT[:, :, 0, t * P:(t + 1) * P], quarters(PS[:, 2 + t % 2]), b, TP1)

                def hi_v(t):
                    hi(MM0 + t, V[t][:, 0, :], PS[:, 4 + t % 2], b, MM1, (mm_full, mm_hi))

                def hi_q(g, m):
                    hi(MM0 + NB + g * C + m, QT[:, m, 0, :], PS[:, 4 + m % 2], b, MM1, (mm_full, mm_hi))

                act.wait_ge(tp_full, b * TP1 + TP0)
                load_xa(act, b, 0)
                load_xa(act, b, 1)
                act.dma_start(stage[:, 0], a["L0_xattn_Wv1"].rearrange("(c p) n -> p c n", p=P)).then_inc(wv_in, 16)
                load_xa(act, b, 2)
                load_xa(act, b, 3)
                hi_x(0)
                act.wait_ge(wv_in, b * 16 + 16)
                for c in range(C):
                    nc.scalar.activation(wv[:, c, 0, :], stage[:, 0, c], copy).then_inc(wv_hi, 1)
                for t in range(1, NB):
                    hi_x(t)
                    if t == 5:
                        act.wait_ge(parked, 32)
                    hi_v(t - 1)
                hi_v(NB - 1)
                for m in range(C):
                    hi_q(0, m)
                for kind, i, c in ORDER:
                    if kind == "S" and c == i // 4:
                        w = i // 4 * 512 + width_of(i, i // 4)
                        act.wait_ge(mx_ready, b * NB + i + 1)
                        nc.scalar.activation(Srow[:, i % 2, 0:w], Srow[:, i % 2, 0:w], ACT.Exp,
                                             bias=nb[:, i % 2:i % 2 + 1], scale=SCALE,
                                             accum_out=rowsum[:, i % 4:i % 4 + 1]).then_inc(p_ready, 1)
                    elif kind == "Q":
                        hi_q(i, c)
                    elif kind == "T":
                        k, w = T_BEFORE[i] + c, width_of(i, c)
                        act.wait_ge(pt_free, b * PTK + k + 1)
                        hi(TP0 + NB + k, PT[k % 2][:, 0, 0:w], PS[:, 2 + k % 2, 0:w], b, TP1)

            act.wait_ge(s_free, 2 + B * SS1)
            act.wait_ge(parked, 32)
            for p in range(2):
                act.wait_ge(x1_out[p], 16 + 16 * (NB // 2) + 16)
            for b in range(B):
                act.dma_start(rows_in[:, b], x1_dram[b * S:b * S + 1, :].rearrange("a (c p) -> p (a c)", p=P),
                              allow_slow_non_contiguous=True).then_inc(rows_loaded, 16)
            for b in range(B):
                act.dma_start(G[:, b:b + 1].rearrange("p s c h n -> p s (c h n)").bitcast(F32),
                              g_dram[b:b + 1].rearrange("b p n -> p b n")).then_inc(g_in[b], 16)
            act.wait_ge(tp_full, TP2)

            def load_fc(n, w):
                act.dma_start(fc_stage[n], a[f"L0_xattn_{w}_w"].rearrange("(c p) n -> p c n", p=P)).then_inc(
                    fcw_in[n], 16)

            load_fc(0, "fc1")
            act.wait_ge(pt_free, 1 + B * PTK)
            act.wait_ge(rows_loaded, 32)
            nc.scalar.activation(rows_1[:, 0], rows_in, copy).then_inc(rows_hi, 1)
            act.wait_ge(pt_free, 2 + B * PTK)
            for k in range(BT):
                act.dma_start(x1b[:, k], x1_dram[k * P:(k + 1) * P, :]).then_inc(x1b_in[k], 16)
            act.dma_start(V2[0:SC].rearrange("p c h n -> p (c h n)").bitcast(F32), v_dram).then_inc(cross_in, 16)
            load_fc(1, "fc2")
            def split_fc(n, w):
                act.wait_ge(fcw_in[n], 16)
                for c in range(C):
                    nc.scalar.activation(w[:, c, 0, :], fc_stage[n][:, c], copy).then_inc(fcw_hi, 1)

            split_fc(0, fc1)

            def hi_x1(t, k):
                hi(TP2 + k, x1T[:, :, 0, k * P:(k + 1) * P], quarters(PS[:, 2 + k % 2]), t, TPT)

            def copy_st(t):
                act.wait_ge(st_full, t + 1)
                act.wait_ge(h_lo, t * C + 1)
                nc.scalar.activation(ST, PS[0:SC, 0], copy).then_inc(st_copied, 1)

            def probs(t, slot):
                act.wait_ge(sm_ready, t + 1)
                s = S2[:, slot, :].rearrange("p (k n) -> p k n", k=BT)[:, :, 0:SC]
                nc.scalar.activation(s, s, ACT.Exp, scale=SCALE).then_inc(e_ready, 1)

            def hi_p(t):
                hi(TP2 + BT + 1, PT2[0:SC, 0, :], PS[0:SC, 2], t, TPT, inc=2)

            def hi_x2(t, k):
                hi(TP2 + BT + 2 + k, x2T[:, :, 0, k * P:(k + 1) * P],
                   quarters(PS[:, 2 + k % 2]), t, TPT)

            act.sem_inc(hf_ready, C)
            for k in range(BT):
                hi_x1(0, k)
            copy_st(0)
            probs(0, 0)
            hi_p(0)
            split_fc(1, fc2)
            for k in range(BT):
                hi_x2(0, k)

            def hi_w(n, src, dst):
                act.wait_ge(codes_scaled, n + 1)
                nc.scalar.activation(dst[0], src, copy).then_inc(w_hi, 1)

            def hi_h(t, slot, k):
                hi(TP3 + k, hT[:, slot * C:(slot + 1) * C, 0, k * P:(k + 1) * P],
                   quarters(PS[:, 2 + k % 2]), t, BT)

            def hidden(t, turn_next=True):
                for f in range(C):
                    if turn_next and f < 2:
                        hi_x1(t + 1, f)
                    if turn_next and f == 2:
                        hi_x1(t + 1, 2)
                    act.wait_ge(h_full, t * C + f + 1)
                    act.wait_ge(h_lo, t * C + f + 1)
                    nc.scalar.activation(HF2[:, f % 2], PS[:, HIDDEN[f]], ACT.Relu,
                                         bias=b1x[:, f:f + 1]).then_inc(hf_ready, 1)
                    if turn_next and f == 2:
                        hi_x1(t + 1, 3)
                    act.wait_ge(hf_ready, t * C + C + f + 1)
                    nc.scalar.activation(hid2[:, f, 0, :], HF2[:, f % 2], copy).then_inc(h_hi, 1)

            hidden(0)

            def tile2(t, u, slot, final, last):
                if not last:
                    copy_st(t + 1)
                    probs(t + 1, 1 - slot)
                    hi_p(t + 1)
                    hi_x2(t + 1, 0)
                    hi_x2(t + 1, 1)
                    hi_x2(t + 1, 2)
                    hi_x2(t + 1, 3)
                    hi_w(t * 2, q1, w1_unit(u, slot * 2))
                    hidden(t + 1, not final)
                    hi_w(t * 2 + 1, q1, w1_unit(u, slot * 2 + 1))
                    return
                nc.scalar.preload_act_table(ACT.Silu)
                act.sem_inc(hf3_ready, 2)
                hi_w(t * 2, q1, LAST_UNITS[0])
                hi_h(0, 0, 0)
                hi_h(0, 0, 1)
                hi_h(0, 0, 2)
                hi_w(t * 2 + 1, q1, LAST_UNITS[1])
                hi_h(0, 0, 3)
                hi_w(t * 2 + 2, q1, LAST_UNITS[2])

            with act.Fori(0, NT // 2 - 1) as u:
                for slot in range(2):
                    tile2(u * 2 + slot, u, slot, False, False)
            for slot in range(2):
                tile2(NT - 2 + slot, NT // 2 - 1, slot, True, slot == 1)

            def tile3(t, slot, first, last):
                for f in range(NF):
                    act.wait_ge(f_full, t * NF + f + 1)
                    act.wait_ge(f_lo, t * NF + f + 1)
                    nc.scalar.activation(HF3[:, f % 2], PS[:, f % 2], ACT.Silu,
                                         bias=b1f[:, f:f + 1]).then_inc(hf3_ready, 1)
                    act.wait_ge(hf3_ready, t * NF + 2 + f + 1)
                    if first and f == 1:
                        act.wait_ge(w_ready, NT * 2 + 2)
                    act.wait_ge(hid_free, t * NF + f + 1)
                    nc.scalar.activation(hid3[f % 2][:, 0, :], HF3[:, f % 2], copy).then_inc(f_hi, 1)
                    if first and f == 0:
                        hi_w(NT * 2 + 1, q1, LAST_UNITS[3])
                    if first and 0 < f and f + 1 < NF:
                        hi_w(NT * 2 + f + 1, w2_stage(f + 1)[0], w2_unit(f + 1))
                    if f in TURN_AT and not last:
                        hi_h(t + 1, 1 - slot, TURN_AT.index(f))

            tiles(act, tile3)

        @block.gpsimd
        def _(pool):
            nc.gpsimd.memset(ident[:], 0.0).then_inc(made, 1)
            nc.gpsimd.memset(tri[:], 0.0).then_inc(made, 1)
            nc.gpsimd.memset(half, -0.5)
            nc.gpsimd.memset(eps_col, EPS).then_inc(made, 1)
            pool.wait_ge(made, 3)
            nc.gpsimd.affine_select(out=ident[:], in_=ident[:], compare_op=ALU.not_equal, fill=1.0, base=0,
                                    pattern=[[-1, P]], channel_multiplier=1).then_inc(consts, 1)
            nc.gpsimd.affine_select(out=tri[:], in_=tri[:], compare_op=ALU.is_ge, fill=-BIG, base=0,
                                    pattern=[[-1, P]], channel_multiplier=1).then_inc(consts, 1)
            nc.gpsimd.iota(keys[:], [[1, 512]], base=0, channel_multiplier=0).then_inc(consts, 1)

            def rstd(n, var, out, turn=0, per=0):
                pool.wait_ge(var_ready, turn * per + n + 1)
                nc.gpsimd.tensor_tensor(out, var, eps_col.to_broadcast(list(out.shape)), ALU.add).then_inc(eps_added, 1)
                pool.wait_ge(eps_added, turn * per + n + 1)
                nc.gpsimd.tensor_tensor(out, out, half.to_broadcast(list(out.shape)), ALU.pow).then_inc(
                    rstd_ready, 1)

            with pool.Fori(0, B) as b:
                for t in range(NB):
                    rstd(t, mv1[:, t, 1:2], rs1[:, t:t + 1], b, 2 * NB)
                for i in range(NB):
                    rstd(NB + i, mvE[:, i % 2, 1:2], rsE[:, i % 2:i % 2 + 1], b, 2 * NB)

            pool.wait_ge(rows_hi, 1)
            nc.gpsimd.tensor_tensor(rows_1[:, 1], rows_in, rows_1[:, 0].bitcast(F32), ALU.subtract).then_inc(
                rows_lo, 1)
            R2 = 2 * NB * B

            def norm_z(t, k):
                rstd(R2 + BT + k, mvZ[:, k, 1:2], rsZ[:, k:k + 1], t, 2 * BT)

            def norm_y(t, k):
                rstd(R2 + BT + BT + k, mvE[:, k, 1:2], rsE[:, k:k + 1], t, 2 * BT)

            def lo_hid(t, f):
                pool.wait_ge(h_hi, t * C + f + 1)
                nc.gpsimd.tensor_tensor(hid2[:, f, 1, :], HF2[:, f % 2], hid2[:, f, 0, :].bitcast(F32),
                                        ALU.subtract).then_inc(h_lo, 1)

            def lo_w(n, dst):
                pool.wait_ge(w_hi, n + 1)
                nc.gpsimd.tensor_tensor(dst[1], q1, dst[0].bitcast(F32), ALU.subtract).then_inc(w_ready, 1)

            def bias_x2(t, slot, k):
                pool.wait_ge(tp_full, t * TPT + TP2 + BT + 2 + k + 1)
                nc.gpsimd.tensor_tensor(N[:, slot, k], N[:, slot, k], vec2[:, 4], ALU.add).then_inc(x2_biased, 1)

            def bias_xo(t, k):
                pool.wait_ge(xo_in[k], t * 16 + 16)
                nc.gpsimd.tensor_tensor(xo[:, k], xo[:, k], vec2[:, 3], ALU.add).then_inc(xo_ready, 1)

            for k in range(BT):
                rstd(R2 + k, mvZ[:, k, 1:2], rsZ[:, k:k + 1])

            R3 = R2 + NT * 2 * BT

            def rstd_of_x(t):
                rstd(R3, mvX[:, :, 1], rs_x, t, 1 + BT)

            def rstd_of_h0(t, k):
                rstd(R3 + 1 + k, mvH[:, k, 1:2], rsH[:, k:k + 1], t, 1 + BT)

            def tile2(t, u, slot, final, last):
                first = R2 + BT + (NT - 1) * 2 * BT

                def norm_h0(k):
                    rstd(first + 1 + k, mvH[:, k, 1:2], rsH[:, k:k + 1])

                if last:
                    bias_xo(t, 0)
                    bias_xo(t, 1)
                    norm_h0(2)
                    norm_h0(3)
                    bias_xo(t, 2)
                    bias_xo(t, 3)
                    for k in range(BT):
                        rstd(first + 1 + BT + k, mvE[:, k, 1:2], rsE[:, k:k + 1])
                    return
                norm_z(t, 0)
                bias_xo(t, 0)
                norm_z(t, 1)
                bias_xo(t, 1)
                norm_z(t, 2)
                norm_z(t, 3)
                norm_y(t, 0)
                bias_xo(t, 2)
                norm_y(t, 1)
                lo_w(t * 2, w1_unit(u, slot * 2))
                for f in range(C):
                    lo_hid(t + 1, f)
                    if f == 1:
                        bias_xo(t, 3)
                norm_y(t, 2)
                norm_y(t, 3)
                if final:
                    rstd(first, mvX[:, :, 1], rs_x)
                    lo_w(t * 2 + 1, w1_unit(u, slot * 2 + 1))
                for k in range(2):
                    bias_x2(t + 1, 1 - slot, k)
                    if final:
                        norm_h0(k)
                if not final:
                    lo_w(t * 2 + 1, w1_unit(u, slot * 2 + 1))
                bias_x2(t + 1, 1 - slot, 2)
                bias_x2(t + 1, 1 - slot, 3)

            pool.wait_ge(vec2_ready, 2)
            for k in range(BT):
                lo_hid(0, k)
                bias_x2(0, 0, k)
            with pool.Fori(0, NT // 2 - 1) as u:
                for slot in range(2):
                    tile2(u * 2 + slot, u, slot, False, False)
            for slot in range(2):
                tile2(NT - 2 + slot, NT // 2 - 1, slot, True, slot == 1)

            pool.wait_ge(bias3_ready, 1)
            for k in range(BT):
                pool.wait_ge(hn_ready, k + 1)
                nc.gpsimd.tensor_tensor(base[:, 0, k], base[:, 0, k], bias3, ALU.add).then_inc(base_biased, 1)
            with pool.Fori(1, NT) as t:
                rstd_of_x(t)
                for k in range(BT):
                    rstd_of_h0(t, k)

        @block.vector
        def _(dve):
            for s, n in ((tp_free, 2), (mm_free, 2), (s_free, 2), (z_free, 2), (y_free, 4), (h_lo, 2),
                         (f_lo, 2), (o_free, 4)):
                dve.sem_inc(s, n)

            def lo(k, dst, src, hi_part, turn=0, per=0, sems=(tp_hi, tp_free), inc=1):
                dve.wait_ge(sems[0], turn * per + k + 1)
                nc.vector.tensor_tensor(dst, src, hi_part.bitcast(F32), ALU.subtract).then_inc(sems[1], inc)

            def quarters(bank):
                return bank.rearrange("p (c n) -> p c n", c=C)

            def apart():
                dve.sem_inc(waited, 1)

            p0 = Steps(dve, dve_p0)
            for at in (SC, SCP + SC):
                p0.done(nc.vector.memset(ctxT[:, :, :, at:at + SCP - SC].bitcast(F32), 0.0))
            p0.done(nc.vector.memset(ones, 1.0))
            dve.wait_ge(consts, 3)

            for k in range(3 * C):
                w = (wq1T, wk1T, wq2T)[k // C]
                lo(k, w[:, k % C, 1, :], PS[:, 2 + k % 2], w[:, k % C, 0, :])
            for c in range(C):
                halves = [ctxT[:, c, h, :].rearrange("p (b n) -> p b n", b=B)[:, :, 0:SC] for h in range(2)]
                lo(3 * C + c, halves[1],
                   PS[:, 2 + c % 2, 0:2 * SCP].rearrange("p (b n) -> p b n", b=B)[:, :, 0:SC], halves[0])

            def split_stage(slot, w, his, n0, done):
                for c in range(C):
                    dve.wait_ge(his, n0 + c + 1)
                    nc.vector.tensor_tensor(w[:, c, 1, :], stage[:, slot, c], w[:, c, 0, :].bitcast(F32),
                                            ALU.subtract).then_inc(done, 1)

            mm = (mm_hi, mm_free)
            split_stage(1, wk2, split_hi, 0, split_lo)
            for m in range(C):
                lo(m, A[:, m, 1, :], PS[:, 4 + m % 2], A[:, m, 0, :], sems=mm)
            split_stage(0, wv2, split_hi, C, split_lo)
            for m in range(C):
                lo(C + m, kT2[:, m, 1, :], PS[:, 4 + m % 2, 0:2 * SCP], kT2[:, m, 0, :], sems=mm)
            for b in range(B):
                lo(2 * C + b, v_0[0:SC, b, 1, :], PS[0:SC, 4 + b % 2], v_0[0:SC, b, 0, :], sems=mm)
            for m in range(C):
                lo(2 * C + B + m, g_0[:, :, m, 1, :], PS[:, 4 + m % 2, 0:2 * SCP].rearrange(
                    "p (b n) -> p b n", b=B), g_0[:, :, m, 0, :], sems=mm)
            dve.wait_ge(gates_ready, 2)
            p0.link(nc.vector.tensor_scalar(gf_half, gate_f, 0.5, None, ALU.mult))

            def statistics(steps, x, mv, k):
                steps.link(nc.vector.bn_stats(st[:, k % 2], x))
                apart()
                nc.vector.bn_aggr(mv, st[:, k % 2]).then_inc(var_ready, 1)

            def scale_shift(steps, x, mean, rs, g, b, done):
                steps.link(nc.vector.scalar_tensor_tensor(out=x, in0=x, scalar=mean, in1=g,
                                                          op0=ALU.subtract, op1=ALU.mult))
                nc.vector.scalar_tensor_tensor(out=x, in0=x, scalar=rs, in1=b,
                                               op0=ALU.mult, op1=ALU.add).then_inc(done, 1)

            with dve.Fori(0, B) as b:
                p1 = Steps(dve, dve_p1, DVE1, b)

                def stats_x(t):
                    dve.wait_ge(xa_in[t % 4], b * NB * 4 + (t // 4 + 1) * 16)
                    statistics(p1, xa[:, t % 4], mv1[:, t], t)

                def norm_x(t):
                    dve.wait_ge(rstd_ready, b * 2 * NB + t + 1)
                    dve.wait_ge(tp_full, b * TP1 + TP0 + max(t - 1, 0))
                    nc.vector.tensor_scalar(xn[:, t % 2], xa[:, t % 4], mv1[:, t, 0:1], rs1[:, t:t + 1],
                                            ALU.subtract, ALU.mult).then_inc(x_normed, 1)

                def lo_x(t):
                    halves = [xT[:, :, h, t * P:(t + 1) * P] for h in range(2)]
                    lo(TP0 + t, halves[1], quarters(PS[:, 2 + t % 2]), halves[0], b, TP1)

                def lo_v(t):
                    lo(MM0 + t, V[t][:, 1, :], PS[:, 4 + t % 2], V[t][:, 0, :], b, MM1, mm)

                def lo_q(g, m):
                    lo(MM0 + NB + g * C + m, QT[:, m, 1, :], PS[:, 4 + m % 2], QT[:, m, 0, :], b, MM1, mm)

                stats_x(0)
                for t in range(NB + 2):
                    if t + 1 < NB:
                        stats_x(t + 1)
                    if t < NB:
                        norm_x(t)
                    if 1 <= t <= NB:
                        lo_x(t - 1)
                    if t == 1:
                        for c in range(C):
                            dve.wait_ge(wv_hi, b * C + c + 1)
                            nc.vector.tensor_tensor(wv[:, c, 1, :], stage[:, 0, c],
                                                    wv[:, c, 0, :].bitcast(F32),
                                                    ALU.subtract).then_inc(wv_lo, 1)
                    if t >= 2:
                        lo_v(t - 2)
                for m in range(C):
                    lo_q(0, m)
                for c in range(4):
                    dve.wait_ge(s_full, b * SS1 + c + 1)
                    if c > 1:
                        dve.wait_ge(s_free, b * SS1 + 2 + c - 1)
                    nc.vector.tensor_scalar(xn[0:1, c % 2], PS[0:1, c % 2], 0.0, None, ALU.not_equal, ALU.add,
                                            accum_out=cnt[0:1, c:c + 1]).then_inc(s_free, 1)
                dve.wait_ge(s_free, b * SS1 + 2 + 4)
                nc.vector.tensor_reduce(keys_seen[0:1], cnt[0:1], AX.X, ALU.add).then_inc(counted, 1)
                dve.wait_ge(s_full, b * SS1 + 6)
                for c in range(4):
                    ins = nc.vector.tensor_scalar(lnc[:, c:c + 1], PS[:, 0, 0:1], -512.0 * c, None, ALU.add)
                    if c < 3:
                        p1.done(ins)
                ins.then_inc(s_free, 2)
                dve.wait_ge(s_free, b * SS1 + 2 + 6)
                for c in range(4):
                    last = p1.done(nc.vector.tensor_scalar(pad[:, c * 512:(c + 1) * 512], keys[:],
                                                           lnc[:, c:c + 1], -BIG, ALU.is_ge, ALU.mult))
                p1.wait(last)
                p1.link(nc.vector.reciprocal(ln, lnc[:, 0:1]))
                p1.link(nc.vector.tensor_scalar(ln, ln, 0.0, None, ALU.mult))
                p1.link(nc.vector.tensor_scalar(pad, pad, ln, None, ALU.add))

                def scores(i, c):
                    k, w, at = 6 + T_BEFORE[i] + c, width_of(i, c), c * 512
                    bank, row = PS[:, k % 2], Srow[:, i % 2]
                    dve.wait_ge(s_full, b * SS1 + k + 1)
                    if c == 0:
                        dve.wait_ge(tp_full, b * TP1 + TP0 + (NB + T_BEFORE[i - 1] if i > 1 else 0))

                    def masked_max(lo_, n, src, m):
                        apart()
                        return nc.vector.tensor_tensor_reduce(
                            out=row[:, at + lo_:at + lo_ + n], in0=src, in1=pad[:, at + lo_:at + lo_ + n],
                            scale=1.0, scalar=-3.4e38, op0=ALU.add, op1=ALU.max, accum_out=mx[:, i % 2, m:m + 1])

                    if c < i // 4:
                        masked_max(0, w, bank[:, 0:w], c).then_inc(s_free, 1)
                        return
                    d = w - P
                    if d:
                        p1.done(masked_max(0, d, bank[:, 0:d], c))
                    nc.vector.tensor_tensor(row[:, at + d:at + w], bank[:, d:w], tri[:], ALU.add).then_inc(
                        s_free, 1)
                    dve.wait_ge(s_free, b * SS1 + 2 + k + 1)
                    n = c + (2 if d else 1)
                    p1.link(masked_max(d, P, row[:, at + d:at + w], n - 1))
                    p1.link(nc.vector.tensor_reduce(nmx[:, 0:1], mx[:, i % 2, 0:n], AX.X, ALU.max))
                    nc.vector.tensor_scalar(nb[:, i % 2:i % 2 + 1], nmx[:, 0:1], -SCALE, None,
                                            ALU.mult).then_inc(mx_ready, 1)

                def end_a(i):
                    dve.wait_ge(x_in[i % 2], b * NB * 8 + (i // 2 + 1) * 16)
                    p1.done(nc.vector.tensor_scalar(xin[:, i % 2], xin[:, i % 2], mv1[:, i, 0:1],
                                                    rs1[:, i:i + 1], ALU.subtract, ALU.mult))
                    p1.link(nc.vector.reciprocal(rcp[:, i % 2:i % 2 + 1], rowsum[:, i % 4:i % 4 + 1]))
                    dve.wait_ge(x1_out[i % 2], b * NB * 8 + (i // 2 + 1) * 16)
                    dve.wait_ge(pt_free, b * PTK + 2 + T_BEFORE[i + 1])
                    nc.vector.scalar_tensor_tensor(out=U[:, i % 2], in0=PS[:, 6 + i % 2],
                                                   scalar=rcp[:, i % 2:i % 2 + 1], in1=xin[:, i % 2],
                                                   op0=ALU.mult, op1=ALU.add).then_inc(z_free, 1)
                    dve.wait_ge(z_free, b * NB + 2 + i + 1)
                    statistics(p1, U[:, i % 2], mvE[:, i % 2], i)

                def end_b(i):
                    dve.wait_ge(rstd_ready, b * 2 * NB + NB + i + 1)
                    scale_shift(p1, U[:, i % 2], mvE[:, i % 2, 0:1], rsE[:, i % 2:i % 2 + 1],
                                ln1[:, 0], ln1[:, 1], x1_ready)

                for kind, i, c in ORDER:
                    if kind == "S":
                        scores(i, c)
                    elif kind == "Q":
                        lo_q(i, c)
                    elif kind == "T":
                        k, w = T_BEFORE[i] + c, width_of(i, c)
                        lo(TP0 + NB + k, PT[k % 2][:, 1, 0:w], PS[:, 2 + k % 2, 0:w],
                           PT[k % 2][:, 0, 0:w], b, TP1)
                    elif kind == "A":
                        end_a(i)
                    elif kind == "B":
                        end_b(i)
            assert p1.n == DVE1

            R2 = 2 * NB * B

            def lo_t(k, dst, k_bank, turn=0, per=0):
                lo(k, dst[1], quarters(PS[:, 2 + k_bank % 2]), dst[0], turn, per)

            def lo_x1(t, k):
                lo_t(TP2 + k, [x1T[:, :, h, k * P:(k + 1) * P] for h in range(2)], k, t, TPT)

            def split_fc(n, w):
                for c in range(C):
                    dve.wait_ge(fcw_hi, n * C + c + 1)
                    nc.vector.tensor_tensor(w[:, c, 1, :], fc_stage[n][:, c], w[:, c, 0, :].bitcast(F32),
                                            ALU.subtract).then_inc(fcw_lo, 1)

            dve.wait_ge(c_full, 1)
            for b in range(B):
                ins = nc.vector.tensor_scalar(S2[0:1, b, 0:SC], PS[0:1, 0, b * SCP:b * SCP + SC], 0.0, None,
                                              ALU.not_equal, ALU.add, accum_out=keys_seen2[0:1, b:b + 1])
                if b == 0:
                    p0.done(ins)
            ins.then_inc(c_free, 1)
            dve.wait_ge(c_free, 1)
            p0.wait()
            nc.vector.tensor_copy(sum2[0:1, 0:1], keys_seen2[0:1, 0:1]).then_inc(counted, 1)
            split_fc(0, fc1)
            lo_x1(0, 0)
            lo_x1(0, 1)
            dve.wait_ge(c_full, 2)
            p0.link(nc.vector.tensor_copy(len2, PS[:, 1, 0:B]))
            for b in range(B):
                p0.done(nc.vector.tensor_scalar(mask2[:, b], keys[:, 0:SC], len2[:, b:b + 1], -BIG,
                                                ALU.is_ge, ALU.mult))
            p0.wait()
            p0.link(nc.vector.reciprocal(rc2[:, 0:B], len2))
            p0.link(nc.vector.tensor_scalar(rc2[:, 0:B], rc2[:, 0:B], 0.0, None, ALU.mult))
            p0.link(nc.vector.tensor_tensor(mask2[:], mask2[:],
                                            rc2[:, 0:B].unsqueeze(2).to_broadcast([P, B, SC]), ALU.add))
            nc.vector.tensor_copy(sum2[:, 0:1], len2[:, 0:1]).then_inc(len_seen, 1)

            def rows(slot):
                return S2[:, slot, :].rearrange("p (k n) -> p k n", k=BT)[:, :, 0:SC]

            def softmax(steps, t, slot):
                s = rows(slot)
                dve.wait_ge(c_full, t + 3)
                bank = PS[:, 1, 0:BT * SCP].rearrange("p (k n) -> p k n", k=BT)[:, :, 0:SC]
                m = mask2[:, bass.ds(t // TPB, 1), :].to_broadcast([P, BT, SC])
                nc.vector.tensor_tensor(s, bank, m, ALU.add).then_inc(c_free, 1)
                dve.wait_ge(c_free, t + 2)
                steps.link(nc.vector.tensor_reduce(mx2, s, AX.X, ALU.max))
                nc.vector.tensor_tensor(s, s, mx2.unsqueeze(2).to_broadcast([P, BT, SC]),
                                        ALU.subtract).then_inc(sm_ready, 1)

            def sum_probs(steps, t, slot):
                dve.wait_ge(e_ready, t + 1)
                steps.link(nc.vector.tensor_reduce(sum2, rows(slot), AX.X, ALU.add))
                steps.link(nc.vector.reciprocal(rc2, sum2))

            def lo_probs(t):
                lo(TP2 + BT + 1, PT2[0:SC, 1, :], PS[0:SC, 2], PT2[0:SC, 0, :], t, TPT, inc=2)

            def add_z(t, slot, k):
                x = N[:, slot, k]
                dve.wait_ge(n_in[slot][k], (t // 2) * 16 + 16)
                dve.wait_ge(z2_full, t * BT + k + 1)
                nc.vector.scalar_tensor_tensor(out=x, in0=PS[:, 6 + k % 2], scalar=rc2[:, k:k + 1], in1=x,
                                               op0=ALU.mult, op1=ALU.add).then_inc(z_free, 1)

            def norm_stats(steps, x, k):
                return steps.done(nc.vector.bn_stats(st[:, k % 2], x))

            def norm_mean(steps, at, mv, k):
                steps.wait(at)
                apart()
                nc.vector.bn_aggr(mv[:, k], st[:, k % 2]).then_inc(var_ready, 1)

            def norm_scale(steps, x, mv, k, g, n):
                dve.wait_ge(var_ready, n)
                return steps.done(nc.vector.scalar_tensor_tensor(out=x, in0=x, scalar=mv[:, k, 0:1], in1=g,
                                                                 op0=ALU.subtract, op1=ALU.mult))

            def norm_shift(steps, at, out, x, rs, k, b, n, done):
                steps.wait(at)
                dve.wait_ge(rstd_ready, n)
                nc.vector.scalar_tensor_tensor(out=out, in0=x, scalar=rs[:, k:k + 1], in1=b,
                                               op0=ALU.mult, op1=ALU.add).then_inc(done, 1)

            def norms_z(steps, t, slot, n0, a, between):
                def stats(k):
                    dve.wait_ge(z_free, t * BT + 2 + B * NB + k + 1)
                    return norm_stats(steps, N[:, slot, k], k)

                def scale(k):
                    return norm_scale(steps, N[:, slot, k], mvZ, k, vec2[:, 0], n0 + k + 1)

                def shift(k, at):
                    x = N[:, slot, k]
                    norm_shift(steps, at, x, x, rsZ, k, vec2[:, 1], n0 + k + 1, x2_ready)

                c = a + 1
                add_z(t, slot, a)
                sa = stats(a)
                between(0)
                add_z(t, slot, c)
                norm_mean(steps, sa, mvZ, a)
                sc = stats(c)
                ga = scale(a)
                norm_mean(steps, sc, mvZ, c)
                shift(a, ga)
                between(1)
                gc = scale(c)
                shift(c, gc)

            def lo_x2(t, k):
                lo_t(TP2 + BT + 2 + k, [x2T[:, :, h, k * P:(k + 1) * P] for h in range(2)], k, t, TPT)

            lo_x1(0, 2)
            lo_x1(0, 3)
            softmax(p0, 0, 0)
            sum_probs(p0, 0, 0)
            lo_probs(0)
            dve.wait_ge(vec2_in, 16 * 5)
            for n in (2, 3):
                nc.vector.tensor_scalar(vec2[:, n], vec2[:, n], gate_x, None, ALU.mult).then_inc(vec2_ready, 1)
            dve.wait_ge(vec2_ready, 2)
            norms_z(p0, 0, 0, R2, 0, lambda _: None)
            lo_x2(0, 0)
            norms_z(p0, 0, 0, R2, 2, lambda n: n or lo_x2(0, 1))
            lo_x2(0, 2)
            lo_x2(0, 3)
            split_fc(1, fc2)
            for k in range(BT):
                lo_x1(1, k)

            def scale_codes(q, sc, *loads):
                for sem_, v in loads:
                    dve.wait_ge(sem_, v)
                nc.vector.scalar_tensor_tensor(out=q, in0=q.bitcast(I32), scalar=-128.0, in1=sc,
                                               op0=ALU.add, op1=ALU.mult).then_inc(codes_scaled, 1)

            def lo_w(n, src, dst):
                dve.wait_ge(w_hi, n + 1)
                nc.vector.tensor_tensor(dst[1], src, dst[0].bitcast(F32), ALU.subtract).then_inc(w_ready, 1)

            def tile2(t, slot, final, last):
                p2 = Steps(dve, dve_p2, DVE2, t)

                def scale_w(n):
                    scale_codes(q1, sc1, (q1_in, t * 64 + 32 * n + 32))

                def add_y(k):
                    x = N[:, slot, k]
                    dve.wait_ge(y_full, t * BT + k + 1)
                    dve.wait_ge(x2_biased, t * BT + k + 1)
                    nc.vector.tensor_tensor(x, PS[:, 4 + k % 2], x, ALU.add).then_inc(y_free, 1)

                def begin(k):
                    return norm_stats(p2, N[:, slot, k], k)

                def mean(k, at):
                    norm_mean(p2, at, mvE, k)

                def scale(k, n):
                    return norm_scale(p2, N[:, slot, k], mvE, k, vec2[:, 2], n)

                def shift(k, at, n):
                    dve.wait_ge(xo_ready, t * BT + k + 1)
                    norm_shift(p2, at, xo[:, k], N[:, slot, k], rsE, k, xo[:, k], n, xg_ready)

                n0 = t * 2 * BT + R2 + BT
                if not last:
                    def lx1(k):
                        if not final:
                            lo_x1(t + 2, k)

                    ny = n0 + BT + 1
                    softmax(p2, t + 1, 1 - slot)
                    sum_probs(p2, t + 1, 1 - slot)
                    add_y(0)
                    lo_probs(t + 1)
                    add_y(1)
                    norms_z(p2, t + 1, 1 - slot, n0, 0, lambda _: None)
                    lo_x2(t + 1, 0)
                    norms_z(p2, t + 1, 1 - slot, n0, 2, lambda n: add_y(2) if n else lo_x2(t + 1, 1))
                    add_y(3)
                    lo_x2(t + 1, 2)
                    dve.wait_ge(y_free, t * BT + 4 + BT)
                    s0 = begin(0)
                    lo_x2(t + 1, 3)
                    mean(0, s0)
                    s1 = begin(1)
                    scale_w(0)
                    mean(1, s1)
                    g0 = scale(0, ny)
                    lx1(0)
                    shift(0, g0, ny)
                    s2 = begin(2)
                    g1 = scale(1, ny + 1)
                    mean(2, s2)
                    shift(1, g1, ny + 1)
                    lx1(1)
                    s3 = begin(3)
                    lx1(2)
                    mean(3, s3)
                    lx1(3)
                    if final:
                        stats_x3(p0, x1b, (x1b_in[0], NT * 16 + 16), (var_ready, ny + 3))
                    scale_w(1)
                    g2 = scale(2, ny + 2)
                    g3 = scale(3, ny + 3)
                    shift(2, g2, ny + 2)
                    shift(3, g3, ny + 3)
                    assert p2.n == DVE2, p2.n
                    return

                def finish(n):
                    lo_w(t * 2 + n, q1, LAST_UNITS[n])

                def h0(k):
                    return make_h0(p2, 0, k, x1b[:, k])

                ny = n0 + BT + 2
                dve.wait_ge(rstd_ready, n0 + 1)
                dve.wait_ge(vec3_in, 32)
                h0(0)
                a0 = h0(1)
                s0 = h0_stats(p2, 0, a0)
                norm_mean(p2, s0, mvH, 0)
                s1 = h0_stats(p2, 1, a0)
                dve.wait_ge(xg_ready, t * BT)
                g0 = h_scale(p2, 0, 0, x1b[:, 0], n0 + 2)
                norm_mean(p2, s1, mvH, 1)
                add_y(0)
                h_shift(p2, 0, g0, n0 + 2)
                scale_w(0)
                g1 = h_scale(p2, 0, 1, x1b[:, 1], n0 + 3)
                add_y(1)
                h_shift(p2, 1, g1, n0 + 3)
                a2 = h0(2)
                s2 = h0_stats(p2, 2, a2)
                lo_h(0, 0, 0)
                norm_mean(p2, s2, mvH, 2)
                g2 = h_scale(p2, 0, 2, x1b[:, 2], n0 + 4)
                finish(0)
                h_shift(p2, 2, g2, n0 + 4)
                a3 = h0(3)
                s3 = h0_stats(p2, 3, a3)
                lo_h(0, 0, 1)
                norm_mean(p2, s3, mvH, 3)
                g3 = h_scale(p2, 0, 3, x1b[:, 3], n0 + 5)
                scale_w(1)
                h_shift(p2, 3, g3, n0 + 5)
                lo_h(0, 0, 2)
                add_y(2)
                finish(1)
                add_y(3)
                dve.wait_ge(y_free, NT * BT + 4)
                s0 = begin(0)
                lo_h(0, 0, 3)
                mean(0, s0)
                s1 = begin(1)
                scale_w(2)
                mean(1, s1)
                g0 = scale(0, ny)
                s2 = begin(2)
                finish(2)
                shift(0, g0, ny)
                g1 = scale(1, ny + 1)
                mean(2, s2)
                s3 = begin(3)
                shift(1, g1, ny + 1)
                mean(3, s3)
                lo_hid3(0, 0)
                scale_w(3)
                g2 = scale(2, ny + 2)
                g3 = scale(3, ny + 3)
                finish(3)
                shift(2, g2, ny + 2)
                shift(3, g3, ny + 3)

            def lo_hid3(t, f):
                dve.wait_ge(f_hi, t * NF + f + 1)
                nc.vector.tensor_tensor(hid3[f % 2][:, 1, :], HF3[:, f % 2],
                                        hid3[f % 2][:, 0, :].bitcast(F32), ALU.subtract).then_inc(f_lo, 1)

            R3 = R2 + NT * 2 * BT

            def stats_x3(steps, x, *loads):
                for sem_, v in loads:
                    dve.wait_ge(sem_, v)
                at = [None] * BT
                for k in range(BT + 1):
                    if 1 < k < BT:
                        steps.wait()
                    if k < BT:
                        at[k] = norm_stats(steps, x[:, k], k)
                    if k:
                        steps.wait(at[k - 1])
                        apart()
                        ins = nc.vector.bn_aggr(mvX[:, k - 1], st[:, (k - 1) % 2])
                        if k < BT:
                            steps.done(ins)
                ins.then_inc(var_ready, 1)

            def make_h0(steps, t, k, x):
                dve.wait_ge(tp_full, t * BT + TP3 + max(k - 1, 0))
                return steps.done(nc.vector.tensor_scalar(H0[:, k % 2], x, mvX[:, k, 0:1],
                                                          rs_x[:, k:k + 1], ALU.subtract, ALU.mult))

            def h0_stats(steps, k, at):
                steps.wait(at)
                return norm_stats(steps, H0[:, k % 2], k)

            def h_scale(steps, slot, k, x, n):
                steps.done(nc.vector.scalar_tensor_tensor(out=base[:, slot, k], in0=H0[:, k % 2], scalar=gate_f,
                                                          in1=x, op0=ALU.mult, op1=ALU.add))
                return norm_scale(steps, H0[:, k % 2], mvH, k, vec3[:, 0], n)

            def h_shift(steps, k, at, n):
                norm_shift(steps, at, H0[:, k % 2], H0[:, k % 2], rsH, k, vec3[:, 1], n, hn_ready)

            def lo_h(t, slot, k):
                lo_t(TP3 + k, [hT[:, slot * C:(slot + 1) * C, h, k * P:(k + 1) * P] for h in range(2)],
                     k, t, BT)

            with dve.Fori(0, NT // 2 - 1) as u:
                for slot in range(2):
                    tile2(u * 2 + slot, slot, False, False)
            for slot in range(2):
                tile2(NT - 2 + slot, slot, True, slot == 1)
            nc.vector.tensor_copy(sum2[:, 0:1], len2[:, 0:1]).then_inc(p2_end, 1)

            dve.wait_ge(bias3_in, 16)
            nc.vector.tensor_scalar(bias3, bias3, gf_half, None, ALU.mult).then_inc(bias3_ready, 1)

            def scale_w2(f):
                if f < 4:
                    scale_codes(*w2_stage(f), (x1b_in[f], NT * 16 + 32))
                else:
                    scale_codes(*w2_stage(f), (q2_in[f % 2], (f - 2) // 2 * 16), (sc2_in, (f - 3) * 16))

            def tile3(t, slot, first, last):
                p3 = Steps(dve, dve_p3, DVE3, t)
                for f in range(NF):
                    if not (first and f == 0):
                        lo_hid3(t, f)
                    if first and 0 < f and f + 1 < NF:
                        lo_w(NT * 2 + f + 1, w2_stage(f + 1)[0], w2_unit(f + 1))
                    if first and f + 2 < NF:
                        scale_w2(f + 2)
                    if not last:
                        n0 = (t + 1) * (1 + BT) + R3 + 1
                        if f in TURN_AT:
                            lo_h(t + 1, 1 - slot, TURN_AT.index(f))
                        if f == TURN_AT[0] - 3:
                            stats_x3(p3, base[:, 1 - slot], (b_in[1 - slot], (t + 1) // 2 * 16 + 16 * (1 - slot)))
                        if f + 2 in TURN_AT:
                            k = TURN_AT.index(f + 2)
                            if k == 0:
                                dve.wait_ge(rstd_ready, n0)
                            at = make_h0(p3, t + 1, k, base[:, 1 - slot, k])
                            at = h0_stats(p3, k, at)
                            norm_mean(p3, at, mvH, k)
                        if f + 1 in TURN_AT:
                            k = TURN_AT.index(f + 1)
                            x = base[:, 1 - slot, k]
                            at = h_scale(p3, 1 - slot, k, x, n0 + k + 1)
                            p3.wait(at)
                            p3.done(nc.vector.tensor_tensor(x, x, bias3, ALU.add))
                            h_shift(p3, k, at, n0 + k + 1)
                dve.wait_ge(base_biased, BT)
                for k in range(BT):
                    x = base[:, slot, k]
                    if k < BT - 1:
                        dve.wait_ge(o_full, t * (BT - 1) + k + 1)
                    else:
                        dve.wait_ge(hid_free, t * NF + 2 + NF)
                    nc.vector.scalar_tensor_tensor(out=x, in0=PS[:, 4 + k], scalar=gf_half, in1=x,
                                                   op0=ALU.mult, op1=ALU.add).then_inc(o_free, 1)
                if not last:
                    assert p3.n == DVE3, p3.n

            tiles(dve, tile3)


_INS = ["x", "ctx_1024", "g_xattn", "g_ffn", "L0_xattn_Wq1", "L0_xattn_Wk1", "L0_xattn_Wv1", "L0_xattn_Wq2",
        "L0_xattn_Wk2", "L0_xattn_Wv2", "L0_xattn_fc1_w", "L0_xattn_fc1_b", "L0_xattn_fc2_w", "L0_xattn_fc2_b",
        "L0_xattn_ln1_g", "L0_xattn_ln1_b", "L0_xattn_ln2_g", "L0_xattn_ln2_b", "L0_xattn_ln3_g",
        "L0_xattn_ln3_b", "L0_ffn_ln_gamma", "L0_ffn_ln_beta", "L0_ffn_fc1_q", "L0_ffn_fc1_scales",
        "L0_ffn_fc1_bias", "L0_ffn_fc2_q", "L0_ffn_fc2_scales", "L0_ffn_fc2_bias"]


def kernel(**inputs):
    import numpy as _np
    import concourse.bacc as _bacc
    from concourse import mybir as _mybir
    from concourse.bass_utils import run_bass_kernel_spmd as _run

    nc = _bacc.Bacc("TRN2", target_bir_lowering=False, num_devices=1)
    arrays, aps = {}, {}
    for name in _INS:
        v = _np.ascontiguousarray(inputs[name])
        arrays[f"in_{name}"] = v
        aps[name] = nc.dram_tensor(f"in_{name}", v.shape, _mybir.dt.from_np(v.dtype), kind="ExternalInput").ap()
    out = nc.dram_tensor("out_0", (B, S, E), F32, kind="ExternalOutput").ap()
    build(nc, aps, out)
    r = _run(nc, [arrays], core_ids=[0])
    return r.results[0]["out_0"]
```
